# Optimizing a Trainium2 kernel written in Bass

```python
import numpy as np
import jax
import jax.numpy as jnp

def _softmax(x, axis=-1):
    return jax.nn.softmax(x, axis=axis)

def _gelu(x):
    return jax.nn.gelu(x, approximate=True)

def _silu(x):
    return jax.nn.silu(x)

def _sigmoid(x):
    return jax.nn.sigmoid(x)

def _layernorm(x, axis=-1, eps=1e-05):
    m = jnp.mean(x, axis=axis, keepdims=True)
    v = jnp.var(x, axis=axis, keepdims=True)
    return (x - m) / jnp.sqrt(v + eps)

def _scatter_add(tgt, idx, src, axis=0):
    return tgt.at[idx].add(src)

def _segment_sum(src, seg, n):
    return jax.ops.segment_sum(src, seg, n)
kernel_name = 'mk_xattn_seq_d4_seqx_r8_46a64a'

def setup_inputs(seed: int=0):
    np.random.seed(seed)
    _w = jnp.asarray

    def _rec_inputs():
        import jax
        import jax.numpy as jnp
        _rk = jax.random.key(seed)
        x = -0.0005146 + 1 * jax.random.normal(jax.random.fold_in(_rk, 1), (16, 128, 256), jnp.float32)
        _lenS = 128 - jax.random.randint(jax.random.fold_in(_rk, 7), (16,), 0, max(1, 128 // 4) + 1, jnp.int32)
        _lenS2 = 128 - jax.random.randint(jax.random.fold_in(_rk, 8), (16,), 0, max(1, 128 // 4) + 1, jnp.int32)
        _ctx_2048P = jax.random.normal(jax.random.fold_in(_rk, 11), (16, 16, 256), jnp.float32)
        _ctx_2048c = jax.random.dirichlet(jax.random.fold_in(_rk, 511), 0.3 * jnp.ones((16,), jnp.float32), (16, 128))
        _ctx_2048t = jnp.einsum('bsk,bkd->bsd', _ctx_2048c, _ctx_2048P)
        _ctx_2048t = _ctx_2048t * jax.lax.rsqrt(jnp.mean(jnp.square(_ctx_2048t)) + 1e-12) * 0.953939
        ctx_2048 = -0.000392918 + 0.999932 * (_ctx_2048t + 0.3 * jax.random.normal(jax.random.fold_in(_rk, 611), (16, 128, 256), jnp.float32))
        _validS = jnp.arange(128)[None, :] < _lenS[:, None]
        _validS2 = jnp.arange(128)[None, :] < _lenS2[:, None]
        _causal = jnp.tril(jnp.ones((128, 128), dtype=bool))
        mask_BxS2_ik0 = jnp.where(jnp.broadcast_to(_validS2[:, :], (16, 128)), 0, 1).astype(jnp.int32)
        mask_Bx1xSxS2_ff0 = jnp.where(jnp.ones((16, 1, 128, 128), dtype=bool), 0.0, -1000000000.0).astype(jnp.float32)
        return (x, ctx_2048, mask_BxS2_ik0, mask_Bx1xSxS2_ff0)
    x, ctx_2048, mask_BxS2_ik0, mask_Bx1xSxS2_ff0 = _rec_inputs()

    def _L0_xattn_setup():
        import jax, jax.numpy as jnp
        import numpy as np
        B, P, K, H, NH = (4, 256, 32, 256, 16)
        DH = H // NH
        EPS = 1e-06

        def rmsnorm(x, w):
            var = jnp.mean(jnp.square(x), axis=-1, keepdims=True)
            return x * jax.lax.rsqrt(var + EPS) * w
        key = jax.random.key(seed)
        ks = jax.random.split(key, 12)
        s = 0.02
        return {'x': jax.random.normal(ks[0], (B, P, H), jnp.float32), 'latents': jax.random.normal(ks[1], (B, K, H), jnp.float32), 'attention_mask': jax.random.randint(ks[2], (B, P), 0, 2, jnp.int32), 'q_w': s * jax.random.normal(ks[3], (H, H), jnp.float32), 'q_b': jnp.zeros((H,), jnp.float32), 'kv_w': s * jax.random.normal(ks[4], (H, 2 * H), jnp.float32), 'kv_b': jnp.zeros((2 * H,), jnp.float32), 'out_w': s * jax.random.normal(ks[5], (H, H), jnp.float32), 'out_b': jnp.zeros((H,), jnp.float32), 'postnorm_w': jnp.ones((H,), jnp.float32), 'mlp_w1': s * jax.random.normal(ks[6], (H, 4 * H), jnp.float32), 'mlp_b1': jnp.zeros((4 * H,), jnp.float32), 'mlp_w2': s * jax.random.normal(ks[7], (4 * H, H), jnp.float32), 'mlp_b2': jnp.zeros((H,), jnp.float32)}
    _L0_xattn_all = _L0_xattn_setup()
    _L0_xattn_in = {k: v for k, v in _L0_xattn_all.items() if k in ('q_w', 'q_b', 'kv_w', 'kv_b', 'out_w', 'out_b', 'postnorm_w', 'mlp_w1', 'mlp_b1', 'mlp_w2', 'mlp_b2')}
    del _L0_xattn_all

    def _L1_xattn_setup():
        import jax, jax.numpy as jnp
        import numpy as np
        H = 256
        NH = 32
        KVH = 8
        HD = H // NH
        GROUPS = NH // KVH
        EPS = 1e-06
        B, L, S = (4, 128, 128)

        def _gqa_forward(hidden_state, encoder_hidden_state, encoder_attention_mask, Wq, bq, Wk, bk, Wv, bv, Wo, bo, gamma, beta):
            b, l, _ = hidden_state.shape
            s = encoder_hidden_state.shape[1]
            q = hidden_state @ Wq + bq
            k = encoder_hidden_state @ Wk + bk
            v = encoder_hidden_state @ Wv + bv
            q = q.reshape(b, l, KVH, GROUPS, HD).transpose(0, 2, 3, 1, 4)
            k = k.reshape(b, s, KVH, HD).transpose(0, 2, 1, 3)
            v = v.reshape(b, s, KVH, HD).transpose(0, 2, 1, 3)
            scale = 1.0 / jnp.sqrt(jnp.asarray(HD, q.dtype))
            scores = jnp.einsum('bkgld,bksd->bkgls', q, k) * scale
            scores = scores + encoder_attention_mask[:, :, None, :, :]
            attn = jax.nn.softmax(scores, axis=-1)
            out = jnp.einsum('bkgls,bksd->bkgld', attn, v)
            out = out.transpose(0, 3, 1, 2, 4).reshape(b, l, H)
            out = out @ Wo + bo
            x = out + hidden_state
            mu = jnp.mean(x, axis=-1, keepdims=True)
            var = jnp.var(x, axis=-1, keepdims=True)
            return (x - mu) * jax.lax.rsqrt(var + EPS) * gamma + beta
        key = jax.random.key(seed)
        ks = jax.random.split(key, 12)
        sd = 0.02
        return {'hidden_state': jax.random.normal(ks[0], (B, L, H), jnp.float32), 'encoder_hidden_state': jax.random.normal(ks[1], (B, S, H), jnp.float32), 'encoder_attention_mask': jnp.zeros((B, 1, L, S), jnp.float32), 'Wq': jax.random.normal(ks[2], (H, H), jnp.float32) * sd, 'bq': jnp.zeros((H,), jnp.float32), 'Wk': jax.random.normal(ks[3], (H, KVH * HD), jnp.float32) * sd, 'bk': jnp.zeros((KVH * HD,), jnp.float32), 'Wv': jax.random.normal(ks[4], (H, KVH * HD), jnp.float32) * sd, 'bv': jnp.zeros((KVH * HD,), jnp.float32), 'Wo': jax.random.normal(ks[5], (H, H), jnp.float32) * sd, 'bo': jnp.zeros((H,), jnp.float32), 'gamma': jnp.ones((H,), jnp.float32), 'beta': jnp.zeros((H,), jnp.float32)}
    _L1_xattn_all = _L1_xattn_setup()
    _L1_xattn_in = {k: v for k, v in _L1_xattn_all.items() if k in ('Wq', 'bq', 'Wk', 'bk', 'Wv', 'bv', 'Wo', 'bo', 'gamma', 'beta')}
    del _L1_xattn_all

    def _L2_xattn_setup():
        import jax, jax.numpy as jnp
        import numpy as np
        B, C1, C2, N = (8, 128, 128, 256)
        D = C2 // 8
        key = jax.random.key(seed)
        ks = jax.random.split(key, 8)
        s1 = 1.0 / np.sqrt(C1)
        s2 = 1.0 / np.sqrt(C2)
        return {'x1': jax.random.normal(ks[0], (B, C1, N), jnp.float32), 'x2': jax.random.normal(ks[1], (B, C2, N), jnp.float32), 'Wq': jax.random.uniform(ks[2], (D, C1), jnp.float32, -s1, s1), 'bq': jax.random.uniform(ks[3], (D,), jnp.float32, -s1, s1), 'Wk': jax.random.uniform(ks[4], (D, C2), jnp.float32, -s2, s2), 'bk': jax.random.uniform(ks[5], (D,), jnp.float32, -s2, s2), 'Wv': jax.random.uniform(ks[6], (C1, C2), jnp.float32, -s2, s2), 'bv': jax.random.uniform(ks[7], (C1,), jnp.float32, -s2, s2)}
    _L2_xattn_all = _L2_xattn_setup()
    _L2_xattn_in = {k: v for k, v in _L2_xattn_all.items() if k in ('Wq', 'bq', 'Wk', 'bk', 'Wv', 'bv')}
    del _L2_xattn_all

    def _L3_xattn_setup():
        import jax, jax.numpy as jnp
        import numpy as np
        H = 256
        B, L, S = (4, 512, 10)
        key = jax.random.key(seed)
        k1, k2, k3, k4, k5, k6 = jax.random.split(key, 6)
        scale = 1.0 / np.sqrt(H)
        return {'h_english': jax.random.normal(k1, (B, L, H), dtype=jnp.float32), 'h_lojban': jax.random.normal(k2, (B, S, H), dtype=jnp.float32), 'w_q': jax.random.normal(k3, (H, H), dtype=jnp.float32) * scale, 'w_k': jax.random.normal(k4, (H, H), dtype=jnp.float32) * scale, 'w_v': jax.random.normal(k5, (H, H), dtype=jnp.float32) * scale, 'w_o': jax.random.normal(k6, (H, H), dtype=jnp.float32) * scale, 'alpha': jnp.float32(0.1)}
    _L3_xattn_all = _L3_xattn_setup()
    _L3_xattn_in = {k: v for k, v in _L3_xattn_all.items() if k in ('w_q', 'w_k', 'w_v', 'w_o', 'alpha')}
    del _L3_xattn_all
    return {'x': x, 'ctx_2048': ctx_2048, 'mask_BxS2_ik0': mask_BxS2_ik0, 'mask_Bx1xSxS2_ff0': mask_Bx1xSxS2_ff0, 'L0_xattn_q_w': _L0_xattn_in['q_w'], 'L0_xattn_q_b': _L0_xattn_in['q_b'], 'L0_xattn_kv_w': _L0_xattn_in['kv_w'], 'L0_xattn_kv_b': _L0_xattn_in['kv_b'], 'L0_xattn_out_w': _L0_xattn_in['out_w'], 'L0_xattn_out_b': _L0_xattn_in['out_b'], 'L0_xattn_postnorm_w': _L0_xattn_in['postnorm_w'], 'L0_xattn_mlp_w1': _L0_xattn_in['mlp_w1'], 'L0_xattn_mlp_b1': _L0_xattn_in['mlp_b1'], 'L0_xattn_mlp_w2': _L0_xattn_in['mlp_w2'], 'L0_xattn_mlp_b2': _L0_xattn_in['mlp_b2'], 'L1_xattn_Wq': _L1_xattn_in['Wq'], 'L1_xattn_bq': _L1_xattn_in['bq'], 'L1_xattn_Wk': _L1_xattn_in['Wk'], 'L1_xattn_bk': _L1_xattn_in['bk'], 'L1_xattn_Wv': _L1_xattn_in['Wv'], 'L1_xattn_bv': _L1_xattn_in['bv'], 'L1_xattn_Wo': _L1_xattn_in['Wo'], 'L1_xattn_bo': _L1_xattn_in['bo'], 'L1_xattn_gamma': _L1_xattn_in['gamma'], 'L1_xattn_beta': _L1_xattn_in['beta'], 'L2_xattn_Wq': _L2_xattn_in['Wq'], 'L2_xattn_bq': _L2_xattn_in['bq'], 'L2_xattn_Wk': _L2_xattn_in['Wk'], 'L2_xattn_bk': _L2_xattn_in['bk'], 'L2_xattn_Wv': _L2_xattn_in['Wv'], 'L2_xattn_bv': _L2_xattn_in['bv'], 'L3_xattn_w_q': _L3_xattn_in['w_q'], 'L3_xattn_w_k': _L3_xattn_in['w_k'], 'L3_xattn_w_v': _L3_xattn_in['w_v'], 'L3_xattn_w_o': _L3_xattn_in['w_o'], 'L3_xattn_alpha': _L3_xattn_in['alpha']}

def reference(x, ctx_2048, mask_BxS2_ik0, mask_Bx1xSxS2_ff0, L0_xattn_q_w, L0_xattn_q_b, L0_xattn_kv_w, L0_xattn_kv_b, L0_xattn_out_w, L0_xattn_out_b, L0_xattn_postnorm_w, L0_xattn_mlp_w1, L0_xattn_mlp_b1, L0_xattn_mlp_w2, L0_xattn_mlp_b2, L1_xattn_Wq, L1_xattn_bq, L1_xattn_Wk, L1_xattn_bk, L1_xattn_Wv, L1_xattn_bv, L1_xattn_Wo, L1_xattn_bo, L1_xattn_gamma, L1_xattn_beta, L2_xattn_Wq, L2_xattn_bq, L2_xattn_Wk, L2_xattn_bk, L2_xattn_Wv, L2_xattn_bv, L3_xattn_w_q, L3_xattn_w_k, L3_xattn_w_v, L3_xattn_w_o, L3_xattn_alpha):
    import jax
    import jax.numpy as jnp

    def _L0_xattn_ref(x, latents, attention_mask, q_w, q_b, kv_w, kv_b, out_w, out_b, postnorm_w, mlp_w1, mlp_b1, mlp_w2, mlp_b2):
        import jax, jax.numpy as jnp
        import numpy as np
        B, P, K, H, NH = (4, 256, 32, 256, 16)
        DH = H // NH
        EPS = 1e-06

        def rmsnorm(x, w):
            var = jnp.mean(jnp.square(x), axis=-1, keepdims=True)
            return x * jax.lax.rsqrt(var + EPS) * w
        b, p, _ = x.shape
        k_len = latents.shape[1]
        residual = latents
        h = jnp.concatenate([x, latents], axis=1)
        q = (latents @ q_w + q_b).reshape(b, k_len, NH, DH)
        kv = (h @ kv_w + kv_b).reshape(b, p + k_len, NH, DH, 2)
        kmat, v = (kv[..., 0], kv[..., 1])
        attn = jnp.einsum('bkhd,bnhd->bhkn', q, kmat) / DH
        full_mask = jnp.concatenate([attention_mask.astype(bool), jnp.ones((b, k_len), bool)], axis=-1)
        attn = jnp.where(full_mask[:, None, None, :], attn, -jnp.inf)
        attn = jax.nn.softmax(attn.astype(jnp.float32), axis=-1).astype(q.dtype)
        attn_out = jnp.einsum('bhkn,bnhd->bkhd', attn, v).reshape(b, k_len, H)
        attn_out = attn_out @ out_w + out_b + residual
        out = rmsnorm(attn_out, postnorm_w)
        out = jax.nn.gelu(out @ mlp_w1 + mlp_b1) @ mlp_w2 + mlp_b2
        return out + residual

    def _L1_xattn_ref(hidden_state, encoder_hidden_state, encoder_attention_mask, Wq, bq, Wk, bk, Wv, bv, Wo, bo, gamma, beta):
        import jax, jax.numpy as jnp
        import numpy as np
        H = 256
        NH = 32
        KVH = 8
        HD = H // NH
        GROUPS = NH // KVH
        EPS = 1e-06
        B, L, S = (4, 128, 128)

        def _gqa_forward(hidden_state, encoder_hidden_state, encoder_attention_mask, Wq, bq, Wk, bk, Wv, bv, Wo, bo, gamma, beta):
            b, l, _ = hidden_state.shape
            s = encoder_hidden_state.shape[1]
            q = hidden_state @ Wq + bq
            k = encoder_hidden_state @ Wk + bk
            v = encoder_hidden_state @ Wv + bv
            q = q.reshape(b, l, KVH, GROUPS, HD).transpose(0, 2, 3, 1, 4)
            k = k.reshape(b, s, KVH, HD).transpose(0, 2, 1, 3)
            v = v.reshape(b, s, KVH, HD).transpose(0, 2, 1, 3)
            scale = 1.0 / jnp.sqrt(jnp.asarray(HD, q.dtype))
            scores = jnp.einsum('bkgld,bksd->bkgls', q, k) * scale
            scores = scores + encoder_attention_mask[:, :, None, :, :]
            attn = jax.nn.softmax(scores, axis=-1)
            out = jnp.einsum('bkgls,bksd->bkgld', attn, v)
            out = out.transpose(0, 3, 1, 2, 4).reshape(b, l, H)
            out = out @ Wo + bo
            x = out + hidden_state
            mu = jnp.mean(x, axis=-1, keepdims=True)
            var = jnp.var(x, axis=-1, keepdims=True)
            return (x - mu) * jax.lax.rsqrt(var + EPS) * gamma + beta
        return _gqa_forward(hidden_state, encoder_hidden_state, encoder_attention_mask, Wq, bq, Wk, bk, Wv, bv, Wo, bo, gamma, beta)

    def _L2_xattn_ref(x1, x2, Wq, bq, Wk, bk, Wv, bv):
        import jax, jax.numpy as jnp
        import numpy as np
        B, C1, C2, N = (8, 128, 128, 256)
        D = C2 // 8
        q = jnp.einsum('bcn,dc->bnd', x1, Wq) + bq
        k = jnp.einsum('bcn,dc->bdn', x2, Wk) + bk[:, None]
        v = jnp.einsum('bcn,dc->bdn', x2, Wv) + bv[:, None]
        attn = jax.nn.softmax(jnp.einsum('bnd,bdm->bnm', q, k), axis=2)
        attn_out = jnp.einsum('bcm,bnm->bcn', v, attn)
        return attn_out + x1

    def _L3_xattn_ref(h_english, h_lojban, w_q, w_k, w_v, w_o, alpha):
        import jax, jax.numpy as jnp
        import numpy as np
        H = 256
        B, L, S = (4, 512, 10)
        h = h_english.shape[-1]
        q = jnp.einsum('blh,oh->blo', h_english, w_q)
        k = jnp.einsum('bsh,oh->bso', h_lojban, w_k)
        v = jnp.einsum('bsh,oh->bso', h_lojban, w_v)
        scores = jnp.einsum('blh,bsh->bls', q, k) / jnp.sqrt(jnp.float32(h))
        probs = jax.nn.softmax(scores, axis=-1)
        context = jnp.einsum('bls,bsh->blh', probs, v)
        delta = jnp.einsum('blh,oh->blo', context, w_o)
        return h_english + alpha * delta
    x = _L0_xattn_ref(ctx_2048, x, mask_BxS2_ik0, L0_xattn_q_w, L0_xattn_q_b, L0_xattn_kv_w, L0_xattn_kv_b, L0_xattn_out_w, L0_xattn_out_b, L0_xattn_postnorm_w, L0_xattn_mlp_w1, L0_xattn_mlp_b1, L0_xattn_mlp_w2, L0_xattn_mlp_b2)
    x = _L1_xattn_ref(x, ctx_2048, mask_Bx1xSxS2_ff0, L1_xattn_Wq, L1_xattn_bq, L1_xattn_Wk, L1_xattn_bk, L1_xattn_Wv, L1_xattn_bv, L1_xattn_Wo, L1_xattn_bo, L1_xattn_gamma, L1_xattn_beta)
    x = _L2_xattn_ref(x, ctx_2048, L2_xattn_Wq, L2_xattn_bq, L2_xattn_Wk, L2_xattn_bk, L2_xattn_Wv, L2_xattn_bv)
    x = _L3_xattn_ref(x, ctx_2048, L3_xattn_w_q, L3_xattn_w_k, L3_xattn_w_v, L3_xattn_w_o, L3_xattn_alpha)
    return x

_drawn_inputs = setup_inputs


def setup_inputs(seed=0):
    import zlib

    import numpy as np

    out = dict(_drawn_inputs(seed))
    spreads = {'L0_xattn_q_b': (0.0, 0.8),
     'L0_xattn_kv_b': (0.0, 0.8),
     'L0_xattn_out_b': (0.0, 0.665),
     'L0_xattn_postnorm_w': (1.0, 0.6),
     'L0_xattn_mlp_b1': (0.0, 0.1),
     'L0_xattn_mlp_b2': (0.0, 0.1),
     'L1_xattn_bq': (0.0, 0.8),
     'L1_xattn_bk': (0.0, 0.8),
     'L1_xattn_bv': (0.0, 0.1),
     'L1_xattn_bo': (0.0, 0.1),
     'L1_xattn_gamma': (1.0, 0.2),
     'L1_xattn_beta': (0.0, 0.1)}
    factors = {'L0_xattn_q_w': 8.0,
     'L0_xattn_kv_w': 8.0,
     'L0_xattn_out_w': 8.0,
     'L1_xattn_Wq': 8.0,
     'L1_xattn_Wk': 8.0,
     'L2_xattn_bq': 2.803,
     'L2_xattn_bk': 8.0,
     'L3_xattn_w_q': 2.667,
     'L3_xattn_w_k': 2.699}
    for name, (base, spread) in spreads.items():
        noise = np.random.default_rng([zlib.crc32(name.encode()), seed]).standard_normal(out[name].shape)
        drawn = base * np.exp(spread * noise) if base else spread * noise
        out[name] = jnp.asarray(drawn.astype(out[name].dtype))
    for name, factor in factors.items():
        out[name] = (out[name] * factor).astype(out[name].dtype)
    return out
```

```python
from contextlib import ExitStack

import concourse.bass as bass
from concourse import mybir

F32 = mybir.dt.float32
BF16 = mybir.dt.bfloat16
I32 = mybir.dt.int32
ALU = mybir.AluOpType
ACT = mybir.ActivationFunctionType
AX_X = mybir.AxisListType.X

P = 128
B = 16
J = 2
UNITS = B // J
T = J * P
H = 256
KT = H // P
NH0, D0 = 16, 16
NH1, KV1, D1 = 32, 8, 8
G1 = NH1 // KV1
FF = 4 * H
MT = FF // P
D2 = 16
S0, S1 = 96, 72
MASK_ROW = S0
R0 = S0 + 1 + 3
R1 = S1 + 3
OUT_W = 32
MASKED = -1.0e30
M0_COLS = 5
EPS = 1.0e-6
WEIGHTS, CONSTANTS = 25, 12

A_Q, A_K, A_V, A_S, A_M, A_ST, A_PV, A_OT, A_FT, A_OUT, A_TILES, A_NEXT = 0, 1, 3, 5, 21, 22, 30, 31, 42, 43, 44, 10
B_KV, B_NT, B_UP, B_DOWN, B_XT, B_Q, B_V, B_TILES = 0, 1, 2, 6, 7, 8, 9, 10
C_S, C_M, C_ST, C_PV, C_TR, C_FT, C_OUT, C_TILES, C_NEXT = 0, 16, 17, 25, 27, 41, 42, 44, 12
D_K, D_V, D_KK, D_VV, D_Q, D_S, D_PT, D_PV, D_XT, D_S3, D_PT3, D_OUT, D_TILES = 0, 1, 2, 3, 4, 5, 7, 9, 10, 11, 12, 13, 14

LOAD, FIRST, SECOND, THIRD = 0, 1, 2, 3
ROUND = [
    (THIRD, "d_load"), (FIRST, "a_residual"), (FIRST, "a_project"), (THIRD, "c_scores", 1, 0), (SECOND, "b_norm"), (FIRST, "a_values"),
    (FIRST, "a_stack"), (THIRD, "c_scores", 1, 1), (SECOND, "b_up", 0), (SECOND, "b_up", 1), (THIRD, "c_maxima"),
    (SECOND, "b_up", 2), (SECOND, "b_up", 3), (THIRD, "c_weights", 0, 0), (SECOND, "b_down", 0), (THIRD, "c_weights", 0, 1),
    (SECOND, "b_down", 1), (THIRD, "c_attend", 0), (THIRD, "d_context"), (THIRD, "c_turn", 0), (THIRD, "c_weights", 1, 0),
    (SECOND, "b_turn"), (THIRD, "c_weights", 1, 1), (FIRST, "b_residual"), (THIRD, "d_context_products"), (THIRD, "c_attend", 1),
    (SECOND, "b_project"), (THIRD, "c_turn", 1), (FIRST, "b_keys"), (THIRD, "c_join"), (SECOND, "b_stack"), (THIRD, "c_out"),
    (SECOND, "c_residual"), (LOAD, "a_load"), (FIRST, "a_scores", 0, 0), (THIRD, "c_norm"), (FIRST, "a_scores", 0, 1),
    (THIRD, "d_query"), (FIRST, "a_scores", 1, 0), (THIRD, "d_scores", 0), (FIRST, "a_scores", 1, 1), (THIRD, "d_scores", 1),
    (FIRST, "a_maxima"), (SECOND, "b_load"), (THIRD, "d_attend"), (FIRST, "a_weights", 0, 0), (FIRST, "a_weights", 0, 1),
    (THIRD, "d_x"), (FIRST, "a_attend", 0), (SECOND, "c_scores", 0, 0), (FIRST, "a_turn", 0), (THIRD, "d_text_scores"),
    (FIRST, "a_weights", 1, 0), (FIRST, "a_weights", 1, 1), (SECOND, "c_scores", 0, 1), (THIRD, "d_text"), (FIRST, "a_attend", 1),
    (FIRST, "a_turn", 1), (FIRST, "a_join"), (FIRST, "a_out"), (FIRST, "a_norm"),
]


def build(nc, x, x_t, ctx, ctx_t, mask0, mask1, mask1_t, w, out):
    with ExitStack() as stack:
        def sb(name, shape, dt=F32):
            return stack.enter_context(nc.sbuf_tensor(name, shape, dt))

        def signal(name):
            return stack.enter_context(nc.semaphore(name))

        wq0, wk0, wv0, wo0 = (sb(n, [P, KT, H]) for n in ("wq0", "wk0", "wv0", "wo0"))
        w_up, w_down = sb("w_up", [P, KT, FF]), sb("w_down", [P, MT, H])
        wq1, wkv1, wo1 = sb("wq1", [P, KT, H]), sb("wkv1", [P, KT, P]), sb("wo1", [P, KT, H])
        wq2, wk2, wv2 = sb("wq2", [P, D2]), sb("wk2", [P, D2]), sb("wv2", [P, P])
        cols = sb("cols", [P, 20])
        bq0, bk0, norm_w = cols[:, 0:2], cols[:, 2:4], cols[:, 4:6]
        b_up, bq1_raw, bkv1 = cols[:, 6:14], cols[:, 14:16], cols[:, 16:17]
        bq2, bk2, alpha = cols[0:D2, 17:18], cols[0:D2, 18:19], cols[:, 19:20]
        bv0, bo0, b_down, bo1, gamma, beta = (sb(n, [P, H]) for n in ("bv0", "bo0", "b_down", "bo1", "gamma", "beta"))
        bv2 = sb("bv2", [P, P])
        ident, ident_bf = sb("ident", [P, P]), sb("ident_bf", [P, P], BF16)
        bq1 = sb("bq1", [P, KT])
        power = sb("power", [P, J])
        spare = sb("spare", [P, 1])
        key3 = sb("key3", [P, KT, H])
        val3 = sb("val3", [P, KT, H])

        h_t = sb("h_t", [P, KT, J, 2, P])
        x_a = sb("x_a", [P, J, H])
        mask_i, mask_b = sb("mask_i", [1, J, P], I32), sb("mask_b", [1, J, 2, P], BF16)
        q0p, k0p = sb("q0p", [P, 3, KT, T], BF16), sb("k0p", [P, 3, KT, 2 * T], BF16)
        q0s, k0s = sb("q0s", [P, NH0, T], BF16), sb("k0s", [P, NH0, 2 * T], BF16)
        v0 = sb("v0", [P, J, 2, NH0, OUT_W])
        m0, m0r, m0p = sb("m0", [P, J, NH0]), sb("m0r", [P, J, NH0]), sb("m0p", [P, J, M0_COLS, NH0], BF16)
        m0t = sb("m0t", [3 * NH0, T], BF16)
        p0 = sb("p0", [P, 2, NH0, P])
        p0_flat = p0[:].rearrange("p s h q -> p (s h q)")
        q0f = p0_flat[:, 0:KT * T].rearrange("p (t q) -> p t q", t=KT)
        k0f = p0_flat[:, KT * T:3 * KT * T].rearrange("p (t q) -> p t q", t=KT)
        up = p0_flat[:, 2048:2048 + MT * T].rearrange("p (m q) -> p m q", m=MT)
        f0t = p0_flat[:, 1536:2048].rearrange("p (t q) -> p t q", t=KT)
        o0t, rc0, o0 = sb("o0t", [P, 512]), sb("rc0", [P, J, NH0]), sb("o0", [P, J, H])
        res0, y0, y0n = sb("res0", [P, J, H]), sb("y0", [P, J, H]), sb("y0n", [P, J, H])
        ss0, ms0, rs0 = sb("ss0", [P, J]), sb("ms0", [P, J]), sb("rs0", [P, J])
        n_t = sb("n_t", [P, KT, T])
        res_b, x1, x1_t = sb("res_b", [P, J, H]), sb("x1", [P, J, H]), sb("x1_t", [P, KT, T])
        kv1f = sb("kv1f", [P, T])
        q1p, k1p = sb("q1p", [P, 3, KT, T], BF16), sb("k1p", [KV1 * D1, 3, T], BF16)
        q1s, k1s = sb("q1s", [R1, NH1, T], BF16), sb("k1s", [P, KV1, T], BF16)
        v1 = sb("v1", [P, J, KV1, OUT_W])
        m_l, m_s = sb("m_l", [P, J, P]), sb("m_s", [P, J, P])
        res1 = sb("res1", [P, J, H])
        sm = [sb(f"sm_{n}", [P, 4, P]) for n in range(2)]
        m1, m1r, m1p = sb("m1", [P, J, NH1]), sb("m1r", [P, J, NH1]), sb("m1p", [P, J, 3, NH1], BF16)
        m1t = sb("m1t", [3 * NH1, T], BF16)
        p1 = sb("p1", [P, NH1, P])
        p1_flat = p1[:].rearrange("p h q -> p (h q)")
        p2 = p1_flat[:, 0:1024].rearrange("p (j t m) -> p j t m", j=J, t=KT)
        p2t = p1_flat[:, 1024:2048].rearrange("p (j m n) -> p j m n", j=J, m=KT)
        p3 = p1_flat[:, 2048:2304].rearrange("p (j s) -> p j s", j=J)
        p3t = p1_flat[:, 2304:2560].rearrange("p (j q) -> p j q", j=J)
        q1f = p1_flat[:, 2560:3072].rearrange("p (t q) -> p t q", t=KT)
        x3_t = p1_flat[:, 3328:3840].rearrange("p (t q) -> p t q", t=KT)
        k1r = p1_flat[0:KV1 * D1, 3072:3328]
        wq3, wk3, wv3, wo3 = (p1_flat[:, n * KT * H:(n + 1) * KT * H].rearrange("p (t h) -> p t h", t=KT) for n in range(4))
        o1t, rc1, o1 = sb("o1t", [P, 2, 512]), sb("rc1", [P, 2, 4, 4]), sb("o1", [P, J, H])
        f1t = sb("f1t", [P, KT, T])
        y1, st1, mv1, ve1, rs1 = sb("y1", [P, J, H]), sb("st1", [P, J, 6]), sb("mv1", [P, J, 2]), sb("ve1", [P, J]), sb("rs1", [P, J])
        x2 = sb("x2", [P, J, H])
        ctx_d, ctx_td = sb("ctx_d", [P, J, H]), sb("ctx_td", [P, KT, T])
        q2, k2, v2 = sb("q2", [D2, J, H]), sb("k2", [D2, J, H]), sb("v2", [P, J, KT, P])
        m2, sum2, rc2 = sb("m2", [P, J, KT]), sb("sum2", [P, J, KT]), sb("rc2", [P, J, KT])
        x3 = sb("x3", [P, J, H])
        kk3, vv3 = sb("kk3", [P, KT, T]), sb("vv3", [P, J, H])
        m3, m3s, sum3, rc3, ar3 = (sb(n, [P, J]) for n in ("m3", "m3s", "sum3", "rc3", "ar3"))

        tiles_of = {"a": A_TILES, "b": B_TILES, "c": C_TILES, "d": D_TILES}
        bank = {s: [stack.enter_context(nc.psum_tensor(f"bank_{s}{n}", [P, 512], F32)) for n in range(2)] for s in "abcd"}
        made = {s: signal(f"{s}_made") for s in "abcd"}
        read = {s: [signal(f"{s}_read{n}") for n in range(2)] for s in "abcd"}

        s_weights, s_const, s_fused, s_fused_read = signal("s_weights"), signal("s_const"), signal("s_fused"), signal("s_fused_read")
        s_ha, s_xa, s_mask_i = signal("s_ha"), signal("s_xa"), signal("s_mask_i")
        s_q0_gather, s_k0_gather, s_q0_stack, s_k0_stack, s_m0_stack = (
            signal(n) for n in ("s_q0_gather", "s_k0_gather", "s_q0_stack", "s_k0_stack", "s_m0_stack"))
        s_masks1, s_q1_gather, s_k1_gather, s_q1_stack, s_k1_stack, s_m1_stack = (
            signal(n) for n in ("s_masks1", "s_q1_gather", "s_k1_gather", "s_q1_stack", "s_k1_stack", "s_m1_stack"))
        s_ctxd, s_out = signal("s_ctxd"), signal("s_out")
        s_mask_b = signal("s_mask_b")
        s_q0, s_k0, s_q1, s_k1 = (signal(n) for n in ("s_q0", "s_k0", "s_q1", "s_k1"))
        s_m0, s_m1 = signal("s_m0"), signal("s_m1")
        s_max1 = signal("s_max1")
        s_rc0, s_rc1 = signal("s_rc0"), signal("s_rc1")
        s_res0, s_resb, s_res1 = signal("s_res0"), signal("s_resb"), signal("s_res1")
        s_rms = signal("s_rms")
        s_exp1 = signal("s_exp1")
        s_ln = signal("s_ln")
        s_g, s_x2 = signal("s_g"), signal("s_x2")
        s_m2, s_rc2, s_p2n = signal("s_m2"), signal("s_rc2"), signal("s_p2n")
        s_m3, s_r3 = signal("s_m3"), signal("s_r3")

        def before(eng, sem, value):
            if not isinstance(value, int) or value > 0:
                eng.wait_ge(sem, value)

        def wait_made(eng, s, u, n):
            eng.wait_ge(made[s], u * tiles_of[s] + n + 1)

        def wait_read(eng, s, u, n):
            eng.wait_ge(read[s][n % 2], u * (tiles_of[s] // 2) + n // 2 + 1)

        def wait_bank(pe, s, u, n):
            before(pe, read[s][n % 2], u * (tiles_of[s] // 2) + n // 2)

        def before_made(eng, s, u, n):
            before(eng, made[s], (u - 1) * tiles_of[s] + n + 1)

        def before_read(eng, s, u, n):
            before(eng, read[s][n % 2], (u - 1) * (tiles_of[s] // 2) + n // 2 + 1)

        def tile(s, n):
            return bank[s][n % 2]

        def each_round(eng, steps):
            def one(i):
                for lag, name, *args in ROUND:
                    if name in steps and not (isinstance(i, int) and not 0 <= i - lag < UNITS):
                        steps[name](i - lag, *args)
            for i in range(THIRD + 1):
                one(i)
            with eng.Fori(THIRD + 1, UNITS) as i:
                one(i)
            for i in range(UNITS, UNITS + THIRD):
                one(i)

        block = stack.enter_context(nc.Block())

        @block.sync
        def _(sp):
            pairs = [(wq0, "wq0"), (wk0, "wk0"), (wv0, "wv0"), (cols, "cols"), (bv0, "bv0"), (ident, "ident"), (wo0, "wo0"),
                     (bo0, "bo0"), (w_up, "w_up"), (w_down, "w_down"), (b_down, "b_down"), (wq1, "wq1"), (wkv1, "wkv1"),
                     (wo1, "wo1"), (bo1, "bo1"), (gamma, "gamma"), (beta, "beta"), (wq2, "wq2"), (wk2, "wk2"), (wv2, "wv2"),
                     (bv2, "bv2"), (wq3, "wq3"), (wk3, "wk3"), (wv3, "wv3"), (wo3, "wo3")]
            for dst, name in pairs:
                src = w[name]
                if len(src.shape) == 1:
                    src = src.rearrange("(o f) -> o f", o=1).broadcast_to([P, src.shape[0]])
                sp.dma_start(dst if dst.shape[0] == P and name.endswith('3') else dst[:], src).then_inc(s_weights, 16)
            sp.wait_ge(s_weights, 16 * WEIGHTS)
            sp.wait_ge(s_const, CONSTANTS)

            def a_load(u):
                before_made(sp, "b", u, B_KV)
                sp.dma_start(h_t[:, :, :, 0, :], ctx_t[u]).then_inc(s_ha, 16)
                sp.dma_start(h_t[:, :, :, 1, :], x_t[u]).then_inc(s_ha, 16)
                before(sp, s_resb, u)
                sp.dma_start(x_a[:], x[u]).then_inc(s_xa, 16)
                before(sp, s_mask_b, u)
                sp.dma_start(mask_i[:], mask0[u]).then_inc(s_mask_i, 16)

            def a_stack(u):
                before_made(sp, "a", u, A_ST + 7 + A_NEXT)
                sp.wait_ge(s_q0, 4 * u + 4)
                for p, block_at in ((0, 0), (1, 3), (2, 5)):
                    for t in range(KT):
                        r = D0 * block_at + 8 * t
                        sp.dma_start(q0s[r:r + 8], q0p[:, p, t, :]).then_inc(s_q0_gather, 16)
                sp.wait_ge(s_k0, 4 * u + 4)
                for p in range(3):
                    for t in range(KT):
                        r = D0 * p + 8 * t
                        sp.dma_start(k0s[r:r + 8], k0p[:, p, t, :]).then_inc(s_k0_gather, 16)
                sp.wait_ge(s_mask_b, u + 1)
                sp.dma_start(k0s[MASK_ROW:MASK_ROW + 1],
                             mask_b[:].rearrange("o j s p -> o (j s p)").unsqueeze(1).broadcast_to([1, NH0, 2 * T])).then_inc(s_k0_stack, 16)
                sp.wait_ge(s_q0_gather, 16 * (6 * u + 6))
                for of, to in ((0, 1), (0, 2), (3, 4)):
                    sp.dma_start(q0s[D0 * to:D0 * to + D0], q0s[D0 * of:D0 * of + D0]).then_inc(s_q0_stack, 16)
                sp.wait_ge(s_k0_gather, 16 * (6 * u + 6))
                sp.dma_start(k0s[3 * D0:5 * D0], k0s[0:2 * D0]).then_inc(s_k0_stack, 16)
                sp.dma_start(k0s[5 * D0:6 * D0], k0s[0:D0]).then_inc(s_k0_stack, 16)

            def a_maxima(u):
                wait_read(sp, "a", u, A_M)
                sp.dma_start(q0s[MASK_ROW + 1:R0], m0t[:]).then_inc(s_m0_stack, 16)

            def b_load(u):
                before_made(sp, "c", u, C_PV + 1 + C_NEXT)
                sp.dma_start(m_l[:], mask1[u]).then_inc(s_masks1, 16)
                sp.dma_start(m_s[:], mask1_t[u]).then_inc(s_masks1, 16)

            def b_stack(u):
                before_made(sp, "c", u, C_ST + 7 + C_NEXT)
                sp.wait_ge(s_k1, 4 * u + 4)
                for p in range(3):
                    sp.dma_start(k1s[D1 * p:D1 * p + D1], k1p[:, p, :]).then_inc(s_k1_gather, 16)
                sp.wait_ge(s_q1, 4 * u + 4)
                for p in range(3):
                    for t in range(KT):
                        r = D1 * p + 4 * t
                        sp.dma_start(q1s[r:r + 4], q1p[:, p, t, :]).then_inc(s_q1_gather, 16)
                sp.wait_ge(s_k1_gather, 16 * (3 * u + 3))
                for of, to, n in ((1, 3, 2), (0, 5, 1), (2, 6, 1), (0, 7, 2)):
                    sp.dma_start(k1s[D1 * to:D1 * (to + n)], k1s[D1 * of:D1 * (of + n)]).then_inc(s_k1_stack, 16)
                sp.wait_ge(s_q1_gather, 16 * (6 * u + 6))
                for to in (3, 6):
                    sp.dma_start(q1s[D1 * to:D1 * (to + 3)], q1s[0:3 * D1]).then_inc(s_q1_stack, 16)

            def c_maxima(u):
                wait_read(sp, "c", u, C_M)
                sp.dma_start(q1s[S1:R1], m1t[:]).then_inc(s_m1_stack, 16)

            def d_load(u):
                before_made(sp, "d", u, D_VV)
                sp.dma_start(ctx_d[:], ctx[u]).then_inc(s_ctxd, 16)
                sp.dma_start(ctx_td[:], ctx_t[u]).then_inc(s_ctxd, 16)

            def d_text(u):
                wait_read(sp, "d", u, D_OUT)
                sp.dma_start(out[u], x3[:]).then_inc(s_out, 16)

            each_round(sp, dict(a_load=a_load, a_stack=a_stack, a_maxima=a_maxima, b_load=b_load, b_stack=b_stack,
                                c_maxima=c_maxima, d_load=d_load, d_text=d_text))
            sp.wait_ge(s_out, 16 * UNITS)

        @block.tensor
        def _(pe):
            def dense(dst, lhs, rhs):
                for t in range(KT):
                    mm = pe.matmul(dst, lhs(t), rhs(t), start=(t == 0), stop=(t == KT - 1))
                return mm

            pe.wait_ge(s_weights, 16 * WEIGHTS)
            for n, (left, right) in enumerate(((wk3, wq3), (wv3, wo3))):
                for m in range(KT):
                    mm = dense(bank["d"][n][:, m * H:(m + 1) * H], lambda t: left[:, t, m * P:(m + 1) * P], lambda t: right[:, t, :])
                mm.then_inc(s_fused, 1)
            pe.wait_ge(s_const, CONSTANTS)
            pe.wait_ge(s_fused_read, 2)

            def a_project(u):
                pe.wait_ge(s_ha, 16 * (2 * u + 2))
                wait_bank(pe, "a", u, A_Q)
                dst = tile("a", A_Q)
                for m in range(KT):
                    mm = dense(dst[:, m * T:(m + 1) * T].rearrange("p (j q) -> p j q", j=J), lambda t: wq0[:, t, m * P:(m + 1) * P], lambda t: h_t[:, t, :, 1, :])
                mm.then_inc(made["a"], 1)
                for m in range(KT):
                    wait_bank(pe, "a", u, A_K + m)
                    dense(tile("a", A_K + m)[:, :], lambda t: wk0[:, t, m * P:(m + 1) * P],
                          lambda t: h_t[:, t].rearrange("p j s q -> p (j s q)")).then_inc(made["a"], 1)

            def a_values(u):
                for j in range(J):
                    wait_bank(pe, "a", u, A_V + j)
                    for s in range(2):
                        mm = dense(tile("a", A_V + j)[:, s * H:(s + 1) * H], lambda t: h_t[:, t, j, s, :], lambda t: wv0[:, t, :])
                    mm.then_inc(made["a"], 1)

            def b_keys(u):
                wait_bank(pe, "b", u, B_KV)
                dense(tile("b", B_KV)[:, 0:T].rearrange("p (j q) -> p j q", j=J), lambda t: wkv1[:, t, :], lambda t: h_t[:, t, :, 0, :]).then_inc(made["b"], 1)

            def a_scores(u, j, half):
                if (j, half) == (0, 0):
                    pe.wait_ge(s_q0_stack, 16 * (3 * u + 3))
                    pe.wait_ge(s_q0_gather, 16 * (6 * u + 6))
                    pe.wait_ge(s_k0_stack, 16 * (3 * u + 3))
                    pe.wait_ge(s_k0_gather, 16 * (6 * u + 6))
                for n in range(4 * half, 4 * half + 4):
                    k = A_S + 8 * j + n
                    wait_bank(pe, "a", u, k)
                    for h in (2 * n, 2 * n + 1):
                        mm = pe.matmul(tile("a", k)[:, (h % 2) * 2 * P:(h % 2 + 1) * 2 * P], q0s[0:S0 + 1, h, j * P:(j + 1) * P],
                                       k0s[0:S0 + 1, h, j * 2 * P:(j + 1) * 2 * P], start=True, stop=True)
                    mm.then_inc(made["a"], 1)

            def a_maxima(u):
                pe.wait_ge(s_m0, 4 * u + 4)
                wait_bank(pe, "a", u, A_M)
                for j in range(J):
                    mm = pe.transpose(tile("a", A_M).bitcast(BF16)[0:M0_COLS * NH0, j * P:(j + 1) * P], m0p[:, j].rearrange("p c h -> p (c h)"), ident_bf[:])
                mm.then_inc(made["a"], 1)

            def a_weights(u, j, s):
                if (j, s) == (0, 0):
                    pe.wait_ge(s_m0_stack, 16 * (u + 1))
                for g in range(4):
                    k = A_ST + A_NEXT * j + 4 * s + g
                    wait_bank(pe, "a", u, k)
                    for h in range(4 * g, 4 * g + 4):
                        mm = pe.matmul(tile("a", k)[:, (h % 4) * P:(h % 4 + 1) * P], k0s[0:R0, h, (2 * j + s) * P:(2 * j + s + 1) * P],
                                       q0s[0:R0, h, j * P:(j + 1) * P], start=True, stop=True)
                    mm.then_inc(made["a"], 1)

            def a_attend(u, j):
                wait_read(pe, "a", u, A_ST + A_NEXT * j + 7)
                wait_bank(pe, "a", u, A_PV + A_NEXT * j)
                for g in range(4):
                    for s in range(2):
                        for c in range(4):
                            mm = pe.matmul(tile("a", A_PV + A_NEXT * j)[32 * c:32 * c + 32, g * P:(g + 1) * P], v0[:, j, s, 4 * g + c, :],
                                           p0[:, s, 4 * g + c, :], start=(s == 0), stop=(s == 1), tile_position=(0, 32 * c))
                mm.then_inc(made["a"], 1)

            def a_turn(u, j):
                wait_read(pe, "a", u, A_PV + A_NEXT * j)
                wait_bank(pe, "a", u, A_OT + A_NEXT * j)
                for g in range(4):
                    mm = pe.transpose(tile("a", A_OT + A_NEXT * j)[:, g * P:(g + 1) * P], o0t[:, g * P:(g + 1) * P], ident[:])
                mm.then_inc(made["a"], 1)

            def a_join(u):
                wait_bank(pe, "a", u, A_FT)
                wait_read(pe, "a", u, A_OT + A_NEXT)
                for j in range(J):
                    for t in range(KT):
                        mm = pe.transpose(tile("a", A_FT)[:, t * T + j * P:t * T + (j + 1) * P], o0[:, j, t * P:(t + 1) * P], ident[:])
                mm.then_inc(made["a"], 1)

            def a_out(u):
                wait_read(pe, "a", u, A_FT)
                wait_bank(pe, "a", u, A_OUT)
                for j in range(J):
                    mm = dense(tile("a", A_OUT)[:, j * H:(j + 1) * H], lambda t: f0t[:, t, j * P:(j + 1) * P], lambda t: wo0[:, t, :])
                mm.then_inc(made["a"], 1)

            def b_norm(u):
                pe.wait_ge(s_rms, 5 * u + 5)
                wait_bank(pe, "b", u, B_NT)
                for j in range(J):
                    for t in range(KT):
                        mm = pe.transpose(tile("b", B_NT)[:, t * T + j * P:t * T + (j + 1) * P], y0n[:, j, t * P:(t + 1) * P], ident[:])
                mm.then_inc(made["b"], 1)

            def b_up(u, n):
                if n == 0:
                    wait_read(pe, "b", u, B_NT)
                wait_bank(pe, "b", u, B_UP + n)
                for m in (2 * n, 2 * n + 1):
                    mm = dense(tile("b", B_UP + n)[:, (m % 2) * T:(m % 2 + 1) * T], lambda t: w_up[:, t, m * P:(m + 1) * P], lambda t: n_t[:, t, :])
                mm.then_inc(made["b"], 1)

            def b_down_(u, j):
                if j == 0:
                    wait_read(pe, "b", u, B_UP + 3)
                    wait_bank(pe, "b", u, B_DOWN)
                for m in range(MT):
                    mm = pe.matmul(tile("b", B_DOWN)[:, j * H:(j + 1) * H], up[:, m, j * P:(j + 1) * P], w_down[:, m, :], start=(m == 0), stop=(m == MT - 1))
                if j == J - 1:
                    mm.then_inc(made["b"], 1)

            def b_turn(u):
                wait_read(pe, "b", u, B_DOWN)
                wait_bank(pe, "b", u, B_XT)
                for j in range(J):
                    for t in range(KT):
                        mm = pe.transpose(tile("b", B_XT)[:, t * T + j * P:t * T + (j + 1) * P], x1[:, j, t * P:(t + 1) * P], ident[:])
                mm.then_inc(made["b"], 1)

            def b_project(u):
                wait_read(pe, "b", u, B_XT)
                wait_bank(pe, "b", u, B_Q)
                for m in range(KT):
                    mm = dense(tile("b", B_Q)[:, m * T:(m + 1) * T], lambda t: wq1[:, t, m * P:(m + 1) * P], lambda t: x1_t[:, t, :])
                mm.then_inc(made["b"], 1)
                wait_read(pe, "b", u, B_KV)
                wait_bank(pe, "b", u, B_V)
                for j in range(J):
                    mm = pe.transpose(tile("b", B_V)[:, j * P:(j + 1) * P], kv1f[:, j * P:(j + 1) * P], ident[:])
                mm.then_inc(made["b"], 1)

            def c_scores(u, j, half):
                if (j, half) == (0, 0):
                    pe.wait_ge(s_q1_stack, 16 * (2 * u + 2))
                    pe.wait_ge(s_q1_gather, 16 * (6 * u + 6))
                    pe.wait_ge(s_k1_stack, 16 * (4 * u + 4))
                    pe.wait_ge(s_k1_gather, 16 * (3 * u + 3))
                for kv in range(4 * half, 4 * half + 4):
                    k = C_S + 8 * j + kv
                    wait_bank(pe, "c", u, k)
                    for g in range(G1):
                        mm = pe.matmul(tile("c", k)[:, g * P:(g + 1) * P], q1s[0:S1, kv * G1 + g, j * P:(j + 1) * P],
                                       k1s[0:S1, kv, j * P:(j + 1) * P], start=True, stop=True)
                    mm.then_inc(made["c"], 1)

            def c_maxima(u):
                pe.wait_ge(s_m1, 4 * u + 4)
                wait_bank(pe, "c", u, C_M)
                for j in range(J):
                    mm = pe.transpose(tile("c", C_M).bitcast(BF16)[0:3 * NH1, j * P:(j + 1) * P], m1p[:, j].rearrange("p c h -> p (c h)"), ident_bf[:])
                mm.then_inc(made["c"], 1)

            def c_weights(u, j, half):
                if (j, half) == (0, 0):
                    pe.wait_ge(s_m1_stack, 16 * (u + 1))
                for kv in range(4 * half, 4 * half + 4):
                    k = C_ST + C_NEXT * j + kv
                    wait_bank(pe, "c", u, k)
                    pe.matmul(tile("c", k)[:, :].rearrange("p (g q) -> p g q", g=G1), k1s[0:R1, kv, j * P:(j + 1) * P],
                              q1s[0:R1, kv * G1:(kv + 1) * G1, j * P:(j + 1) * P], start=True, stop=True).then_inc(made["c"], 1)

            def c_attend(u, j):
                if j == 0:
                    wait_read(pe, "b", u, B_V)
                pe.wait_ge(s_exp1, 16 * u + 8 * j + 8)
                for half in range(2):
                    k = C_PV + C_NEXT * j + half
                    wait_bank(pe, "c", u, k)
                    for c in range(4):
                        kv = 4 * half + c
                        mm = pe.matmul(tile("c", k)[32 * c:32 * c + 32, :], v1[:, j, kv, :],
                                       p1[:, kv * G1:(kv + 1) * G1, :].rearrange("p g q -> p (g q)"), start=True, stop=True, tile_position=(0, 32 * c))
                    mm.then_inc(made["c"], 1)

            def c_turn(u, j):
                for half in range(2):
                    k = C_TR + C_NEXT * j + half
                    wait_read(pe, "c", u, k - 2)
                    wait_bank(pe, "c", u, k)
                    for g in range(G1):
                        mm = pe.transpose(tile("c", k)[:, g * P:(g + 1) * P], o1t[:, half, g * P:(g + 1) * P], ident[:])
                    mm.then_inc(made["c"], 1)

            def c_join(u):
                wait_bank(pe, "c", u, C_FT)
                wait_read(pe, "c", u, C_TR + C_NEXT + 1)
                for j in range(J):
                    for t in range(KT):
                        mm = pe.transpose(tile("c", C_FT)[:, t * T + j * P:t * T + (j + 1) * P], o1[:, j, t * P:(t + 1) * P], ident[:])
                mm.then_inc(made["c"], 1)

            def c_out(u):
                wait_read(pe, "c", u, C_FT)
                for j in range(J):
                    wait_bank(pe, "c", u, C_OUT + j)
                    dense(tile("c", C_OUT + j)[:, 0:H], lambda t: f1t[:, t, j * P:(j + 1) * P], lambda t: wo1[:, t, :]).then_inc(made["c"], 1)

            def d_context(u):
                pe.wait_ge(s_ctxd, 16 * (2 * u + 2))
                wait_bank(pe, "d", u, D_K)
                pe.matmul(tile("d", D_K)[0:D2, :], wk2[:], ctx_d[:].rearrange("p j n -> p (j n)"), start=True, stop=True).then_inc(made["d"], 1)
                wait_bank(pe, "d", u, D_V)
                for j in range(J):
                    for t in range(KT):
                        mm = pe.matmul(tile("d", D_V)[:, (KT * j + t) * P:(KT * j + t + 1) * P], ctx_d[:, j, t * P:(t + 1) * P], wv2[:], start=True, stop=True)
                mm.then_inc(made["d"], 1)

            def d_context_products(u):
                wait_bank(pe, "d", u, D_KK)
                for m in range(KT):
                    mm = dense(tile("d", D_KK)[:, m * T:(m + 1) * T], lambda t: key3[:, t, m * P:(m + 1) * P], lambda t: ctx_td[:, t, :])
                mm.then_inc(made["d"], 1)
                wait_bank(pe, "d", u, D_VV)
                for j in range(J):
                    mm = dense(tile("d", D_VV)[:, j * H:(j + 1) * H], lambda t: ctx_td[:, t, j * P:(j + 1) * P], lambda t: val3[:, t, :])
                mm.then_inc(made["d"], 1)

            def d_query(u):
                pe.wait_ge(s_x2, u + 1)
                wait_bank(pe, "d", u, D_Q)
                pe.matmul(tile("d", D_Q)[0:D2, :], wq2[:], x2[:].rearrange("p j n -> p (j n)"), start=True, stop=True).then_inc(made["d"], 1)

            def d_scores(u, j):
                wait_read(pe, "d", u, D_Q)
                wait_bank(pe, "d", u, D_S + j)
                for t in range(KT):
                    mm = pe.matmul(tile("d", D_S + j)[:, t * H:(t + 1) * H], q2[:, j, t * P:(t + 1) * P], k2[:, j, :], start=True, stop=True)
                mm.then_inc(made["d"], 1)

            def d_attend(u):
                for j in range(J):
                    pe.wait_ge(s_p2n, 2 * u + j + 1)
                    wait_bank(pe, "d", u, D_PT + j)
                    for m in range(KT):
                        for t in range(KT):
                            mm = pe.transpose(tile("d", D_PT + j)[:, m * H + t * P:m * H + (t + 1) * P], p2[:, j, t, m * P:(m + 1) * P], ident[:])
                    mm.then_inc(made["d"], 1)
                wait_bank(pe, "d", u, D_PV)
                for j in range(J):
                    wait_read(pe, "d", u, D_PT + j)
                    for m in range(KT):
                        mm = pe.matmul(tile("d", D_PV)[:, j * H:(j + 1) * H], v2[:, j, m, :], p2t[:, j, m, :], start=(m == 0), stop=(m == KT - 1))
                mm.then_inc(made["d"], 1)

            def d_x(u):
                wait_read(pe, "d", u, D_PV)
                wait_bank(pe, "d", u, D_XT)
                for j in range(J):
                    for t in range(KT):
                        mm = pe.transpose(tile("d", D_XT)[:, t * T + j * P:t * T + (j + 1) * P], x3[:, j, t * P:(t + 1) * P], ident[:])
                mm.then_inc(made["d"], 1)

            def d_text_scores(u):
                wait_read(pe, "d", u, D_XT)
                wait_bank(pe, "d", u, D_S3)
                for j in range(J):
                    mm = dense(tile("d", D_S3)[:, j * P:(j + 1) * P], lambda t: x3_t[:, t, j * P:(j + 1) * P], lambda t: kk3[:, t, j * P:(j + 1) * P])
                mm.then_inc(made["d"], 1)

            def d_text(u):
                wait_read(pe, "d", u, D_S3)
                wait_bank(pe, "d", u, D_PT3)
                for j in range(J):
                    mm = pe.transpose(tile("d", D_PT3)[:, j * P:(j + 1) * P], p3[:, j, :], ident[:])
                mm.then_inc(made["d"], 1)
                wait_read(pe, "d", u, D_PT3)
                wait_bank(pe, "d", u, D_OUT)
                for j in range(J):
                    mm = pe.matmul(tile("d", D_OUT)[:, j * H:(j + 1) * H], p3t[:, j, :], vv3[:, j, :], start=True, stop=True)
                mm.then_inc(made["d"], 1)

            each_round(pe, dict(a_project=a_project, a_values=a_values, a_scores=a_scores, a_maxima=a_maxima, a_weights=a_weights,
                                a_attend=a_attend, a_turn=a_turn, a_join=a_join, a_out=a_out, b_keys=b_keys, b_norm=b_norm, b_up=b_up,
                                b_down=b_down_, b_turn=b_turn, b_project=b_project, c_scores=c_scores, c_maxima=c_maxima,
                                c_weights=c_weights, c_attend=c_attend, c_turn=c_turn, c_join=c_join, c_out=c_out,
                                d_context=d_context, d_context_products=d_context_products, d_query=d_query, d_scores=d_scores,
                                d_attend=d_attend, d_x=d_x, d_text_scores=d_text_scores, d_text=d_text))

        @block.scalar
        def _(act):
            act.wait_ge(s_weights, 16 * WEIGHTS)
            act.activation(bq1[:], bq1_raw, ACT.Copy, scale=float(D1) ** -0.5).then_inc(s_const, 1)
            act.activation(ident_bf[:], ident[:], ACT.Copy).then_inc(s_const, 1)
            for n, dst in enumerate((key3, val3)):
                act.wait_ge(s_fused, n + 1)
                act.activation(dst[:].rearrange("p t h -> p (t h)"), bank["d"][n][:, :], ACT.Copy).then_inc(s_fused_read, 1)
            act.wait_ge(s_const, CONSTANTS)

            def a_project(u):
                wait_made(act, "a", u, A_Q)
                for m in range(KT):
                    ins = act.activation(q0f[:, m, :], tile("a", A_Q)[:, m * T:(m + 1) * T], ACT.Identity, bias=bq0[:, m:m + 1])
                ins.then_inc(read["a"][A_Q % 2], 1)
                for m in range(KT):
                    wait_made(act, "a", u, A_K + m)
                    act.activation(k0f[:, m, :], tile("a", A_K + m)[:, :], ACT.Identity, bias=bk0[:, m:m + 1]).then_inc(read["a"][(A_K + m) % 2], 1)

            def b_keys(u):
                before(act, s_k1, 4 * u)
                before_made(act, "b", u, B_V)
                wait_made(act, "b", u, B_KV)
                act.activation(kv1f[:], tile("b", B_KV)[:, 0:T], ACT.Identity, bias=bkv1).then_inc(read["b"][B_KV % 2], 1)

            def a_weights(u, j, s):
                if (j, s) == (0, 0):
                    before_made(act, "b", u, B_DOWN)
                for g in range(4):
                    k = A_ST + A_NEXT * j + 4 * s + g
                    wait_made(act, "a", u, k)
                    act.activation(p0[:, s, 4 * g:4 * g + 4, :].rearrange("p h q -> p (h q)"), tile("a", k)[:, :], ACT.Exp,
                                   scale=1.0 / D0).then_inc(read["a"][k % 2], 1)

            def a_attend(u, j):
                wait_made(act, "a", u, A_PV + A_NEXT * j)
                act.activation(o0t[:], tile("a", A_PV + A_NEXT * j)[:, :], ACT.Copy).then_inc(read["a"][(A_PV + A_NEXT * j) % 2], 1)

            def a_join(u):
                wait_made(act, "a", u, A_FT)
                act.activation(f0t.rearrange("p t q -> p (t q)"), tile("a", A_FT)[:, :], ACT.Copy).then_inc(read["a"][A_FT % 2], 1)

            def a_out(u):
                before(act, s_rms, 5 * u)
                before_made(act, "b", u, B_NT)
                wait_read(act, "a", u, A_OUT)
                for j in range(J):
                    act.activation(y0n[:, j, :], y0[:, j, :], ACT.Square, accum_out=ss0[:, j:j + 1]).then_inc(s_rms, 1)

            def b_norm(u):
                before_made(act, "b", u, B_UP + 3)
                wait_made(act, "b", u, B_NT)
                for t in range(KT):
                    ins = act.activation(n_t[:, t, :], tile("b", B_NT)[:, t * T:(t + 1) * T], ACT.Copy, scale=norm_w[:, t:t + 1])
                ins.then_inc(read["b"][B_NT % 2], 1)

            def b_up_(u, n):
                if n == 0:
                    wait_made(act, "a", u, A_PV + A_NEXT)
                wait_made(act, "b", u, B_UP + n)
                for m in (2 * n, 2 * n + 1):
                    ins = act.activation(up[:, m, :], tile("b", B_UP + n)[:, (m % 2) * T:(m % 2 + 1) * T], ACT.Gelu_apprx_tanh, bias=b_up[:, m:m + 1])
                ins.then_inc(read["b"][(B_UP + n) % 2], 1)

            def b_turn(u):
                wait_made(act, "b", u, B_XT)
                act.activation(x1_t[:].rearrange("p t q -> p (t q)"), tile("b", B_XT)[:, :], ACT.Copy).then_inc(read["b"][B_XT % 2], 1)

            def b_project(u):
                before_made(act, "c", u, C_PV + 1 + C_NEXT)
                wait_made(act, "b", u, B_Q)
                for m in range(KT):
                    ins = act.activation(q1f[:, m, :], tile("b", B_Q)[:, m * T:(m + 1) * T], ACT.Identity, bias=bq1[:, m:m + 1], scale=float(D1) ** -0.5)
                ins.then_inc(read["b"][B_Q % 2], 1)

            def c_weights(u, j, half):
                for kv in range(4 * half, 4 * half + 4):
                    wait_read(act, "c", u, C_ST + C_NEXT * j + kv)
                    rows = p1[:, kv * G1:(kv + 1) * G1, :]
                    act.activation(rows, rows, ACT.Exp).then_inc(s_exp1, 1)

            def c_attend(u, j):
                for half in range(2):
                    k = C_PV + C_NEXT * j + half
                    wait_made(act, "c", u, k)
                    act.activation(o1t[:, half, :], tile("c", k)[:, :], ACT.Copy).then_inc(read["c"][k % 2], 1)

            def c_join(u):
                wait_made(act, "c", u, C_FT)
                act.activation(f1t[:].rearrange("p t q -> p (t q)"), tile("c", C_FT)[:, :], ACT.Copy).then_inc(read["c"][C_FT % 2], 1)

            def d_context(u):
                wait_made(act, "d", u, D_K)
                act.activation(k2[:].rearrange("p j n -> p (j n)"), tile("d", D_K)[0:D2, :], ACT.Identity, bias=bk2).then_inc(read["d"][D_K % 2], 1)

            def d_context_products(u):
                wait_made(act, "d", u, D_KK)
                act.activation(kk3[:].rearrange("p t s -> p (t s)"), tile("d", D_KK)[:, :], ACT.Copy).then_inc(read["d"][D_KK % 2], 1)
                wait_made(act, "d", u, D_VV)
                act.activation(vv3[:].rearrange("p j o -> p (j o)"), tile("d", D_VV)[:, :], ACT.Copy).then_inc(read["d"][D_VV % 2], 1)

            def d_query(u):
                wait_made(act, "d", u, D_Q)
                act.activation(q2[:].rearrange("p j n -> p (j n)"), tile("d", D_Q)[0:D2, :], ACT.Identity, bias=bq2).then_inc(read["d"][D_Q % 2], 1)

            def d_scores(u, j):
                before(act, s_p2n, 2 * (u - 1) + j + 1)
                act.wait_ge(s_m2, 2 * u + j + 1)
                for t in range(KT):
                    ins = act.activation(p2[:, j, t, :], tile("d", D_S + j)[:, t * H:(t + 1) * H], ACT.Exp, bias=m2[:, j, t:t + 1],
                                         accum_out=sum2[:, j, t:t + 1])
                ins.then_inc(read["d"][(D_S + j) % 2], 1)

            def d_attend(u):
                for j in range(J):
                    wait_made(act, "d", u, D_PT + j)
                    act.activation(p2t[:, j].rearrange("p m n -> p (m n)"), tile("d", D_PT + j)[:, :], ACT.Copy).then_inc(read["d"][(D_PT + j) % 2], 1)

            def d_x(u):
                wait_made(act, "d", u, D_XT)
                act.activation(x3_t.rearrange("p t q -> p (t q)"), tile("d", D_XT)[:, :], ACT.Copy).then_inc(read["d"][D_XT % 2], 1)

            def d_text_scores(u):
                act.wait_ge(s_m3, 2 * u + 2)
                for j in range(J):
                    ins = act.activation(p3[:, j, :], tile("d", D_S3)[:, j * P:(j + 1) * P], ACT.Exp, bias=m3s[:, j:j + 1], scale=1.0 / 16,
                                         accum_out=sum3[:, j:j + 1])
                ins.then_inc(read["d"][D_S3 % 2], 1)

            each_round(act, dict(a_project=a_project, a_weights=a_weights, a_attend=a_attend, a_join=a_join, a_out=a_out, b_keys=b_keys,
                                 b_norm=b_norm, b_up=b_up_, b_turn=b_turn, b_project=b_project, c_weights=c_weights,
                                 c_attend=c_attend, c_join=c_join, d_context=d_context, d_context_products=d_context_products,
                                 d_query=d_query, d_scores=d_scores, d_attend=d_attend, d_x=d_x, d_text_scores=d_text_scores))

        @block.vector
        def _(dve):
            dve.memset(q0s[MASK_ROW:P], 1.0).then_inc(s_const, 1)
            dve.memset(k0s[MASK_ROW:P], 1.0).then_inc(s_const, 1)
            dve.memset(mask_b[:, :, 1, :], 0.0).then_inc(s_const, 1)
            dve.memset(k1s[64:P], 1.0).then_inc(s_const, 1)
            dve.memset(m0p[:, :, 3:M0_COLS, :], 0.0).then_inc(s_const, 1)
            dve.memset(v0[:, :, :, :, D0:D0 + 1], 1.0).then_inc(s_const, 1)
            dve.memset(v0[:, :, :, :, D0 + 1:OUT_W], 0.0).then_inc(s_const, 1)
            dve.memset(v1[:, :, :, D1:D1 + 1], 1.0).then_inc(s_const, 1)
            dve.memset(v1[:, :, :, D1 + 1:OUT_W], 0.0).then_inc(s_const, 1)
            dve.wait_ge(s_weights, 16 * WEIGHTS)
            dve.wait_ge(s_const, CONSTANTS)

            def high(u, full, pieces, sem, gathered, dmas):
                before(dve, gathered, 16 * dmas * u)
                dve.tensor_copy(pieces, full).then_inc(sem, 1)

            def middle(u, rest, pieces, sem):
                dve.wait_ge(sem, 4 * u + 2)
                dve.tensor_copy(pieces, rest).then_inc(sem, 1)

            def split_maxima(u, m, rest, pieces, sem):
                dve.tensor_copy(pieces[:, :, 0, :], m).then_inc(sem, 1)
                dve.wait_ge(sem, 4 * u + 1)
                dve.tensor_tensor(rest, m, pieces[:, :, 0, :], ALU.subtract).then_inc(sem, 1)
                dve.wait_ge(sem, 4 * u + 2)
                dve.tensor_copy(pieces[:, :, 1, :], rest).then_inc(sem, 1)
                dve.wait_ge(sem, 4 * u + 3)
                dve.tensor_tensor(pieces[:, :, 2, :], rest, pieces[:, :, 1, :], ALU.subtract).then_inc(sem, 1)

            def a_project(u):
                before(dve, s_k0_stack, 16 * 3 * u)
                dve.wait_ge(s_mask_i, 16 * (u + 1))
                dve.tensor_scalar(mask_b[:, :, 0, :], mask_i[:], 0.0, MASKED, ALU.is_equal, ALU.mult).then_inc(s_mask_b, 1)
                wait_read(dve, "a", u, A_Q)
                high(u, q0f, q0p[:, 0], s_q0, s_q0_gather, 6)
                for m in range(KT):
                    wait_read(dve, "a", u, A_K + m)
                high(u, k0f, k0p[:, 0], s_k0, s_k0_gather, 6)

            def a_values(u):
                for j in range(J):
                    wait_made(dve, "a", u, A_V + j)
                    dve.tensor_tensor(v0[:, j, :, :, 0:D0], tile("a", A_V + j)[:, :].rearrange("p (s h d) -> p s h d", s=2, h=NH0),
                                      bv0[:].rearrange("p (o h d) -> p o h d", o=1, h=NH0).broadcast_to([P, 2, NH0, D0]),
                                      ALU.add).then_inc(read["a"][(A_V + j) % 2], 1)

            def a_stack(u):
                middle(u, q0f, q0p[:, 1], s_q0)
                middle(u, k0f, k0p[:, 1], s_k0)

            def a_scores(u, j, half):
                if (j, half) == (0, 0):
                    before(dve, s_m0, 4 * u)
                for n in range(4 * half, 4 * half + 4):
                    k = A_S + 8 * j + n
                    wait_made(dve, "a", u, k)
                    dve.tensor_reduce(m0[:, j, 2 * n:2 * n + 2], tile("a", k)[:, :].rearrange("p (h n) -> p h n", h=2), AX_X, ALU.max,
                                      negate=True).then_inc(read["a"][k % 2], 1)

            def a_maxima(u):
                for n in (14, 15):
                    wait_read(dve, "a", u, A_S + n)
                split_maxima(u, m0[:], m0r[:], m0p, s_m0)
                before(dve, s_m0_stack, 16 * u)
                wait_made(dve, "a", u, A_M)
                dve.tensor_copy(m0t[:], tile("a", A_M).bitcast(BF16)[0:3 * NH0, 0:T]).then_inc(read["a"][A_M % 2], 1)

            def a_turn(u, j):
                heads = tile("a", A_OT + A_NEXT * j)[:, :].rearrange("p (h e) -> p h e", h=NH0)
                wait_made(dve, "a", u, A_OT + A_NEXT * j)
                dve.reciprocal(rc0[:, j, :].unsqueeze(2), heads[:, :, D0:D0 + 1]).then_inc(s_rc0, 1)
                dve.wait_ge(s_rc0, 2 * u + j + 1)
                dve.tensor_tensor(o0[:, j, :].rearrange("p (h d) -> p h d", h=NH0), heads[:, :, 0:D0],
                                  rc0[:, j, :].unsqueeze(2).broadcast_to([P, NH0, D0]), ALU.mult).then_inc(read["a"][(A_OT + A_NEXT * j) % 2], 1)

            def a_out(u):
                dve.wait_ge(s_res0, u + 1)
                wait_made(dve, "a", u, A_OUT)
                dve.tensor_tensor(y0[:], tile("a", A_OUT)[:, :].rearrange("p (j h) -> p j h", j=J), res0[:], ALU.add).then_inc(read["a"][A_OUT % 2], 1)

            def a_norm(u):
                dve.wait_ge(s_rms, 5 * u + 2)
                dve.tensor_scalar(ms0[:], ss0[:], 1.0 / H, EPS, ALU.mult, ALU.add).then_inc(s_rms, 1)
                dve.wait_ge(s_rms, 5 * u + 4)
                for j in range(J):
                    ins = dve.tensor_scalar(y0n[:, j, :], y0[:, j, :], rs0[:, j:j + 1], None, ALU.mult)
                ins.then_inc(s_rms, 1)

            def b_turn(u):
                dve.wait_ge(s_resb, u + 1)
                before(dve, s_res1, u)
                wait_made(dve, "b", u, B_DOWN)
                dve.tensor_tensor(x1[:], tile("b", B_DOWN)[:, :].rearrange("p (j h) -> p j h", j=J), res_b[:], ALU.add).then_inc(read["b"][B_DOWN % 2], 1)

            def b_project(u):
                wait_read(dve, "b", u, B_Q)
                high(u, q1f, q1p[:, 0], s_q1, s_q1_gather, 6)
                wait_read(dve, "b", u, B_KV)
                high(u, kv1f[0:KV1 * D1], k1p[:, 0], s_k1, s_k1_gather, 3)
                before_made(dve, "c", u, C_PV + 1 + C_NEXT)
                wait_made(dve, "b", u, B_V)
                dve.tensor_copy(v1[:, :, :, 0:D1], tile("b", B_V)[:, 0:T].rearrange("p (j c) -> p j c", j=J)[:, :, KV1 * D1:]
                                .rearrange("p j (k d) -> p j k d", d=D1)).then_inc(read["b"][B_V % 2], 1)

            def b_stack(u):
                middle(u, k1r, k1p[:, 1], s_k1)
                middle(u, q1f, q1p[:, 1], s_q1)

            def c_scores(u, j, half):
                if (j, half) == (0, 0):
                    dve.wait_ge(s_masks1, 16 * (2 * u + 2))
                    before(dve, s_m1, 4 * u)

                def maxima(n):
                    wait_read(dve, "c", u, C_S + n)
                    dve.tensor_reduce(m1[:, j, (n % 8) * G1:(n % 8 + 1) * G1], sm[n % 2][:], AX_X, ALU.max, negate=True).then_inc(s_max1, 1)

                first = 8 * j + 4 * half
                for n in range(first, first + 4):
                    if n >= 2:
                        dve.wait_ge(s_max1, 16 * u + n - 1)
                    elif not isinstance(u, int) or u > 0:
                        dve.wait_ge(s_max1, 16 * u + n - 1)
                    wait_made(dve, "c", u, C_S + n)
                    dve.tensor_tensor(sm[n % 2][:], tile("c", C_S + n)[:, :].rearrange("p (g s) -> p g s", g=G1),
                                      m_l[:, j:j + 1, :].broadcast_to([P, G1, P]), ALU.add).then_inc(read["c"][(C_S + n) % 2], 1)
                    if n > first:
                        maxima(n - 1)
                maxima(first + 3)

            def c_maxima(u):
                dve.wait_ge(s_max1, 16 * u + 16)
                split_maxima(u, m1[:], m1r[:], m1p, s_m1)
                before(dve, s_m1_stack, 16 * u)
                wait_made(dve, "c", u, C_M)
                dve.tensor_copy(m1t[:], tile("c", C_M).bitcast(BF16)[0:3 * NH1, 0:T]).then_inc(read["c"][C_M % 2], 1)

            def c_weights(u, j, half):
                if (j, half) == (0, 0):
                    before_made(dve, "d", u, D_OUT)
                    dve.wait_ge(s_q1, 4 * u + 4)
                    dve.wait_ge(s_k1, 4 * u + 4)
                for kv in range(4 * half, 4 * half + 4):
                    k = C_ST + C_NEXT * j + kv
                    wait_made(dve, "c", u, k)
                    dve.tensor_tensor(p1[:, kv * G1:(kv + 1) * G1, :], tile("c", k)[:, :].rearrange("p (g s) -> p g s", g=G1),
                                      m_s[:, j:j + 1, :].broadcast_to([P, G1, P]), ALU.add).then_inc(read["c"][k % 2], 1)

            def c_turn(u, j):
                for half in range(2):
                    k = C_TR + C_NEXT * j + half
                    heads = tile("c", k)[:, :].rearrange("p (g k e) -> p g k e", g=G1, k=4)
                    wait_made(dve, "c", u, k)
                    dve.reciprocal(rc1[:, half].unsqueeze(3), heads[:, :, :, D1:D1 + 1]).then_inc(s_rc1, 1)
                    dve.wait_ge(s_rc1, 4 * u + 2 * j + half + 1)
                    dve.tensor_tensor(o1[:, j, half * P:(half + 1) * P].rearrange("p (k g d) -> p g k d", k=4, g=G1), heads[:, :, :, 0:D1],
                                      rc1[:, half].unsqueeze(3).broadcast_to([P, G1, 4, D1]), ALU.mult).then_inc(read["c"][k % 2], 1)

            def c_out(u):
                dve.wait_ge(s_res1, u + 1)
                before(dve, s_x2, u)
                for j in range(J):
                    wait_made(dve, "c", u, C_OUT + j)
                    dve.tensor_tensor(y1[:, j, :], tile("c", C_OUT + j)[:, 0:H], res1[:, j, :], ALU.add).then_inc(read["c"][(C_OUT + j) % 2], 1)

            def c_norm(u):
                for j in range(J):
                    wait_read(dve, "c", u, C_OUT + j)
                    dve.bn_stats(st1[:, j, :], y1[:, j, :]).then_inc(s_ln, 1)
                dve.wait_ge(s_ln, 8 * u + 2)
                dve.memset(spare[:], 0.0)
                for j in range(J):
                    dve.bn_aggr(mv1[:, j, :], st1[:, j, :]).then_inc(s_ln, 1)
                dve.wait_ge(s_ln, 8 * u + 4)
                dve.tensor_scalar(ve1[:], mv1[:, :, 1], EPS, None, ALU.add).then_inc(s_ln, 1)
                dve.wait_ge(s_ln, 8 * u + 6)
                for j in range(J):
                    dve.tensor_scalar(y1[:, j, :], y1[:, j, :], mv1[:, j, 0:1], rs1[:, j:j + 1], ALU.subtract, ALU.mult).then_inc(s_ln, 1)

            def d_context(u):
                wait_made(dve, "d", u, D_V)
                dve.tensor_tensor(v2[:].rearrange("p j t c -> p (j t) c"), tile("d", D_V)[:, :].rearrange("p (j c) -> p j c", j=J * KT),
                                  bv2[:].unsqueeze(1).broadcast_to([P, J * KT, P]), ALU.add).then_inc(read["d"][D_V % 2], 1)

            def d_scores(u, j):
                wait_made(dve, "d", u, D_S + j)
                dve.tensor_reduce(m2[:, j, :], tile("d", D_S + j)[:, :].rearrange("p (t m) -> p t m", t=KT), AX_X, ALU.max,
                                  negate=True).then_inc(s_m2, 1)

            def d_attend(u):
                for j in range(J):
                    wait_read(dve, "d", u, D_S + j)
                    dve.reciprocal(rc2[:, j, :], sum2[:, j, :]).then_inc(s_rc2, 1)
                    dve.wait_ge(s_rc2, 2 * u + j + 1)
                    for t in range(KT):
                        ins = dve.tensor_scalar(p2[:, j, t, :], p2[:, j, t, :], rc2[:, j, t:t + 1], None, ALU.mult)
                    ins.then_inc(s_p2n, 1)
                before(dve, s_out, 16 * u)
                wait_made(dve, "d", u, D_PV)
                dve.tensor_tensor(x3[:], tile("d", D_PV)[:, :].rearrange("p (j n) -> p j n", j=J), x2[:], ALU.add).then_inc(read["d"][D_PV % 2], 1)

            def d_text_scores(u):
                wait_made(dve, "d", u, D_S3)
                dve.tensor_reduce(m3[:], tile("d", D_S3)[:, 0:T].rearrange("p (j s) -> p j s", j=J), AX_X, ALU.max, negate=True).then_inc(s_m3, 1)
                dve.wait_ge(s_m3, 2 * u + 1)
                dve.tensor_scalar(m3s[:], m3[:], 1.0 / 16, None, ALU.mult).then_inc(s_m3, 1)

            def d_text(u):
                wait_read(dve, "d", u, D_S3)
                dve.reciprocal(rc3[:], sum3[:]).then_inc(s_r3, 1)
                dve.wait_ge(s_r3, 2 * u + 1)
                dve.tensor_scalar(ar3[:], rc3[:], alpha, None, ALU.mult).then_inc(s_r3, 1)
                wait_made(dve, "d", u, D_PT3)
                dve.tensor_copy(p3t.rearrange("p j q -> p (j q)"), tile("d", D_PT3)[:, 0:T]).then_inc(read["d"][D_PT3 % 2], 1)
                dve.wait_ge(s_r3, 2 * u + 2)
                wait_made(dve, "d", u, D_OUT)
                for j in range(J):
                    ins = dve.scalar_tensor_tensor(out=x3[:, j, :], in0=tile("d", D_OUT)[:, j * H:(j + 1) * H], scalar=ar3[:, j:j + 1],
                                                   in1=x3[:, j, :], op0=ALU.mult, op1=ALU.add)
                ins.then_inc(read["d"][D_OUT % 2], 1)

            each_round(dve, dict(a_project=a_project, a_values=a_values, a_stack=a_stack, a_scores=a_scores, a_maxima=a_maxima,
                                 a_turn=a_turn, a_out=a_out, a_norm=a_norm, b_turn=b_turn, b_project=b_project, b_stack=b_stack,
                                 c_scores=c_scores, c_maxima=c_maxima, c_weights=c_weights, c_turn=c_turn, c_out=c_out,
                                 c_norm=c_norm, d_context=d_context, d_scores=d_scores, d_attend=d_attend,
                                 d_text_scores=d_text_scores, d_text=d_text))

        @block.gpsimd
        def _(pool):
            pool.memset(power[:], -0.5).then_inc(s_const, 1)
            pool.wait_ge(s_weights, 16 * WEIGHTS)
            pool.wait_ge(s_const, CONSTANTS)

            def a_residual(u):
                pool.wait_ge(s_xa, 16 * (u + 1))
                before_read(pool, "a", u, A_OUT)
                pool.tensor_tensor(res0[:], x_a[:], bo0[:].unsqueeze(1).broadcast_to([P, J, H]), ALU.add).then_inc(s_res0, 1)

            def b_residual(u):
                before_read(pool, "b", u, B_DOWN)
                pool.tensor_tensor(res_b[:], x_a[:], b_down[:].unsqueeze(1).broadcast_to([P, J, H]), ALU.add).then_inc(s_resb, 1)

            def rest(u, to, full, piece, sem):
                pool.wait_ge(sem, 4 * u + 1)
                pool.tensor_tensor(to, full, piece, ALU.subtract).then_inc(sem, 1)

            def low(u, piece, left, middle, sem):
                pool.wait_ge(sem, 4 * u + 3)
                pool.tensor_tensor(piece, left, middle, ALU.subtract).then_inc(sem, 1)

            def a_project(u):
                rest(u, q0f, q0f, q0p[:, 0], s_q0)
                rest(u, k0f, k0f, k0p[:, 0], s_k0)

            def a_stack(u):
                low(u, q0p[:, 2], q0f, q0p[:, 1], s_q0)
                low(u, k0p[:, 2], k0f, k0p[:, 1], s_k0)

            def a_norm(u):
                pool.wait_ge(s_rms, 5 * u + 3)
                pool.tensor_tensor(rs0[:], ms0[:], power[:], ALU.pow).then_inc(s_rms, 1)

            def b_stack(u):
                before_made(pool, "c", u, C_PV + 1 + C_NEXT)
                rest(u, k1r, kv1f[0:KV1 * D1], k1p[:, 0], s_k1)
                rest(u, q1f, q1f, q1p[:, 0], s_q1)
                low(u, k1p[:, 2], k1r, k1p[:, 1], s_k1)
                low(u, q1p[:, 2], q1f, q1p[:, 1], s_q1)

            def c_residual(u):
                wait_read(pool, "b", u, B_DOWN)
                for j in range(J):
                    before_read(pool, "c", u, C_OUT + j)
                pool.tensor_tensor(res1[:], x1[:], bo1[:].unsqueeze(1).broadcast_to([P, J, H]), ALU.add).then_inc(s_res1, 1)

            def c_norm(u):
                pool.wait_ge(s_ln, 8 * u + 5)
                pool.tensor_tensor(rs1[:], ve1[:], power[:], ALU.pow).then_inc(s_ln, 1)
                pool.wait_ge(s_ln, 8 * u + 8)
                before(pool, s_x2, u)
                pool.tensor_tensor(y1[:], y1[:], gamma[:].unsqueeze(1).broadcast_to([P, J, H]), ALU.mult).then_inc(s_g, 1)
                pool.wait_ge(s_g, u + 1)
                before_made(pool, "d", u, D_Q)
                before_read(pool, "d", u, D_PV)
                pool.tensor_tensor(x2[:], y1[:], beta[:].unsqueeze(1).broadcast_to([P, J, H]), ALU.add).then_inc(s_x2, 1)

            each_round(pool, dict(a_residual=a_residual, b_residual=b_residual, a_project=a_project, a_stack=a_stack, a_norm=a_norm, b_stack=b_stack,
                                  c_residual=c_residual, c_norm=c_norm))


def kernel(**inputs):
    import numpy as np
    import concourse.bacc as bacc
    from concourse.bass_utils import run_bass_kernel_spmd

    a = {name: np.asarray(value) for name, value in inputs.items()}

    def by_partition(m):
        return m.reshape(-1, P, m.shape[1]).transpose(1, 0, 2)

    def channel_major(heads, channels):
        return np.arange(heads * channels).reshape(heads, channels).T.ravel()

    def column(v):
        return v.reshape(-1, P).T

    order0, order1, order_k1 = channel_major(NH0, D0), channel_major(NH1, D1), channel_major(KV1, D1)
    kv_w, kv_b = a["L0_xattn_kv_w"].reshape(H, H, 2), a["L0_xattn_kv_b"].reshape(H, 2)
    pad = lambda v: np.concatenate([v, np.zeros(P - v.shape[0], v.dtype)])[:, None]
    w = {
        "wq0": by_partition(a["L0_xattn_q_w"][:, order0]), "wk0": by_partition(kv_w[:, order0, 0]), "wv0": by_partition(kv_w[:, :, 1]),
        "wo0": by_partition(a["L0_xattn_out_w"]), "w_up": by_partition(a["L0_xattn_mlp_w1"]), "w_down": by_partition(a["L0_xattn_mlp_w2"]),
        "wq1": by_partition(a["L1_xattn_Wq"][:, order1]),
        "wkv1": by_partition(np.concatenate([a["L1_xattn_Wk"][:, order_k1], a["L1_xattn_Wv"]], axis=1)),
        "wo1": by_partition(a["L1_xattn_Wo"]),
        "wq2": a["L2_xattn_Wq"].T, "wk2": a["L2_xattn_Wk"].T, "wv2": a["L2_xattn_Wv"].T,
        "wq3": by_partition(a["L3_xattn_w_q"]), "wk3": by_partition(a["L3_xattn_w_k"]), "wv3": by_partition(a["L3_xattn_w_v"]),
        "wo3": by_partition(a["L3_xattn_w_o"].T),
        "cols": np.concatenate([
            column(a["L0_xattn_q_b"][order0]), column(kv_b[order0, 0]), column(a["L0_xattn_postnorm_w"]), column(a["L0_xattn_mlp_b1"]),
            column(a["L1_xattn_bq"][order1]), column(np.concatenate([a["L1_xattn_bk"][order_k1], a["L1_xattn_bv"]])),
            pad(a["L2_xattn_bq"]), pad(a["L2_xattn_bk"]), np.broadcast_to(a["L3_xattn_alpha"].reshape(1, 1), (P, 1))], axis=1),
        "bv0": kv_b[:, 1], "bo0": a["L0_xattn_out_b"], "b_down": a["L0_xattn_mlp_b2"], "bo1": a["L1_xattn_bo"],
        "gamma": a["L1_xattn_gamma"], "beta": a["L1_xattn_beta"], "bv2": a["L2_xattn_bv"], "ident": np.eye(P, dtype=np.float32),
    }

    def tokens(m):
        return m.reshape(UNITS, J, P, m.shape[2]).transpose(0, 2, 1, 3)

    def features(m):
        return m.reshape(UNITS, J, P, KT, P).transpose(0, 4, 3, 1, 2)

    x, ctx, mask1 = a["x"], a["ctx_2048"], a["mask_Bx1xSxS2_ff0"][:, 0]
    data = {"x": tokens(x), "x_t": features(x), "ctx": tokens(ctx), "ctx_t": features(ctx),
            "mask0": a["mask_BxS2_ik0"].reshape(UNITS, 1, J, P), "mask1": tokens(mask1), "mask1_t": tokens(mask1.transpose(0, 2, 1))}

    nc = bacc.Bacc("TRN2", target_bir_lowering=False, num_devices=1)
    arrays = {name: np.ascontiguousarray(v) for name, v in {**data, **w}.items()}
    aps = {name: nc.dram_tensor("in_" + name, v.shape, mybir.dt.from_np(v.dtype), kind="ExternalInput").ap() for name, v in arrays.items()}
    out = nc.dram_tensor("out", (UNITS, P, J, H), F32, kind="ExternalOutput").ap()
    build(nc, *(aps[name] for name in data), {name: aps[name] for name in w}, out)
    got = run_bass_kernel_spmd(nc, [{"in_" + name: v for name, v in arrays.items()}], core_ids=[0]).results[0]["out"]
    return np.asarray(got).reshape(UNITS, P, J, H).transpose(0, 2, 1, 3).reshape(B, P, H)
```

```python
from contextlib import ExitStack

import concourse.bass as bass
from concourse import mybir

F32 = mybir.dt.float32
BF16 = mybir.dt.bfloat16
I32 = mybir.dt.int32
ALU = mybir.AluOpType
ACT = mybir.ActivationFunctionType
AX_X = mybir.AxisListType.X

P = 128
B = 16
J = 2
UNITS = B // J
T = J * P
H = 256
KT = H // P
NH0, D0 = 16, 16
NH1, KV1, D1 = 32, 8, 8
G1 = NH1 // KV1
FF = 4 * H
MT = FF // P
D2 = 16
S0, S1 = 96, 72
MASK_ROW = S0
R0 = S0 + 1 + 3
R1 = S1 + 3
OUT_W = 32
MASKED = -1.0e30
LOWEST = -3.4028234e38
M0_COLS = 5
EPS = 1.0e-6
WEIGHTS, CONSTANTS = 25, 12

A_Q, A_K, A_S, A_V, A_M, A_ST, A_PV, A_OT, A_FT, A_OUT, A_TILES, A_NEXT = 0, 1, 3, 11, 21, 22, 30, 31, 42, 43, 44, 10
B_KV, B_NT, B_UP, B_DOWN, B_XT, B_Q, B_V, B_TILES = 0, 1, 2, 6, 7, 8, 9, 10
C_S, C_M, C_ST, C_PV, C_TR, C_FT, C_OUT, C_TILES, C_NEXT = 0, 16, 17, 25, 27, 41, 42, 44, 12
D_K, D_V, D_KK, D_VV, D_Q, D_S, D_PT, D_PV, D_XT, D_S3, D_PT3, D_OUT, D_TILES = 0, 1, 2, 3, 4, 5, 7, 9, 10, 11, 12, 13, 14

LOAD, FIRST, SECOND, THIRD = 0, 1, 2, 3
ROUND = [
    (FIRST, "a_residual"), (FIRST, "a_project", 0), (THIRD, "c_scores", 1, 1), (FIRST, "a_project", 1), (SECOND, "b_norm"),
    (THIRD, "c_scores", 1, 2), (FIRST, "a_project", 2), (THIRD, "c_scores", 1, 3), (SECOND, "b_up", 0), (THIRD, "c_split"),
    (SECOND, "b_up", 1), (THIRD, "c_maxima"), (FIRST, "a_stack"), (FIRST, "a_gather"), (SECOND, "b_up", 2), (SECOND, "b_up", 3),
    (THIRD, "c_weights", 0, 0), (SECOND, "b_down", 0), (THIRD, "c_weights", 0, 1), (SECOND, "b_down", 1),
    (THIRD, "c_weights", 0, 2), (SECOND, "b_down", 2), (THIRD, "c_weights", 0, 3), (SECOND, "b_down", 3), (SECOND, "b_add"),
    (THIRD, "c_attend", 0), (SECOND, "b_turn"), (THIRD, "c_turn", 0), (THIRD, "c_weights", 1, 0), (FIRST, "b_residual"),
    (THIRD, "c_weights", 1, 1), (SECOND, "b_project"), (THIRD, "c_weights", 1, 2), (FIRST, "a_scores", 0, 0),
    (THIRD, "c_weights", 1, 3), (FIRST, "a_scores", 0, 1), (THIRD, "c_attend", 1), (SECOND, "b_keep"), (THIRD, "c_turn", 1),
    (FIRST, "b_keys"), (FIRST, "a_scores", 0, 2), (SECOND, "b_stack"), (THIRD, "c_join"), (FIRST, "a_scores", 0, 3),
    (FIRST, "a_values", 0), (THIRD, "c_out", 0), (THIRD, "c_out", 1), (SECOND, "c_residual"), (FIRST, "a_values", 1),
    (FIRST, "a_scores", 1, 0), (THIRD, "c_norm", 0), (SECOND, "b_load"), (FIRST, "a_scores", 1, 1), (THIRD, "c_norm", 1),
    (THIRD, "d_context_values"), (FIRST, "a_scores", 1, 2), (THIRD, "c_norm", 2), (FIRST, "a_scores", 1, 3), (FIRST, "a_split"),
    (THIRD, "d_query"), (FIRST, "a_maxima"), (LOAD, "a_load"), (SECOND, "d_load"), (THIRD, "d_scores", 0), (THIRD, "d_scores", 1),
    (THIRD, "d_scale", 0), (SECOND, "c_scores", 0, 0), (THIRD, "d_turn", 0), (THIRD, "d_scale", 1), (FIRST, "a_weights", 0, 0),
    (SECOND, "c_scores", 0, 1), (THIRD, "d_turn", 1), (FIRST, "a_weights", 0, 1), (SECOND, "c_scores", 0, 2), (THIRD, "d_attend"),
    (FIRST, "a_weights", 0, 2), (FIRST, "a_weights", 0, 3), (SECOND, "c_scores", 0, 3), (THIRD, "d_x"), (FIRST, "a_attend", 0),
    (THIRD, "d_text_scores"), (FIRST, "a_turn", 0), (SECOND, "c_scores", 1, 0), (FIRST, "a_weights", 1, 0),
    (FIRST, "a_weights", 1, 1), (THIRD, "d_text"), (FIRST, "a_weights", 1, 2), (FIRST, "a_weights", 1, 3), (THIRD, "d_output"),
    (FIRST, "a_attend", 1), (SECOND, "d_context"), (FIRST, "a_turn", 1), (SECOND, "d_context_keys"), (FIRST, "a_join"),
    (FIRST, "a_out"), (FIRST, "a_norm"),
]


def build(nc, x, x_t, ctx, ctx_t, mask0, mask1, mask1_t, w, out):
    with ExitStack() as stack:
        def sb(name, shape, dt=F32):
            return stack.enter_context(nc.sbuf_tensor(name, shape, dt))

        def signal(name):
            return stack.enter_context(nc.semaphore(name))

        wq0, wk0, wv0, wo0 = (sb(n, [P, KT, H]) for n in ("wq0", "wk0", "wv0", "wo0"))
        w_up, w_down = sb("w_up", [P, KT, FF]), sb("w_down", [P, MT, H])
        wq1, wkv1, wo1 = sb("wq1", [P, KT, H]), sb("wkv1", [P, KT, P]), sb("wo1", [P, KT, H])
        wq2, wk2, wv2 = sb("wq2", [P, D2]), sb("wk2", [P, D2]), sb("wv2", [P, P])
        cols = sb("cols", [P, 20])
        bq0, bk0, norm_w = cols[:, 0:2], cols[:, 2:4], cols[:, 4:6]
        b_up, bq1_raw, bkv1 = cols[:, 6:14], cols[:, 14:16], cols[:, 16:17]
        bq2, bk2, alpha = cols[0:D2, 17:18], cols[0:D2, 18:19], cols[:, 19:20]
        bv0, bo0, b_down, bo1, gamma, beta = (sb(n, [P, H]) for n in ("bv0", "bo0", "b_down", "bo1", "gamma", "beta"))
        bv2 = sb("bv2", [P, P])
        ident, ident_bf = sb("ident", [P, P]), sb("ident_bf", [P, P], BF16)
        bq1 = sb("bq1", [P, KT])
        power = sb("power", [P, J])
        spare = sb("spare", [P, 1 + C_M])
        key3 = sb("key3", [P, KT, H])
        val3 = sb("val3", [P, KT, H])

        h_t = sb("h_t", [P, KT, J, 2, P])
        x_a = sb("x_a", [P, J, H])
        mask_i, mask_b = sb("mask_i", [1, J, P], I32), sb("mask_b", [1, J, 2, P], BF16)
        q0p, k0p = sb("q0p", [P, 3, KT, T], BF16), sb("k0p", [P, 3, KT, 2 * T], BF16)
        q0s, k0s = sb("q0s", [P, NH0, T], BF16), sb("k0s", [P, NH0, 2 * T], BF16)
        v0 = sb("v0", [P, J, 2, NH0, OUT_W])
        m0, m0r, m0p = sb("m0", [P, J, NH0]), sb("m0r", [P, J, NH0]), sb("m0p", [P, J, M0_COLS, NH0], BF16)
        m0t = sb("m0t", [3 * NH0, T], BF16)
        p0 = sb("p0", [P, 2, NH0, P])
        p0_flat = p0[:].rearrange("p s h q -> p (s h q)")
        q0f = p0_flat[:, 0:KT * T].rearrange("p (t q) -> p t q", t=KT)
        k0f = p0_flat[:, KT * T:3 * KT * T].rearrange("p (t q) -> p t q", t=KT)
        up = p0_flat[:, 2048:2048 + MT * T].rearrange("p (m q) -> p m q", m=MT)
        f0t = p0_flat[:, 1536:2048].rearrange("p (t q) -> p t q", t=KT)
        o0t, rc0, o0 = sb("o0t", [P, 512]), sb("rc0", [P, J, NH0]), sb("o0", [P, J, H])
        res0, y0, y0n = sb("res0", [P, J, H]), sb("y0", [P, J, H]), sb("y0n", [P, J, H])
        ss0, ms0, rs0 = sb("ss0", [P, J]), sb("ms0", [P, J]), sb("rs0", [P, J])
        n_t = sb("n_t", [P, KT, T])
        res_b, x1, x1_t = sb("res_b", [P, J, H]), sb("x1", [P, J, H]), sb("x1_t", [P, KT, T])
        kv1f = sb("kv1f", [P, T])
        q1p, k1p = sb("q1p", [P, 3, KT, T], BF16), sb("k1p", [KV1 * D1, 3, T], BF16)
        q1s, k1s = sb("q1s", [R1, NH1, T], BF16), sb("k1s", [P, KV1, T], BF16)
        v1 = sb("v1", [P, J, KV1, OUT_W])
        m_l, m_s = sb("m_l", [P, J, P]), sb("m_s", [P, J, P])
        res1 = sb("res1", [P, J, H])
        masked = sb("masked", [P, 2, G1, P])
        m1, m1r, m1p = sb("m1", [P, J, NH1]), sb("m1r", [P, J, NH1]), sb("m1p", [P, J, 3, NH1], BF16)
        m1t = sb("m1t", [3 * NH1, T], BF16)
        p1 = sb("p1", [P, NH1, P])
        p1_flat = p1[:].rearrange("p h q -> p (h q)")
        p2 = p1_flat[:, 0:1024].rearrange("p (j t m) -> p j t m", j=J, t=KT)
        p2t = p1_flat[:, 1024:2048].rearrange("p (j m n) -> p j m n", j=J, m=KT)
        p3 = p1_flat[:, 2048:2304].rearrange("p (j s) -> p j s", j=J)
        p3t = p1_flat[:, 2304:2560].rearrange("p (j q) -> p j q", j=J)
        q1f = p1_flat[:, 2560:3072].rearrange("p (t q) -> p t q", t=KT)
        x3_t = p1_flat[:, 3328:3840].rearrange("p (t q) -> p t q", t=KT)
        k1r = p1_flat[0:KV1 * D1, 3072:3328]
        wq3, wk3, wv3, wo3 = (p1_flat[:, n * KT * H:(n + 1) * KT * H].rearrange("p (t h) -> p t h", t=KT) for n in range(4))
        o1t, rc1, o1 = sb("o1t", [P, 2, 512]), sb("rc1", [P, 2, 4, 4]), sb("o1", [P, J, H])
        f1t = sb("f1t", [P, KT, T])
        y1, st1, mv1, ve1, rs1 = sb("y1", [P, J, H]), sb("st1", [P, J, 6]), sb("mv1", [P, J, 2]), sb("ve1", [P, J]), sb("rs1", [P, J])
        x2 = sb("x2", [P, J, H])
        ctx_d, ctx_td = sb("ctx_d", [P, J, H]), sb("ctx_td", [P, KT, T])
        q2, k2, v2 = sb("q2", [D2, J, H]), sb("k2", [D2, J, H]), sb("v2", [P, J, KT, P])
        m2, sum2, rc2 = sb("m2", [P, J, KT]), sb("sum2", [P, J, KT]), sb("rc2", [P, J, KT])
        x3 = sb("x3", [P, J, H])
        kk3, vv3 = sb("kk3", [P, KT, T]), sb("vv3", [P, J, H])
        m3, m3s, sum3, rc3, ar3 = (sb(n, [P, J]) for n in ("m3", "m3s", "sum3", "rc3", "ar3"))

        tiles_of = {"a": A_TILES, "b": B_TILES, "c": C_TILES, "d": D_TILES}
        bank = {s: [stack.enter_context(nc.psum_tensor(f"bank_{s}{n}", [P, 512], F32)) for n in range(2)] for s in "abcd"}
        made = {s: signal(f"{s}_made") for s in "abcd"}
        read = {s: [signal(f"{s}_read{n}") for n in range(2)] for s in "abcd"}

        s_weights, s_const, s_fused, s_fused_read = signal("s_weights"), signal("s_const"), signal("s_fused"), signal("s_fused_read")
        s_ha, s_xa, s_mask_i = signal("s_ha"), signal("s_xa"), signal("s_mask_i")
        s_q0_gather, s_k0_gather, s_q0_stack, s_k0_stack, s_m0_stack = (
            signal(n) for n in ("s_q0_gather", "s_k0_gather", "s_q0_stack", "s_k0_stack", "s_m0_stack"))
        s_masks1, s_q1_gather, s_k1_gather, s_q1_stack, s_k1_stack, s_m1_stack = (
            signal(n) for n in ("s_masks1", "s_q1_gather", "s_k1_gather", "s_q1_stack", "s_k1_stack", "s_m1_stack"))
        s_ctxd, s_out = signal("s_ctxd"), signal("s_out")
        s_mask_b = signal("s_mask_b")
        s_q0, s_k0, s_q1, s_k1 = (signal(n) for n in ("s_q0", "s_k0", "s_q1", "s_k1"))
        s_m0, s_m1 = signal("s_m0"), signal("s_m1")
        s_rc0, s_rc1 = signal("s_rc0"), signal("s_rc1")
        s_res0, s_resb, s_res1 = signal("s_res0"), signal("s_resb"), signal("s_res1")
        s_rms = signal("s_rms")
        s_exp1 = signal("s_exp1")
        s_ln = signal("s_ln")
        s_g, s_x2 = signal("s_g"), signal("s_x2")
        s_m2, s_rc2, s_p2n = signal("s_m2"), signal("s_rc2"), signal("s_p2n")
        s_m3, s_r3 = signal("s_m3"), signal("s_r3")

        def before(eng, sem, value):
            if not isinstance(value, int) or value > 0:
                eng.wait_ge(sem, value)

        def wait_made(eng, s, u, n):
            eng.wait_ge(made[s], u * tiles_of[s] + n + 1)

        def wait_read(eng, s, u, n):
            eng.wait_ge(read[s][n % 2], u * (tiles_of[s] // 2) + n // 2 + 1)

        def wait_bank(pe, s, u, n):
            before(pe, read[s][n % 2], u * (tiles_of[s] // 2) + n // 2)

        def before_made(eng, s, u, n):
            before(eng, made[s], (u - 1) * tiles_of[s] + n + 1)

        def before_read(eng, s, u, n):
            before(eng, read[s][n % 2], (u - 1) * (tiles_of[s] // 2) + n // 2 + 1)

        def tile(s, n):
            return bank[s][n % 2]

        def each_round(eng, steps):
            def one(i):
                for lag, name, *args in ROUND:
                    if name in steps and not (isinstance(i, int) and not 0 <= i - lag < UNITS):
                        steps[name](i - lag, *args)
            for i in range(THIRD + 1):
                one(i)
            with eng.Fori(THIRD + 1, UNITS) as i:
                one(i)
            for i in range(UNITS, UNITS + THIRD):
                one(i)

        block = stack.enter_context(nc.Block())

        @block.sync
        def _(sp):
            pairs = [(wq0, "wq0"), (wk0, "wk0"), (wv0, "wv0"), (cols, "cols"), (bv0, "bv0"), (ident, "ident"), (wo0, "wo0"),
                     (bo0, "bo0"), (w_up, "w_up"), (w_down, "w_down"), (b_down, "b_down"), (wq1, "wq1"), (wkv1, "wkv1"),
                     (wo1, "wo1"), (bo1, "bo1"), (gamma, "gamma"), (beta, "beta"), (wq2, "wq2"), (wk2, "wk2"), (wv2, "wv2"),
                     (bv2, "bv2"), (wq3, "wq3"), (wk3, "wk3"), (wv3, "wv3"), (wo3, "wo3")]
            for dst, name in pairs:
                src = w[name]
                if len(src.shape) == 1:
                    src = src.rearrange("(o f) -> o f", o=1).broadcast_to([P, src.shape[0]])
                sp.dma_start(dst if dst.shape[0] == P and name.endswith('3') else dst[:], src).then_inc(s_weights, 16)
            sp.wait_ge(s_weights, 16 * WEIGHTS)
            sp.wait_ge(s_const, CONSTANTS)

            def a_load(u):
                before_made(sp, "b", u, B_KV)
                before_made(sp, "a", u, A_V + 1)
                sp.dma_start(h_t[:, :, :, 0, :], ctx_t[u]).then_inc(s_ha, 16)
                sp.dma_start(h_t[:, :, :, 1, :], x_t[u]).then_inc(s_ha, 16)
                before(sp, s_resb, u)
                sp.dma_start(x_a[:], x[u]).then_inc(s_xa, 16)
                before(sp, s_mask_b, u)
                sp.dma_start(mask_i[:], mask0[u]).then_inc(s_mask_i, 16)

            def a_gather(u):
                before_made(sp, "a", u, A_ST + 7 + A_NEXT)
                sp.wait_ge(s_q0, 4 * u + 4)
                for p, block_at in ((0, 0), (1, 3), (2, 5)):
                    for t in range(KT):
                        r = D0 * block_at + 8 * t
                        sp.dma_start(q0s[r:r + 8], q0p[:, p, t, :]).then_inc(s_q0_gather, 16)
                sp.wait_ge(s_k0, 4 * u + 4)
                for p in range(3):
                    for t in range(KT):
                        r = D0 * p + 8 * t
                        sp.dma_start(k0s[r:r + 8], k0p[:, p, t, :]).then_inc(s_k0_gather, 16)
                sp.wait_ge(s_mask_b, u + 1)
                sp.dma_start(k0s[MASK_ROW:MASK_ROW + 1],
                             mask_b[:].rearrange("o j s p -> o (j s p)").unsqueeze(1).broadcast_to([1, NH0, 2 * T])).then_inc(s_k0_stack, 16)
                sp.wait_ge(s_q0_gather, 16 * (6 * u + 6))
                for of, to in ((0, 1), (0, 2), (3, 4)):
                    sp.dma_start(q0s[D0 * to:D0 * to + D0], q0s[D0 * of:D0 * of + D0]).then_inc(s_q0_stack, 16)
                sp.wait_ge(s_k0_gather, 16 * (6 * u + 6))
                sp.dma_start(k0s[3 * D0:5 * D0], k0s[0:2 * D0]).then_inc(s_k0_stack, 16)
                sp.dma_start(k0s[5 * D0:6 * D0], k0s[0:D0]).then_inc(s_k0_stack, 16)

            def a_maxima(u):
                wait_read(sp, "a", u, A_M)
                sp.dma_start(q0s[MASK_ROW + 1:R0], m0t[:]).then_inc(s_m0_stack, 16)

            def b_load(u):
                before_made(sp, "c", u, C_PV + 1 + C_NEXT)
                sp.dma_start(m_l[:], mask1[u]).then_inc(s_masks1, 16)
                sp.dma_start(m_s[:], mask1_t[u]).then_inc(s_masks1, 16)

            def b_stack(u):
                before_made(sp, "c", u, C_ST + 7 + C_NEXT)
                sp.wait_ge(s_k1, 4 * u + 4)
                for p in range(3):
                    sp.dma_start(k1s[D1 * p:D1 * p + D1], k1p[:, p, :]).then_inc(s_k1_gather, 16)
                sp.wait_ge(s_q1, 4 * u + 4)
                for p in range(3):
                    for t in range(KT):
                        r = D1 * p + 4 * t
                        sp.dma_start(q1s[r:r + 4], q1p[:, p, t, :]).then_inc(s_q1_gather, 16)
                sp.wait_ge(s_k1_gather, 16 * (3 * u + 3))
                for of, to, n in ((1, 3, 2), (0, 5, 1), (2, 6, 1), (0, 7, 2)):
                    sp.dma_start(k1s[D1 * to:D1 * (to + n)], k1s[D1 * of:D1 * (of + n)]).then_inc(s_k1_stack, 16)
                sp.wait_ge(s_q1_gather, 16 * (6 * u + 6))
                for to in (3, 6):
                    sp.dma_start(q1s[D1 * to:D1 * (to + 3)], q1s[0:3 * D1]).then_inc(s_q1_stack, 16)

            def c_maxima(u):
                wait_read(sp, "c", u, C_M)
                sp.dma_start(q1s[S1:R1], m1t[:]).then_inc(s_m1_stack, 16)

            def d_load(u):
                before_made(sp, "d", u, D_VV)
                sp.dma_start(ctx_d[:], ctx[u]).then_inc(s_ctxd, 16)
                sp.dma_start(ctx_td[:], ctx_t[u]).then_inc(s_ctxd, 16)

            def d_output(u):
                wait_read(sp, "d", u, D_OUT)
                sp.dma_start(out[u], x3[:]).then_inc(s_out, 16)

            each_round(sp, dict(a_load=a_load, a_gather=a_gather, a_maxima=a_maxima, b_load=b_load, b_stack=b_stack,
                                c_maxima=c_maxima, d_load=d_load, d_output=d_output))
            sp.wait_ge(s_out, 16 * UNITS)

        @block.tensor
        def _(pe):
            def dense(dst, lhs, rhs):
                for t in range(KT):
                    mm = pe.matmul(dst, lhs(t), rhs(t), start=(t == 0), stop=(t == KT - 1))
                return mm

            pe.wait_ge(s_weights, 16 * WEIGHTS)
            for n, (left, right) in enumerate(((wk3, wq3), (wv3, wo3))):
                for m in range(KT):
                    mm = dense(bank["d"][n][:, m * H:(m + 1) * H], lambda t: left[:, t, m * P:(m + 1) * P], lambda t: right[:, t, :])
                mm.then_inc(s_fused, 1)
            pe.wait_ge(s_const, CONSTANTS)
            pe.wait_ge(s_fused_read, 2)

            def a_project(u, n):
                k = A_Q + n
                if n == 0:
                    pe.wait_ge(s_ha, 16 * (2 * u + 2))
                wait_bank(pe, "a", u, k)
                if n == 0:
                    for m in range(KT):
                        mm = dense(tile("a", k)[:, m * T:(m + 1) * T].rearrange("p (j q) -> p j q", j=J), lambda t: wq0[:, t, m * P:(m + 1) * P],
                                   lambda t: h_t[:, t, :, 1, :])
                else:
                    m = k - A_K
                    mm = dense(tile("a", k)[:, :], lambda t: wk0[:, t, m * P:(m + 1) * P], lambda t: h_t[:, t].rearrange("p j s q -> p (j s q)"))
                mm.then_inc(made["a"], 1)

            def a_values(u, j):
                wait_bank(pe, "a", u, A_V + j)
                for s in range(2):
                    mm = dense(tile("a", A_V + j)[:, s * H:(s + 1) * H], lambda t: h_t[:, t, j, s, :], lambda t: wv0[:, t, :])
                mm.then_inc(made["a"], 1)

            def b_keys(u):
                wait_bank(pe, "b", u, B_KV)
                dense(tile("b", B_KV)[:, 0:T].rearrange("p (j q) -> p j q", j=J), lambda t: wkv1[:, t, :], lambda t: h_t[:, t, :, 0, :]).then_inc(made["b"], 1)

            def a_scores(u, j, pair):
                if (j, pair) == (0, 0):
                    pe.wait_ge(s_q0_stack, 16 * (3 * u + 3))
                    pe.wait_ge(s_q0_gather, 16 * (6 * u + 6))
                    pe.wait_ge(s_k0_stack, 16 * (3 * u + 3))
                    pe.wait_ge(s_k0_gather, 16 * (6 * u + 6))
                for n in (2 * pair, 2 * pair + 1):
                    k = A_S + A_NEXT * j + n
                    wait_bank(pe, "a", u, k)
                    for h in (2 * n, 2 * n + 1):
                        mm = pe.matmul(tile("a", k)[:, (h % 2) * 2 * P:(h % 2 + 1) * 2 * P], q0s[0:S0 + 1, h, j * P:(j + 1) * P],
                                       k0s[0:S0 + 1, h, j * 2 * P:(j + 1) * 2 * P], start=True, stop=True)
                    mm.then_inc(made["a"], 1)

            def a_maxima(u):
                pe.wait_ge(s_m0, 4 * u + 4)
                wait_bank(pe, "a", u, A_M)
                for j in range(J):
                    mm = pe.transpose(tile("a", A_M).bitcast(BF16)[0:M0_COLS * NH0, j * P:(j + 1) * P], m0p[:, j].rearrange("p c h -> p (c h)"), ident_bf[:])
                mm.then_inc(made["a"], 1)

            def a_weights(u, j, pair):
                if (j, pair) == (0, 0):
                    pe.wait_ge(s_m0_stack, 16 * (u + 1))
                s = pair // 2
                for g in (pair % 2 * 2, pair % 2 * 2 + 1):
                    k = A_ST + A_NEXT * j + 4 * s + g
                    wait_bank(pe, "a", u, k)
                    for h in range(4 * g, 4 * g + 4):
                        mm = pe.matmul(tile("a", k)[:, (h % 4) * P:(h % 4 + 1) * P], k0s[0:R0, h, (2 * j + s) * P:(2 * j + s + 1) * P],
                                       q0s[0:R0, h, j * P:(j + 1) * P], start=True, stop=True)
                    mm.then_inc(made["a"], 1)

            def a_attend(u, j):
                wait_read(pe, "a", u, A_ST + A_NEXT * j + 7)
                wait_bank(pe, "a", u, A_PV + A_NEXT * j)
                for g in range(4):
                    for s in range(2):
                        for c in range(4):
                            mm = pe.matmul(tile("a", A_PV + A_NEXT * j)[32 * c:32 * c + 32, g * P:(g + 1) * P], v0[:, j, s, 4 * g + c, :],
                                           p0[:, s, 4 * g + c, :], start=(s == 0), stop=(s == 1), tile_position=(0, 32 * c))
                mm.then_inc(made["a"], 1)

            def a_turn(u, j):
                wait_read(pe, "a", u, A_PV + A_NEXT * j)
                wait_bank(pe, "a", u, A_OT + A_NEXT * j)
                for g in range(4):
                    mm = pe.transpose(tile("a", A_OT + A_NEXT * j)[:, g * P:(g + 1) * P], o0t[:, g * P:(g + 1) * P], ident[:])
                mm.then_inc(made["a"], 1)

            def a_join(u):
                wait_bank(pe, "a", u, A_FT)
                wait_read(pe, "a", u, A_OT + A_NEXT)
                for j in range(J):
                    for t in range(KT):
                        mm = pe.transpose(tile("a", A_FT)[:, t * T + j * P:t * T + (j + 1) * P], o0[:, j, t * P:(t + 1) * P], ident[:])
                mm.then_inc(made["a"], 1)

            def a_out(u):
                wait_read(pe, "a", u, A_FT)
                wait_bank(pe, "a", u, A_OUT)
                for j in range(J):
                    mm = dense(tile("a", A_OUT)[:, j * H:(j + 1) * H], lambda t: f0t[:, t, j * P:(j + 1) * P], lambda t: wo0[:, t, :])
                mm.then_inc(made["a"], 1)

            def b_norm(u):
                pe.wait_ge(s_rms, 5 * u + 5)
                wait_bank(pe, "b", u, B_NT)
                for j in range(J):
                    for t in range(KT):
                        mm = pe.transpose(tile("b", B_NT)[:, t * T + j * P:t * T + (j + 1) * P], y0n[:, j, t * P:(t + 1) * P], ident[:])
                mm.then_inc(made["b"], 1)

            def b_up(u, n):
                if n == 0:
                    wait_read(pe, "b", u, B_NT)
                wait_bank(pe, "b", u, B_UP + n)
                for m in (2 * n, 2 * n + 1):
                    mm = dense(tile("b", B_UP + n)[:, (m % 2) * T:(m % 2 + 1) * T], lambda t: w_up[:, t, m * P:(m + 1) * P], lambda t: n_t[:, t, :])
                mm.then_inc(made["b"], 1)

            def b_down_(u, n):
                j, half = n // 2, n % 2
                if n == 0:
                    wait_read(pe, "b", u, B_UP + 3)
                    wait_bank(pe, "b", u, B_DOWN)
                for m in range(half * MT // 2, (half + 1) * MT // 2):
                    mm = pe.matmul(tile("b", B_DOWN)[:, j * H:(j + 1) * H], up[:, m, j * P:(j + 1) * P], w_down[:, m, :], start=(m == 0), stop=(m == MT - 1))
                if n == 3:
                    mm.then_inc(made["b"], 1)

            def b_turn(u):
                wait_read(pe, "b", u, B_DOWN)
                wait_bank(pe, "b", u, B_XT)
                for j in range(J):
                    for t in range(KT):
                        mm = pe.transpose(tile("b", B_XT)[:, t * T + j * P:t * T + (j + 1) * P], x1[:, j, t * P:(t + 1) * P], ident[:])
                mm.then_inc(made["b"], 1)

            def b_project(u):
                wait_read(pe, "b", u, B_XT)
                wait_bank(pe, "b", u, B_Q)
                for m in range(KT):
                    mm = dense(tile("b", B_Q)[:, m * T:(m + 1) * T], lambda t: wq1[:, t, m * P:(m + 1) * P], lambda t: x1_t[:, t, :])
                mm.then_inc(made["b"], 1)

            def b_keep(u):
                wait_read(pe, "b", u, B_KV)
                wait_bank(pe, "b", u, B_V)
                for j in range(J):
                    mm = pe.transpose(tile("b", B_V)[:, j * P:(j + 1) * P], kv1f[:, j * P:(j + 1) * P], ident[:])
                mm.then_inc(made["b"], 1)

            def c_scores(u, j, pair):
                if (j, pair) == (0, 0):
                    pe.wait_ge(s_q1_stack, 16 * (2 * u + 2))
                    pe.wait_ge(s_q1_gather, 16 * (6 * u + 6))
                    pe.wait_ge(s_k1_stack, 16 * (4 * u + 4))
                    pe.wait_ge(s_k1_gather, 16 * (3 * u + 3))
                for kv in (2 * pair, 2 * pair + 1):
                    k = C_S + 8 * j + kv
                    wait_bank(pe, "c", u, k)
                    for g in range(G1):
                        mm = pe.matmul(tile("c", k)[:, g * P:(g + 1) * P], q1s[0:S1, kv * G1 + g, j * P:(j + 1) * P],
                                       k1s[0:S1, kv, j * P:(j + 1) * P], start=True, stop=True)
                    mm.then_inc(made["c"], 1)

            def c_maxima(u):
                pe.wait_ge(s_m1, 5 * u + 5)
                wait_bank(pe, "c", u, C_M)
                for j in range(J):
                    mm = pe.transpose(tile("c", C_M).bitcast(BF16)[0:3 * NH1, j * P:(j + 1) * P], m1p[:, j].rearrange("p c h -> p (c h)"), ident_bf[:])
                mm.then_inc(made["c"], 1)

            def c_weights(u, j, pair):
                if (j, pair) == (0, 0):
                    pe.wait_ge(s_m1_stack, 16 * (u + 1))
                for kv in (2 * pair, 2 * pair + 1):
                    k = C_ST + C_NEXT * j + kv
                    wait_bank(pe, "c", u, k)
                    pe.matmul(tile("c", k)[:, :].rearrange("p (g q) -> p g q", g=G1), k1s[0:R1, kv, j * P:(j + 1) * P],
                              q1s[0:R1, kv * G1:(kv + 1) * G1, j * P:(j + 1) * P], start=True, stop=True).then_inc(made["c"], 1)

            def c_attend(u, j):
                if j == 0:
                    wait_read(pe, "b", u, B_V)
                pe.wait_ge(s_exp1, 16 * u + 8 * j + 8)
                for half in range(2):
                    k = C_PV + C_NEXT * j + half
                    wait_bank(pe, "c", u, k)
                    for c in range(4):
                        kv = 4 * half + c
                        mm = pe.matmul(tile("c", k)[32 * c:32 * c + 32, :], v1[:, j, kv, :],
                                       p1[:, kv * G1:(kv + 1) * G1, :].rearrange("p g q -> p (g q)"), start=True, stop=True, tile_position=(0, 32 * c))
                    mm.then_inc(made["c"], 1)

            def c_turn(u, j):
                for half in range(2):
                    k = C_TR + C_NEXT * j + half
                    wait_read(pe, "c", u, k - 2)
                    wait_bank(pe, "c", u, k)
                    for g in range(G1):
                        mm = pe.transpose(tile("c", k)[:, g * P:(g + 1) * P], o1t[:, half, g * P:(g + 1) * P], ident[:])
                    mm.then_inc(made["c"], 1)

            def c_join(u):
                wait_bank(pe, "c", u, C_FT)
                wait_read(pe, "c", u, C_TR + C_NEXT + 1)
                for j in range(J):
                    for t in range(KT):
                        mm = pe.transpose(tile("c", C_FT)[:, t * T + j * P:t * T + (j + 1) * P], o1[:, j, t * P:(t + 1) * P], ident[:])
                mm.then_inc(made["c"], 1)

            def c_out(u, j):
                if j == 0:
                    wait_read(pe, "c", u, C_FT)
                wait_bank(pe, "c", u, C_OUT + j)
                dense(tile("c", C_OUT + j)[:, 0:H], lambda t: f1t[:, t, j * P:(j + 1) * P], lambda t: wo1[:, t, :]).then_inc(made["c"], 1)

            def d_context(u):
                pe.wait_ge(s_ctxd, 16 * (2 * u + 2))
                wait_bank(pe, "d", u, D_K)
                pe.matmul(tile("d", D_K)[0:D2, :], wk2[:], ctx_d[:].rearrange("p j n -> p (j n)"), start=True, stop=True).then_inc(made["d"], 1)
                wait_bank(pe, "d", u, D_V)
                for j in range(J):
                    for t in range(KT):
                        mm = pe.matmul(tile("d", D_V)[:, (KT * j + t) * P:(KT * j + t + 1) * P], ctx_d[:, j, t * P:(t + 1) * P], wv2[:], start=True, stop=True)
                mm.then_inc(made["d"], 1)

            def d_context_keys(u):
                wait_bank(pe, "d", u, D_KK)
                for m in range(KT):
                    mm = dense(tile("d", D_KK)[:, m * T:(m + 1) * T], lambda t: key3[:, t, m * P:(m + 1) * P], lambda t: ctx_td[:, t, :])
                mm.then_inc(made["d"], 1)

            def d_context_values(u):
                wait_bank(pe, "d", u, D_VV)
                for j in range(J):
                    mm = dense(tile("d", D_VV)[:, j * H:(j + 1) * H], lambda t: ctx_td[:, t, j * P:(j + 1) * P], lambda t: val3[:, t, :])
                mm.then_inc(made["d"], 1)

            def d_query(u):
                pe.wait_ge(s_x2, u + 1)
                wait_bank(pe, "d", u, D_Q)
                pe.matmul(tile("d", D_Q)[0:D2, :], wq2[:], x2[:].rearrange("p j n -> p (j n)"), start=True, stop=True).then_inc(made["d"], 1)

            def d_scores(u, j):
                wait_read(pe, "d", u, D_Q)
                wait_bank(pe, "d", u, D_S + j)
                for t in range(KT):
                    mm = pe.matmul(tile("d", D_S + j)[:, t * H:(t + 1) * H], q2[:, j, t * P:(t + 1) * P], k2[:, j, :], start=True, stop=True)
                mm.then_inc(made["d"], 1)

            def d_turn(u, j):
                pe.wait_ge(s_p2n, 2 * u + j + 1)
                wait_bank(pe, "d", u, D_PT + j)
                for m in range(KT):
                    for t in range(KT):
                        mm = pe.transpose(tile("d", D_PT + j)[:, m * H + t * P:m * H + (t + 1) * P], p2[:, j, t, m * P:(m + 1) * P], ident[:])
                mm.then_inc(made["d"], 1)

            def d_attend(u):
                wait_bank(pe, "d", u, D_PV)
                for j in range(J):
                    wait_read(pe, "d", u, D_PT + j)
                    for m in range(KT):
                        mm = pe.matmul(tile("d", D_PV)[:, j * H:(j + 1) * H], v2[:, j, m, :], p2t[:, j, m, :], start=(m == 0), stop=(m == KT - 1))
                mm.then_inc(made["d"], 1)

            def d_x(u):
                wait_read(pe, "d", u, D_PV)
                wait_bank(pe, "d", u, D_XT)
                for j in range(J):
                    for t in range(KT):
                        mm = pe.transpose(tile("d", D_XT)[:, t * T + j * P:t * T + (j + 1) * P], x3[:, j, t * P:(t + 1) * P], ident[:])
                mm.then_inc(made["d"], 1)

            def d_text_scores(u):
                wait_read(pe, "d", u, D_XT)
                wait_bank(pe, "d", u, D_S3)
                for j in range(J):
                    mm = dense(tile("d", D_S3)[:, j * P:(j + 1) * P], lambda t: x3_t[:, t, j * P:(j + 1) * P], lambda t: kk3[:, t, j * P:(j + 1) * P])
                mm.then_inc(made["d"], 1)

            def d_text(u):
                wait_read(pe, "d", u, D_S3)
                wait_bank(pe, "d", u, D_PT3)
                for j in range(J):
                    mm = pe.transpose(tile("d", D_PT3)[:, j * P:(j + 1) * P], p3[:, j, :], ident[:])
                mm.then_inc(made["d"], 1)

            def d_output(u):
                wait_read(pe, "d", u, D_PT3)
                wait_bank(pe, "d", u, D_OUT)
                for j in range(J):
                    mm = pe.matmul(tile("d", D_OUT)[:, j * H:(j + 1) * H], p3t[:, j, :], vv3[:, j, :], start=True, stop=True)
                mm.then_inc(made["d"], 1)

            each_round(pe, dict(a_project=a_project, a_values=a_values, a_scores=a_scores, a_maxima=a_maxima, a_weights=a_weights,
                                a_attend=a_attend, a_turn=a_turn, a_join=a_join, a_out=a_out, b_keys=b_keys, b_norm=b_norm, b_up=b_up,
                                b_down=b_down_, b_turn=b_turn, b_project=b_project, b_keep=b_keep, c_scores=c_scores, c_maxima=c_maxima,
                                c_weights=c_weights, c_attend=c_attend, c_turn=c_turn, c_join=c_join, c_out=c_out,
                                d_context=d_context, d_context_keys=d_context_keys, d_context_values=d_context_values,
                                d_query=d_query, d_scores=d_scores, d_turn=d_turn, d_attend=d_attend, d_x=d_x,
                                d_text_scores=d_text_scores, d_text=d_text, d_output=d_output))

        @block.scalar
        def _(act):
            act.wait_ge(s_weights, 16 * WEIGHTS)
            act.activation(bq1[:], bq1_raw, ACT.Copy, scale=float(D1) ** -0.5).then_inc(s_const, 1)
            act.activation(ident_bf[:], ident[:], ACT.Copy).then_inc(s_const, 1)
            for n, dst in enumerate((key3, val3)):
                act.wait_ge(s_fused, n + 1)
                act.activation(dst[:].rearrange("p t h -> p (t h)"), bank["d"][n][:, :], ACT.Copy).then_inc(s_fused_read, 1)
            act.wait_ge(s_const, CONSTANTS)

            def a_project(u, n):
                k = A_Q + n
                wait_made(act, "a", u, k)
                if n == 0:
                    for m in range(KT):
                        ins = act.activation(q0f[:, m, :], tile("a", k)[:, m * T:(m + 1) * T], ACT.Identity, bias=bq0[:, m:m + 1])
                else:
                    m = k - A_K
                    ins = act.activation(k0f[:, m, :], tile("a", k)[:, :], ACT.Identity, bias=bk0[:, m:m + 1])
                ins.then_inc(read["a"][k % 2], 1)

            def b_keys(u):
                before(act, s_k1, 4 * u)
                before_made(act, "b", u, B_V)
                wait_made(act, "b", u, B_KV)
                act.activation(kv1f[:], tile("b", B_KV)[:, 0:T], ACT.Identity, bias=bkv1).then_inc(read["b"][B_KV % 2], 1)

            def a_weights(u, j, pair):
                if (j, pair) == (0, 0):
                    before_made(act, "b", u, B_DOWN)
                s = pair // 2
                for g in (pair % 2 * 2, pair % 2 * 2 + 1):
                    k = A_ST + A_NEXT * j + 4 * s + g
                    wait_made(act, "a", u, k)
                    act.activation(p0[:, s, 4 * g:4 * g + 4, :].rearrange("p h q -> p (h q)"), tile("a", k)[:, :], ACT.Exp,
                                   scale=1.0 / D0).then_inc(read["a"][k % 2], 1)

            def a_attend(u, j):
                wait_made(act, "a", u, A_PV + A_NEXT * j)
                act.activation(o0t[:], tile("a", A_PV + A_NEXT * j)[:, :], ACT.Copy).then_inc(read["a"][(A_PV + A_NEXT * j) % 2], 1)

            def a_join(u):
                wait_made(act, "a", u, A_FT)
                act.activation(f0t.rearrange("p t q -> p (t q)"), tile("a", A_FT)[:, :], ACT.Copy).then_inc(read["a"][A_FT % 2], 1)

            def a_out(u):
                before(act, s_rms, 5 * u)
                before_made(act, "b", u, B_NT)
                wait_read(act, "a", u, A_OUT)
                for j in range(J):
                    act.activation(y0n[:, j, :], y0[:, j, :], ACT.Square, accum_out=ss0[:, j:j + 1]).then_inc(s_rms, 1)

            def b_norm(u):
                before_made(act, "b", u, B_UP + 3)
                wait_made(act, "b", u, B_NT)
                for t in range(KT):
                    ins = act.activation(n_t[:, t, :], tile("b", B_NT)[:, t * T:(t + 1) * T], ACT.Copy, scale=norm_w[:, t:t + 1])
                ins.then_inc(read["b"][B_NT % 2], 1)

            def b_up_(u, n):
                if n == 0:
                    wait_made(act, "a", u, A_PV + A_NEXT)
                wait_made(act, "b", u, B_UP + n)
                for m in (2 * n, 2 * n + 1):
                    ins = act.activation(up[:, m, :], tile("b", B_UP + n)[:, (m % 2) * T:(m % 2 + 1) * T], ACT.Gelu_apprx_tanh, bias=b_up[:, m:m + 1])
                ins.then_inc(read["b"][(B_UP + n) % 2], 1)

            def b_turn(u):
                wait_made(act, "b", u, B_XT)
                act.activation(x1_t[:].rearrange("p t q -> p (t q)"), tile("b", B_XT)[:, :], ACT.Copy).then_inc(read["b"][B_XT % 2], 1)

            def b_keep(u):
                before_made(act, "c", u, C_PV + 1 + C_NEXT)
                wait_made(act, "b", u, B_Q)
                for m in range(KT):
                    ins = act.activation(q1f[:, m, :], tile("b", B_Q)[:, m * T:(m + 1) * T], ACT.Identity, bias=bq1[:, m:m + 1], scale=float(D1) ** -0.5)
                ins.then_inc(read["b"][B_Q % 2], 1)

            def c_weights(u, j, pair):
                for kv in (2 * pair, 2 * pair + 1):
                    wait_read(act, "c", u, C_ST + C_NEXT * j + kv)
                    rows = p1[:, kv * G1:(kv + 1) * G1, :]
                    act.activation(rows, rows, ACT.Exp).then_inc(s_exp1, 1)

            def c_attend(u, j):
                for half in range(2):
                    k = C_PV + C_NEXT * j + half
                    wait_made(act, "c", u, k)
                    act.activation(o1t[:, half, :], tile("c", k)[:, :], ACT.Copy).then_inc(read["c"][k % 2], 1)

            def c_join(u):
                wait_made(act, "c", u, C_FT)
                act.activation(f1t[:].rearrange("p t q -> p (t q)"), tile("c", C_FT)[:, :], ACT.Copy).then_inc(read["c"][C_FT % 2], 1)

            def d_context(u):
                wait_made(act, "d", u, D_K)
                act.activation(k2[:].rearrange("p j n -> p (j n)"), tile("d", D_K)[0:D2, :], ACT.Identity, bias=bk2).then_inc(read["d"][D_K % 2], 1)

            def d_context_keys(u):
                wait_made(act, "d", u, D_KK)
                act.activation(kk3[:].rearrange("p t s -> p (t s)"), tile("d", D_KK)[:, :], ACT.Copy).then_inc(read["d"][D_KK % 2], 1)

            def d_context_values(u):
                wait_made(act, "d", u, D_VV)
                act.activation(vv3[:].rearrange("p j o -> p (j o)"), tile("d", D_VV)[:, :], ACT.Copy).then_inc(read["d"][D_VV % 2], 1)

            def d_query(u):
                wait_made(act, "d", u, D_Q)
                act.activation(q2[:].rearrange("p j n -> p (j n)"), tile("d", D_Q)[0:D2, :], ACT.Identity, bias=bq2).then_inc(read["d"][D_Q % 2], 1)

            def d_scores(u, j):
                before(act, s_p2n, 2 * (u - 1) + j + 1)
                act.wait_ge(s_m2, 2 * u + j + 1)
                for t in range(KT):
                    ins = act.activation(p2[:, j, t, :], tile("d", D_S + j)[:, t * H:(t + 1) * H], ACT.Exp, bias=m2[:, j, t:t + 1],
                                         accum_out=sum2[:, j, t:t + 1])
                ins.then_inc(read["d"][(D_S + j) % 2], 1)

            def d_turn(u, j):
                wait_made(act, "d", u, D_PT + j)
                act.activation(p2t[:, j].rearrange("p m n -> p (m n)"), tile("d", D_PT + j)[:, :], ACT.Copy).then_inc(read["d"][(D_PT + j) % 2], 1)

            def d_x(u):
                wait_made(act, "d", u, D_XT)
                act.activation(x3_t.rearrange("p t q -> p (t q)"), tile("d", D_XT)[:, :], ACT.Copy).then_inc(read["d"][D_XT % 2], 1)

            def d_text_scores(u):
                act.wait_ge(s_m3, 2 * u + 2)
                for j in range(J):
                    ins = act.activation(p3[:, j, :], tile("d", D_S3)[:, j * P:(j + 1) * P], ACT.Exp, bias=m3s[:, j:j + 1], scale=1.0 / 16,
                                         accum_out=sum3[:, j:j + 1])
                ins.then_inc(read["d"][D_S3 % 2], 1)

            each_round(act, dict(a_project=a_project, a_weights=a_weights, a_attend=a_attend, a_join=a_join, a_out=a_out, b_keys=b_keys,
                                 b_norm=b_norm, b_up=b_up_, b_turn=b_turn, b_keep=b_keep, c_weights=c_weights,
                                 c_attend=c_attend, c_join=c_join, d_context=d_context, d_context_keys=d_context_keys,
                                 d_context_values=d_context_values, d_query=d_query, d_scores=d_scores, d_turn=d_turn, d_x=d_x,
                                 d_text_scores=d_text_scores))

        @block.vector
        def _(dve):
            dve.memset(q0s[MASK_ROW:P], 1.0).then_inc(s_const, 1)
            dve.memset(k0s[MASK_ROW:P], 1.0).then_inc(s_const, 1)
            dve.memset(mask_b[:, :, 1, :], 0.0).then_inc(s_const, 1)
            dve.memset(k1s[64:P], 1.0).then_inc(s_const, 1)
            dve.memset(m0p[:, :, 3:M0_COLS, :], 0.0).then_inc(s_const, 1)
            dve.memset(v0[:, :, :, :, D0:D0 + 1], 1.0).then_inc(s_const, 1)
            dve.memset(v0[:, :, :, :, D0 + 1:OUT_W], 0.0).then_inc(s_const, 1)
            dve.memset(v1[:, :, :, D1:D1 + 1], 1.0).then_inc(s_const, 1)
            dve.memset(v1[:, :, :, D1 + 1:OUT_W], 0.0).then_inc(s_const, 1)
            dve.wait_ge(s_weights, 16 * WEIGHTS)
            dve.wait_ge(s_const, CONSTANTS)

            def high(u, full, pieces, sem, gathered, dmas):
                before(dve, gathered, 16 * dmas * u)
                dve.tensor_copy(pieces, full).then_inc(sem, 1)

            def middle(u, rest, pieces, sem):
                dve.wait_ge(sem, 4 * u + 2)
                dve.tensor_copy(pieces, rest).then_inc(sem, 1)

            def split_maxima(steps, m, rest, pieces, sem):
                dve.tensor_copy(pieces[:, :, 0, :], m).then_inc(sem, 1)
                dve.wait_ge(sem, steps + 1)
                dve.tensor_tensor(rest, m, pieces[:, :, 0, :], ALU.subtract).then_inc(sem, 1)
                dve.wait_ge(sem, steps + 2)
                dve.tensor_copy(pieces[:, :, 1, :], rest).then_inc(sem, 1)
                dve.wait_ge(sem, steps + 3)
                dve.tensor_tensor(pieces[:, :, 2, :], rest, pieces[:, :, 1, :], ALU.subtract).then_inc(sem, 1)

            def a_project(u, n):
                if n == 0:
                    before(dve, s_k0_stack, 16 * 3 * u)
                    dve.wait_ge(s_mask_i, 16 * (u + 1))
                    dve.tensor_scalar(mask_b[:, :, 0, :], mask_i[:], 0.0, MASKED, ALU.is_equal, ALU.mult).then_inc(s_mask_b, 1)
                    wait_read(dve, "a", u, A_Q)
                    high(u, q0f, q0p[:, 0], s_q0, s_q0_gather, 6)
                elif n == KT:
                    for m in range(KT):
                        wait_read(dve, "a", u, A_K + m)
                    high(u, k0f, k0p[:, 0], s_k0, s_k0_gather, 6)

            def a_values(u, j):
                wait_made(dve, "a", u, A_V + j)
                dve.tensor_tensor(v0[:, j, :, :, 0:D0], tile("a", A_V + j)[:, :].rearrange("p (s h d) -> p s h d", s=2, h=NH0),
                                  bv0[:].rearrange("p (o h d) -> p o h d", o=1, h=NH0).broadcast_to([P, 2, NH0, D0]),
                                  ALU.add).then_inc(read["a"][(A_V + j) % 2], 1)

            def a_stack(u):
                middle(u, q0f, q0p[:, 1], s_q0)
                middle(u, k0f, k0p[:, 1], s_k0)

            def a_scores(u, j, pair):
                if (j, pair) == (0, 0):
                    before(dve, s_m0, 4 * u)
                for n in (2 * pair, 2 * pair + 1):
                    k = A_S + A_NEXT * j + n
                    wait_made(dve, "a", u, k)
                    dve.tensor_reduce(m0[:, j, 2 * n:2 * n + 2], tile("a", k)[:, :].rearrange("p (h n) -> p h n", h=2), AX_X, ALU.max,
                                      negate=True).then_inc(read["a"][k % 2], 1)

            def a_split(u):
                for n in (6, 7):
                    wait_read(dve, "a", u, A_S + A_NEXT + n)
                split_maxima(4 * u, m0[:], m0r[:], m0p, s_m0)

            def a_maxima(u):
                before(dve, s_m0_stack, 16 * u)
                wait_made(dve, "a", u, A_M)
                dve.tensor_copy(m0t[:], tile("a", A_M).bitcast(BF16)[0:3 * NH0, 0:T]).then_inc(read["a"][A_M % 2], 1)

            def a_turn(u, j):
                heads = tile("a", A_OT + A_NEXT * j)[:, :].rearrange("p (h e) -> p h e", h=NH0)
                wait_made(dve, "a", u, A_OT + A_NEXT * j)
                dve.reciprocal(rc0[:, j, :].unsqueeze(2), heads[:, :, D0:D0 + 1]).then_inc(s_rc0, 1)
                dve.wait_ge(s_rc0, 2 * u + j + 1)
                dve.tensor_tensor(o0[:, j, :].rearrange("p (h d) -> p h d", h=NH0), heads[:, :, 0:D0],
                                  rc0[:, j, :].unsqueeze(2).broadcast_to([P, NH0, D0]), ALU.mult).then_inc(read["a"][(A_OT + A_NEXT * j) % 2], 1)

            def a_out(u):
                dve.wait_ge(s_res0, u + 1)
                wait_made(dve, "a", u, A_OUT)
                dve.tensor_tensor(y0[:], tile("a", A_OUT)[:, :].rearrange("p (j h) -> p j h", j=J), res0[:], ALU.add).then_inc(read["a"][A_OUT % 2], 1)

            def a_norm(u):
                dve.wait_ge(s_rms, 5 * u + 2)
                dve.tensor_scalar(ms0[:], ss0[:], 1.0 / H, EPS, ALU.mult, ALU.add).then_inc(s_rms, 1)
                dve.wait_ge(s_rms, 5 * u + 4)
                for j in range(J):
                    ins = dve.tensor_scalar(y0n[:, j, :], y0[:, j, :], rs0[:, j:j + 1], None, ALU.mult)
                ins.then_inc(s_rms, 1)

            def b_add(u):
                dve.wait_ge(s_resb, u + 1)
                before(dve, s_res1, u)
                wait_made(dve, "b", u, B_DOWN)
                dve.tensor_tensor(x1[:], tile("b", B_DOWN)[:, :].rearrange("p (j h) -> p j h", j=J), res_b[:], ALU.add).then_inc(read["b"][B_DOWN % 2], 1)

            def b_keep(u):
                wait_read(dve, "b", u, B_Q)
                high(u, q1f, q1p[:, 0], s_q1, s_q1_gather, 6)
                wait_read(dve, "b", u, B_KV)
                high(u, kv1f[0:KV1 * D1], k1p[:, 0], s_k1, s_k1_gather, 3)
                before_made(dve, "c", u, C_PV + 1 + C_NEXT)
                wait_made(dve, "b", u, B_V)
                dve.tensor_copy(v1[:, :, :, 0:D1], tile("b", B_V)[:, 0:T].rearrange("p (j c) -> p j c", j=J)[:, :, KV1 * D1:]
                                .rearrange("p j (k d) -> p j k d", d=D1)).then_inc(read["b"][B_V % 2], 1)

            def b_stack(u):
                middle(u, k1r, k1p[:, 1], s_k1)
                middle(u, q1f, q1p[:, 1], s_q1)

            def c_scores(u, j, pair):
                if (j, pair) == (0, 0):
                    dve.wait_ge(s_masks1, 16 * (2 * u + 2))
                    before(dve, s_m1, 5 * u)
                for n in (2 * pair, 2 * pair + 1):
                    k = C_S + 8 * j + n
                    wait_made(dve, "c", u, k)
                    dve.memset(spare[:, k + 1:k + 2], 0.0)
                    for g in range(G1):
                        ins = dve.tensor_tensor_reduce(masked[:, k % 2, g, :], tile("c", k)[:, g * P:(g + 1) * P], m_l[:, j, :], 1.0, LOWEST,
                                                       ALU.add, ALU.max, m1[:, j, n * G1 + g:n * G1 + g + 1])
                    ins.then_inc(read["c"][k % 2], 1)

            def c_split(u):
                for n in (14, 15):
                    wait_read(dve, "c", u, C_S + n)
                dve.tensor_scalar(m1[:], m1[:], -1.0, None, ALU.mult).then_inc(s_m1, 1)
                dve.wait_ge(s_m1, 5 * u + 1)
                split_maxima(5 * u + 1, m1[:], m1r[:], m1p, s_m1)

            def c_maxima(u):
                before(dve, s_m1_stack, 16 * u)
                wait_made(dve, "c", u, C_M)
                dve.tensor_copy(m1t[:], tile("c", C_M).bitcast(BF16)[0:3 * NH1, 0:T]).then_inc(read["c"][C_M % 2], 1)

            def c_weights(u, j, pair):
                if (j, pair) == (0, 0):
                    before_made(dve, "d", u, D_OUT)
                    dve.wait_ge(s_q1, 4 * u + 4)
                    dve.wait_ge(s_k1, 4 * u + 4)
                for kv in (2 * pair, 2 * pair + 1):
                    k = C_ST + C_NEXT * j + kv
                    wait_made(dve, "c", u, k)
                    dve.tensor_tensor(p1[:, kv * G1:(kv + 1) * G1, :], tile("c", k)[:, :].rearrange("p (g s) -> p g s", g=G1),
                                      m_s[:, j:j + 1, :].broadcast_to([P, G1, P]), ALU.add).then_inc(read["c"][k % 2], 1)

            def c_turn(u, j):
                for half in range(2):
                    k = C_TR + C_NEXT * j + half
                    heads = tile("c", k)[:, :].rearrange("p (g k e) -> p g k e", g=G1, k=4)
                    wait_made(dve, "c", u, k)
                    dve.reciprocal(rc1[:, half].unsqueeze(3), heads[:, :, :, D1:D1 + 1]).then_inc(s_rc1, 1)
                    dve.wait_ge(s_rc1, 4 * u + 2 * j + half + 1)
                    dve.tensor_tensor(o1[:, j, half * P:(half + 1) * P].rearrange("p (k g d) -> p g k d", k=4, g=G1), heads[:, :, :, 0:D1],
                                      rc1[:, half].unsqueeze(3).broadcast_to([P, G1, 4, D1]), ALU.mult).then_inc(read["c"][k % 2], 1)

            def c_out(u, j):
                if j == 0:
                    dve.wait_ge(s_res1, u + 1)
                    before(dve, s_x2, u)
                wait_made(dve, "c", u, C_OUT + j)
                dve.tensor_tensor(y1[:, j, :], tile("c", C_OUT + j)[:, 0:H], res1[:, j, :], ALU.add).then_inc(read["c"][(C_OUT + j) % 2], 1)

            def c_norm(u, part):
                if part == 0:
                    for j in range(J):
                        wait_read(dve, "c", u, C_OUT + j)
                        dve.bn_stats(st1[:, j, :], y1[:, j, :]).then_inc(s_ln, 1)
                elif part == 1:
                    dve.wait_ge(s_ln, 8 * u + 2)
                    dve.memset(spare[:, 0:1], 0.0)
                    for j in range(J):
                        dve.bn_aggr(mv1[:, j, :], st1[:, j, :]).then_inc(s_ln, 1)
                    dve.wait_ge(s_ln, 8 * u + 4)
                    dve.tensor_scalar(ve1[:], mv1[:, :, 1], EPS, None, ALU.add).then_inc(s_ln, 1)
                else:
                    dve.wait_ge(s_ln, 8 * u + 6)
                    for j in range(J):
                        dve.tensor_scalar(y1[:, j, :], y1[:, j, :], mv1[:, j, 0:1], rs1[:, j:j + 1], ALU.subtract, ALU.mult).then_inc(s_ln, 1)

            def d_context(u):
                wait_made(dve, "d", u, D_V)
                dve.tensor_tensor(v2[:].rearrange("p j t c -> p (j t) c"), tile("d", D_V)[:, :].rearrange("p (j c) -> p j c", j=J * KT),
                                  bv2[:].unsqueeze(1).broadcast_to([P, J * KT, P]), ALU.add).then_inc(read["d"][D_V % 2], 1)

            def d_scores(u, j):
                wait_made(dve, "d", u, D_S + j)
                dve.tensor_reduce(m2[:, j, :], tile("d", D_S + j)[:, :].rearrange("p (t m) -> p t m", t=KT), AX_X, ALU.max,
                                  negate=True).then_inc(s_m2, 1)

            def d_scale(u, j):
                wait_read(dve, "d", u, D_S + j)
                dve.reciprocal(rc2[:, j, :], sum2[:, j, :]).then_inc(s_rc2, 1)
                dve.wait_ge(s_rc2, 2 * u + j + 1)
                for t in range(KT):
                    ins = dve.tensor_scalar(p2[:, j, t, :], p2[:, j, t, :], rc2[:, j, t:t + 1], None, ALU.mult)
                ins.then_inc(s_p2n, 1)

            def d_attend(u):
                before(dve, s_out, 16 * u)
                wait_made(dve, "d", u, D_PV)
                dve.tensor_tensor(x3[:], tile("d", D_PV)[:, :].rearrange("p (j n) -> p j n", j=J), x2[:], ALU.add).then_inc(read["d"][D_PV % 2], 1)

            def d_text_scores(u):
                wait_made(dve, "d", u, D_S3)
                dve.tensor_reduce(m3[:], tile("d", D_S3)[:, 0:T].rearrange("p (j s) -> p j s", j=J), AX_X, ALU.max, negate=True).then_inc(s_m3, 1)
                dve.wait_ge(s_m3, 2 * u + 1)
                dve.tensor_scalar(m3s[:], m3[:], 1.0 / 16, None, ALU.mult).then_inc(s_m3, 1)

            def d_text(u):
                wait_read(dve, "d", u, D_S3)
                dve.reciprocal(rc3[:], sum3[:]).then_inc(s_r3, 1)
                dve.wait_ge(s_r3, 2 * u + 1)
                dve.tensor_scalar(ar3[:], rc3[:], alpha, None, ALU.mult).then_inc(s_r3, 1)
                wait_made(dve, "d", u, D_PT3)
                dve.tensor_copy(p3t.rearrange("p j q -> p (j q)"), tile("d", D_PT3)[:, 0:T]).then_inc(read["d"][D_PT3 % 2], 1)

            def d_output(u):
                dve.wait_ge(s_r3, 2 * u + 2)
                wait_made(dve, "d", u, D_OUT)
                for j in range(J):
                    ins = dve.scalar_tensor_tensor(out=x3[:, j, :], in0=tile("d", D_OUT)[:, j * H:(j + 1) * H], scalar=ar3[:, j:j + 1],
                                                   in1=x3[:, j, :], op0=ALU.mult, op1=ALU.add)
                ins.then_inc(read["d"][D_OUT % 2], 1)

            each_round(dve, dict(a_project=a_project, a_values=a_values, a_stack=a_stack, a_scores=a_scores, a_split=a_split,
                                 a_maxima=a_maxima, a_turn=a_turn, a_out=a_out, a_norm=a_norm, b_add=b_add, b_keep=b_keep,
                                 b_stack=b_stack, c_scores=c_scores, c_split=c_split, c_maxima=c_maxima, c_weights=c_weights,
                                 c_turn=c_turn, c_out=c_out, c_norm=c_norm, d_context=d_context, d_scores=d_scores, d_scale=d_scale,
                                 d_attend=d_attend, d_text_scores=d_text_scores, d_text=d_text, d_output=d_output))

        @block.gpsimd
        def _(pool):
            pool.memset(power[:], -0.5).then_inc(s_const, 1)
            pool.wait_ge(s_weights, 16 * WEIGHTS)
            pool.wait_ge(s_const, CONSTANTS)

            def a_residual(u):
                pool.wait_ge(s_xa, 16 * (u + 1))
                before_read(pool, "a", u, A_OUT)
                pool.tensor_tensor(res0[:], x_a[:], bo0[:].unsqueeze(1).broadcast_to([P, J, H]), ALU.add).then_inc(s_res0, 1)

            def b_residual(u):
                before_read(pool, "b", u, B_DOWN)
                pool.tensor_tensor(res_b[:], x_a[:], b_down[:].unsqueeze(1).broadcast_to([P, J, H]), ALU.add).then_inc(s_resb, 1)

            def rest(u, to, full, piece, sem):
                pool.wait_ge(sem, 4 * u + 1)
                pool.tensor_tensor(to, full, piece, ALU.subtract).then_inc(sem, 1)

            def low(u, piece, left, middle, sem):
                pool.wait_ge(sem, 4 * u + 3)
                pool.tensor_tensor(piece, left, middle, ALU.subtract).then_inc(sem, 1)

            def a_project(u, n):
                if n == 0:
                    rest(u, q0f, q0f, q0p[:, 0], s_q0)
                elif n == KT:
                    rest(u, k0f, k0f, k0p[:, 0], s_k0)

            def a_stack(u):
                low(u, q0p[:, 2], q0f, q0p[:, 1], s_q0)
                low(u, k0p[:, 2], k0f, k0p[:, 1], s_k0)

            def a_norm(u):
                pool.wait_ge(s_rms, 5 * u + 3)
                pool.tensor_tensor(rs0[:], ms0[:], power[:], ALU.pow).then_inc(s_rms, 1)

            def b_stack(u):
                before_made(pool, "c", u, C_PV + 1 + C_NEXT)
                rest(u, k1r, kv1f[0:KV1 * D1], k1p[:, 0], s_k1)
                rest(u, q1f, q1f, q1p[:, 0], s_q1)
                low(u, k1p[:, 2], k1r, k1p[:, 1], s_k1)
                low(u, q1p[:, 2], q1f, q1p[:, 1], s_q1)

            def c_residual(u):
                wait_read(pool, "b", u, B_DOWN)
                for j in range(J):
                    before_read(pool, "c", u, C_OUT + j)
                pool.tensor_tensor(res1[:], x1[:], bo1[:].unsqueeze(1).broadcast_to([P, J, H]), ALU.add).then_inc(s_res1, 1)

            def c_norm(u, part):
                if part != 2:
                    return
                pool.wait_ge(s_ln, 8 * u + 5)
                pool.tensor_tensor(rs1[:], ve1[:], power[:], ALU.pow).then_inc(s_ln, 1)
                pool.wait_ge(s_ln, 8 * u + 8)
                before(pool, s_x2, u)
                pool.tensor_tensor(y1[:], y1[:], gamma[:].unsqueeze(1).broadcast_to([P, J, H]), ALU.mult).then_inc(s_g, 1)
                pool.wait_ge(s_g, u + 1)
                before_made(pool, "d", u, D_Q)
                before_read(pool, "d", u, D_PV)
                pool.tensor_tensor(x2[:], y1[:], beta[:].unsqueeze(1).broadcast_to([P, J, H]), ALU.add).then_inc(s_x2, 1)

            each_round(pool, dict(a_residual=a_residual, b_residual=b_residual, a_project=a_project, a_stack=a_stack, a_norm=a_norm, b_stack=b_stack,
                                  c_residual=c_residual, c_norm=c_norm))


def kernel(**inputs):
    import numpy as np
    import concourse.bacc as bacc
    from concourse.bass_utils import run_bass_kernel_spmd

    a = {name: np.asarray(value) for name, value in inputs.items()}

    def by_partition(m):
        return m.reshape(-1, P, m.shape[1]).transpose(1, 0, 2)

    def channel_major(heads, channels):
        return np.arange(heads * channels).reshape(heads, channels).T.ravel()

    def column(v):
        return v.reshape(-1, P).T

    order0, order1, order_k1 = channel_major(NH0, D0), channel_major(NH1, D1), channel_major(KV1, D1)
    kv_w, kv_b = a["L0_xattn_kv_w"].reshape(H, H, 2), a["L0_xattn_kv_b"].reshape(H, 2)
    pad = lambda v: np.concatenate([v, np.zeros(P - v.shape[0], v.dtype)])[:, None]
    w = {
        "wq0": by_partition(a["L0_xattn_q_w"][:, order0]), "wk0": by_partition(kv_w[:, order0, 0]), "wv0": by_partition(kv_w[:, :, 1]),
        "wo0": by_partition(a["L0_xattn_out_w"]), "w_up": by_partition(a["L0_xattn_mlp_w1"]), "w_down": by_partition(a["L0_xattn_mlp_w2"]),
        "wq1": by_partition(a["L1_xattn_Wq"][:, order1]),
        "wkv1": by_partition(np.concatenate([a["L1_xattn_Wk"][:, order_k1], a["L1_xattn_Wv"]], axis=1)),
        "wo1": by_partition(a["L1_xattn_Wo"]),
        "wq2": a["L2_xattn_Wq"].T, "wk2": a["L2_xattn_Wk"].T, "wv2": a["L2_xattn_Wv"].T,
        "wq3": by_partition(a["L3_xattn_w_q"]), "wk3": by_partition(a["L3_xattn_w_k"]), "wv3": by_partition(a["L3_xattn_w_v"]),
        "wo3": by_partition(a["L3_xattn_w_o"].T),
        "cols": np.concatenate([
            column(a["L0_xattn_q_b"][order0]), column(kv_b[order0, 0]), column(a["L0_xattn_postnorm_w"]), column(a["L0_xattn_mlp_b1"]),
            column(a["L1_xattn_bq"][order1]), column(np.concatenate([a["L1_xattn_bk"][order_k1], a["L1_xattn_bv"]])),
            pad(a["L2_xattn_bq"]), pad(a["L2_xattn_bk"]), np.broadcast_to(a["L3_xattn_alpha"].reshape(1, 1), (P, 1))], axis=1),
        "bv0": kv_b[:, 1], "bo0": a["L0_xattn_out_b"], "b_down": a["L0_xattn_mlp_b2"], "bo1": a["L1_xattn_bo"],
        "gamma": a["L1_xattn_gamma"], "beta": a["L1_xattn_beta"], "bv2": a["L2_xattn_bv"], "ident": np.eye(P, dtype=np.float32),
    }

    def tokens(m):
        return m.reshape(UNITS, J, P, m.shape[2]).transpose(0, 2, 1, 3)

    def features(m):
        return m.reshape(UNITS, J, P, KT, P).transpose(0, 4, 3, 1, 2)

    x, ctx, mask1 = a["x"], a["ctx_2048"], a["mask_Bx1xSxS2_ff0"][:, 0]
    data = {"x": tokens(x), "x_t": features(x), "ctx": tokens(ctx), "ctx_t": features(ctx),
            "mask0": a["mask_BxS2_ik0"].reshape(UNITS, 1, J, P), "mask1": tokens(mask1), "mask1_t": tokens(mask1.transpose(0, 2, 1))}

    nc = bacc.Bacc("TRN2", target_bir_lowering=False, num_devices=1)
    arrays = {name: np.ascontiguousarray(v) for name, v in {**data, **w}.items()}
    aps = {name: nc.dram_tensor("in_" + name, v.shape, mybir.dt.from_np(v.dtype), kind="ExternalInput").ap() for name, v in arrays.items()}
    out = nc.dram_tensor("out", (UNITS, P, J, H), F32, kind="ExternalOutput").ap()
    build(nc, *(aps[name] for name in data), {name: aps[name] for name in w}, out)
    got = run_bass_kernel_spmd(nc, [{"in_" + name: v for name, v in arrays.items()}], core_ids=[0]).results[0]["out"]
    return np.asarray(got).reshape(UNITS, P, J, H).transpose(0, 2, 1, 3).reshape(B, P, H)
```

```python
from contextlib import ExitStack

import concourse.bass as bass
from concourse import mybir

F32 = mybir.dt.float32
BF16 = mybir.dt.bfloat16
I32 = mybir.dt.int32
ALU = mybir.AluOpType
ACT = mybir.ActivationFunctionType
AX_X = mybir.AxisListType.X

P = 128
B = 16
J = 2
UNITS = B // J
T = J * P
H = 256
KT = H // P
NH0, D0 = 16, 16
NH1, KV1, D1 = 32, 8, 8
G1 = NH1 // KV1
FF = 4 * H
MT = FF // P
D2 = 16
S0, S1 = 96, 72
MASK_ROW = S0
R0 = S0 + 1 + 3
R1 = S1 + 3
OUT_W = 32
MASKED = -1.0e30
LOWEST = -3.4028234e38
M0_COLS = 5
EPS = 1.0e-6
WEIGHTS0, WEIGHTS, CONSTANTS = 7, 18, 11

A_Q, A_K, A_V, A_S, A_M, A_ST, A_PV, A_OT, A_FT, A_OUT, A_TILES, A_NEXT = 0, 1, 3, 5, 21, 22, 30, 31, 42, 43, 44, 10
B_KV, B_NT, B_UP, B_DOWN, B_XT, B_Q, B_V, B_TILES = 0, 1, 2, 6, 7, 8, 9, 10
C_S, C_M, C_ST, C_PV, C_TR, C_FT, C_OUT, C_TILES, C_NEXT = 0, 16, 17, 25, 27, 41, 42, 44, 12
D_K, D_V, D_KK, D_VV, D_Q, D_S, D_PT, D_PV, D_XT, D_S3, D_PT3, D_OUT, D_TILES = 0, 1, 2, 3, 4, 5, 7, 9, 10, 11, 12, 13, 14

LOAD, FIRST, SECOND, THIRD = 0, 1, 2, 3
ROUND = [
    (FIRST, "a_residual"), (FIRST, "a_project", 0), (THIRD, "c_scores", 1, 2), (FIRST, "a_project", 1), (SECOND, "b_norm"),
    (THIRD, "c_scores", 1, 3), (FIRST, "a_project", 2), (SECOND, "b_up", 0), (THIRD, "c_split"), (SECOND, "b_up", 1),
    (THIRD, "c_maxima"), (FIRST, "a_stack"), (FIRST, "start"), (FIRST, "a_gather"), (SECOND, "b_up", 2), (SECOND, "b_up", 3),
    (FIRST, "a_values", 0), (THIRD, "c_weights", 0, 0), (SECOND, "b_down", 0), (THIRD, "c_weights", 0, 1), (SECOND, "b_down", 1),
    (THIRD, "c_weights", 0, 2), (SECOND, "b_down", 2), (THIRD, "c_weights", 0, 3), (SECOND, "b_down", 3), (SECOND, "b_add"),
    (THIRD, "c_attend", 0), (SECOND, "b_turn"), (THIRD, "c_turn", 0), (THIRD, "c_weights", 1, 0), (FIRST, "b_residual"),
    (FIRST, "a_values", 1), (THIRD, "c_weights", 1, 1), (SECOND, "b_project"), (THIRD, "c_weights", 1, 2),
    (THIRD, "c_weights", 1, 3), (FIRST, "a_scores", 0, 0), (THIRD, "d_context_values"), (THIRD, "c_attend", 1),
    (FIRST, "a_scores", 0, 1), (THIRD, "c_turn", 1), (SECOND, "b_keep"), (FIRST, "a_scores", 0, 2), (THIRD, "c_join"),
    (SECOND, "b_stack"), (FIRST, "a_scores", 0, 3), (THIRD, "c_out", 0), (THIRD, "c_out", 1), (SECOND, "c_residual"),
    (THIRD, "c_norm", 0), (THIRD, "c_norm", 1), (SECOND, "b_load"), (FIRST, "a_scores", 1, 0), (FIRST, "b_keys"),
    (THIRD, "c_norm", 2), (FIRST, "a_scores", 1, 1), (FIRST, "a_scores", 1, 2), (THIRD, "d_query"), (FIRST, "a_scores", 1, 3),
    (FIRST, "a_split"), (THIRD, "d_scores", 0), (FIRST, "a_maxima"), (THIRD, "d_scores", 1), (LOAD, "a_load"), (SECOND, "d_load"),
    (THIRD, "d_scale", 0), (SECOND, "c_scores", 0, 0), (THIRD, "d_turn", 0), (THIRD, "d_scale", 1), (FIRST, "a_weights", 0, 0),
    (SECOND, "c_scores", 0, 1), (THIRD, "d_turn", 1), (FIRST, "a_weights", 0, 1), (SECOND, "c_scores", 0, 2), (THIRD, "d_attend"),
    (FIRST, "a_weights", 0, 2), (FIRST, "a_weights", 0, 3), (THIRD, "d_x"), (SECOND, "c_scores", 0, 3), (FIRST, "a_attend", 0),
    (THIRD, "d_text_scores"), (FIRST, "a_turn", 0), (SECOND, "c_scores", 1, 0), (FIRST, "a_weights", 1, 0), (THIRD, "d_text"),
    (FIRST, "a_weights", 1, 1), (FIRST, "a_weights", 1, 2), (THIRD, "d_output"), (FIRST, "a_weights", 1, 3),
    (SECOND, "d_context", 0), (SECOND, "d_context", 1), (FIRST, "a_attend", 1), (SECOND, "c_scores", 1, 1), (FIRST, "a_turn", 1),
    (SECOND, "d_context_keys"), (FIRST, "a_join"), (FIRST, "a_out"), (FIRST, "a_norm"),
]


def build(nc, x, x_t, ctx, ctx_t, mask0, mask1, mask1_t, w, out):
    with ExitStack() as stack:
        def sb(name, shape, dt=F32):
            return stack.enter_context(nc.sbuf_tensor(name, shape, dt))

        def signal(name):
            return stack.enter_context(nc.semaphore(name))

        wq0, wk0, wv0, wo0 = (sb(n, [P, KT, H]) for n in ("wq0", "wk0", "wv0", "wo0"))
        w_up, w_down = sb("w_up", [P, KT, FF]), sb("w_down", [P, MT, H])
        wq1, wkv1, wo1 = sb("wq1", [P, KT, H]), sb("wkv1", [P, KT, P]), sb("wo1", [P, KT, H])
        wq2, wk2, wv2 = sb("wq2", [P, D2]), sb("wk2", [P, D2]), sb("wv2", [P, P])
        cols = sb("cols", [P, 20])
        bq0, bk0, norm_w = cols[:, 0:2], cols[:, 2:4], cols[:, 4:6]
        b_up, bq1_raw, bkv1 = cols[:, 6:14], cols[:, 14:16], cols[:, 16:17]
        bq2, bk2, alpha = cols[0:D2, 17:18], cols[0:D2, 18:19], cols[:, 19:20]
        bv0, bo0, b_down, bo1, gamma, beta = (sb(n, [P, H]) for n in ("bv0", "bo0", "b_down", "bo1", "gamma", "beta"))
        bv2 = sb("bv2", [P, P])
        ident, ident_bf = sb("ident", [P, P]), sb("ident_bf", [P, P], BF16)
        bq1 = sb("bq1", [P, KT])
        power = sb("power", [P, J])
        spare = sb("spare", [P, 1 + C_M])
        key3 = sb("key3", [P, KT, H])
        val3 = sb("val3", [P, KT, H])

        h_t = sb("h_t", [P, KT, J, 2, P])
        x_a = sb("x_a", [P, J, H])
        mask_i, mask_b = sb("mask_i", [1, J, P], I32), sb("mask_b", [1, J, 2, P], BF16)
        q0p, k0p = sb("q0p", [P, 3, KT, T], BF16), sb("k0p", [P, 3, KT, 2 * T], BF16)
        q0s, k0s = sb("q0s", [P, NH0, T], BF16), sb("k0s", [P, NH0, 2 * T], BF16)
        v0 = sb("v0", [P, J, 2, NH0, OUT_W])
        m0, m0r, m0p = sb("m0", [P, J, NH0]), sb("m0r", [P, J, NH0]), sb("m0p", [P, J, M0_COLS, NH0], BF16)
        m0t = sb("m0t", [3 * NH0, T], BF16)
        p0 = sb("p0", [P, 2, NH0, P])
        p0_flat = p0[:].rearrange("p s h q -> p (s h q)")
        q0f = p0_flat[:, 0:KT * T].rearrange("p (t q) -> p t q", t=KT)
        k0f = p0_flat[:, KT * T:3 * KT * T].rearrange("p (t q) -> p t q", t=KT)
        up = p0_flat[:, 2048:2048 + MT * T].rearrange("p (m q) -> p m q", m=MT)
        f0t = p0_flat[:, 1536:2048].rearrange("p (t q) -> p t q", t=KT)
        o0t, rc0, o0 = sb("o0t", [P, 512]), sb("rc0", [P, J, NH0]), sb("o0", [P, J, H])
        res0, y0, y0n = sb("res0", [P, J, H]), sb("y0", [P, J, H]), sb("y0n", [P, J, H])
        ss0, ms0, rs0 = sb("ss0", [P, J]), sb("ms0", [P, J]), sb("rs0", [P, J])
        n_t = sb("n_t", [P, KT, T])
        res_b, x1, x1_t = sb("res_b", [P, J, H]), sb("x1", [P, J, H]), sb("x1_t", [P, KT, T])
        kv1f = sb("kv1f", [P, T])
        q1p, k1p = sb("q1p", [P, 3, KT, T], BF16), sb("k1p", [KV1 * D1, 3, T], BF16)
        q1s, k1s = sb("q1s", [R1, NH1, T], BF16), sb("k1s", [P, KV1, T], BF16)
        v1 = sb("v1", [P, J, KV1, OUT_W])
        m_l, m_s = sb("m_l", [P, J, P]), sb("m_s", [P, J, P])
        res1 = sb("res1", [P, J, H])
        masked = sb("masked", [P, 2, G1, P])
        m1, m1r, m1p = sb("m1", [P, J, NH1]), sb("m1r", [P, J, NH1]), sb("m1p", [P, J, 3, NH1], BF16)
        m1t = sb("m1t", [3 * NH1, T], BF16)
        p1 = sb("p1", [P, NH1, P])
        p1_flat = p1[:].rearrange("p h q -> p (h q)")
        p2 = p1_flat[:, 0:1024].rearrange("p (j t m) -> p j t m", j=J, t=KT)
        p2t = p1_flat[:, 1024:2048].rearrange("p (j m n) -> p j m n", j=J, m=KT)
        p3 = p1_flat[:, 2048:2304].rearrange("p (j s) -> p j s", j=J)
        p3t = p1_flat[:, 2304:2560].rearrange("p (j q) -> p j q", j=J)
        q1f = p1_flat[:, 2560:3072].rearrange("p (t q) -> p t q", t=KT)
        x3_t = p1_flat[:, 3328:3840].rearrange("p (t q) -> p t q", t=KT)
        k1r = p1_flat[0:KV1 * D1, 3072:3328]
        wq3, wk3, wv3, wo3 = (p1_flat[:, n * KT * H:(n + 1) * KT * H].rearrange("p (t h) -> p t h", t=KT) for n in range(4))
        o1t, rc1, o1 = sb("o1t", [P, 2, 512]), sb("rc1", [P, 2, 4, 4]), sb("o1", [P, J, H])
        f1t = sb("f1t", [P, KT, T])
        y1, st1, mv1, ve1, rs1 = sb("y1", [P, J, H]), sb("st1", [P, J, 6]), sb("mv1", [P, J, 2]), sb("ve1", [P, J]), sb("rs1", [P, J])
        x2 = sb("x2", [P, J, H])
        ctx_d, ctx_td = sb("ctx_d", [P, J, H]), sb("ctx_td", [P, KT, T])
        q2, k2, v2 = sb("q2", [D2, J, H]), sb("k2", [D2, J, H]), sb("v2", [P, J, KT, P])
        m2, sum2, rc2 = sb("m2", [P, J, KT]), sb("sum2", [P, J, KT]), sb("rc2", [P, J, KT])
        x3 = sb("x3", [P, J, H])
        kk3, vv3 = sb("kk3", [P, KT, T]), sb("vv3", [P, J, H])
        m3, m3s, sum3, rc3, ar3 = (sb(n, [P, J]) for n in ("m3", "m3s", "sum3", "rc3", "ar3"))

        tiles_of = {"a": A_TILES, "b": B_TILES, "c": C_TILES, "d": D_TILES}
        bank = {s: [stack.enter_context(nc.psum_tensor(f"bank_{s}{n}", [P, 512], F32)) for n in range(2)] for s in "abcd"}
        made = {s: signal(f"{s}_made") for s in "abcd"}
        read = {s: [signal(f"{s}_read{n}") for n in range(2)] for s in "abcd"}

        s_weights0, s_weights, s_const, s_fused, s_fused_read = signal("s_weights0"), signal("s_weights"), signal("s_const"), signal("s_fused"), signal("s_fused_read")
        s_ha, s_xa, s_mask_i = signal("s_ha"), signal("s_xa"), signal("s_mask_i")
        s_q0_gather, s_k0_gather, s_q0_stack, s_k0_stack, s_m0_stack = (
            signal(n) for n in ("s_q0_gather", "s_k0_gather", "s_q0_stack", "s_k0_stack", "s_m0_stack"))
        s_masks1, s_q1_gather, s_k1_gather, s_q1_stack, s_k1_stack, s_m1_stack = (
            signal(n) for n in ("s_masks1", "s_q1_gather", "s_k1_gather", "s_q1_stack", "s_k1_stack", "s_m1_stack"))
        s_ones = signal("s_ones")
        s_ctxd, s_out = signal("s_ctxd"), signal("s_out")
        s_mask_b = signal("s_mask_b")
        s_q0, s_k0, s_q1, s_k1 = (signal(n) for n in ("s_q0", "s_k0", "s_q1", "s_k1"))
        s_m0, s_m1 = signal("s_m0"), signal("s_m1")
        s_rc0, s_rc1 = signal("s_rc0"), signal("s_rc1")
        s_res0, s_resb, s_res1 = signal("s_res0"), signal("s_resb"), signal("s_res1")
        s_rms = signal("s_rms")
        s_exp1 = signal("s_exp1")
        s_ln = signal("s_ln")
        s_x2 = signal("s_x2")
        s_m2, s_rc2, s_p2n = signal("s_m2"), signal("s_rc2"), signal("s_p2n")
        s_m3, s_r3 = signal("s_m3"), signal("s_r3")

        def before(eng, sem, value):
            if not isinstance(value, int) or value > 0:
                eng.wait_ge(sem, value)

        def wait_made(eng, s, u, n):
            eng.wait_ge(made[s], u * tiles_of[s] + n + 1)

        def wait_read(eng, s, u, n):
            eng.wait_ge(read[s][n % 2], u * (tiles_of[s] // 2) + n // 2 + 1)

        def wait_bank(pe, s, u, n):
            before(pe, read[s][n % 2], u * (tiles_of[s] // 2) + n // 2)

        def before_made(eng, s, u, n):
            before(eng, made[s], (u - 1) * tiles_of[s] + n + 1)

        def before_read(eng, s, u, n):
            before(eng, read[s][n % 2], (u - 1) * (tiles_of[s] // 2) + n // 2 + 1)

        def tile(s, n):
            return bank[s][n % 2]

        def each_round(eng, steps):
            def one(i):
                for lag, name, *args in ROUND:
                    if name in steps and not (isinstance(i, int) and not 0 <= i - lag < UNITS):
                        steps[name](i - lag, *args)
            for i in range(THIRD + 1):
                one(i)
            with eng.Fori(THIRD + 1, UNITS) as i:
                one(i)
            for i in range(UNITS, UNITS + THIRD):
                one(i)

        block = stack.enter_context(nc.Block())

        @block.sync
        def _(sp):
            def load_weights(pairs, sem):
                for dst, name in pairs:
                    src = w[name]
                    if len(src.shape) == 1:
                        src = src.rearrange("(o f) -> o f", o=1).broadcast_to([P, src.shape[0]])
                    sp.dma_start(dst if name in ("wq3", "wk3", "wv3", "wo3") else dst[:], src).then_inc(sem, 16)

            def a_load(u):
                before_made(sp, "b", u, B_KV)
                sp.dma_start(h_t[:, :, :, 0, :], ctx_t[u]).then_inc(s_ha, 16)
                sp.dma_start(h_t[:, :, :, 1, :], x_t[u]).then_inc(s_ha, 16)
                before(sp, s_resb, u)
                sp.dma_start(x_a[:], x[u]).then_inc(s_xa, 16)
                before(sp, s_mask_b, u)
                sp.dma_start(mask_i[:], mask0[u]).then_inc(s_mask_i, 16)

            load_weights(((wq0, "wq0"), (cols, "cols"), (wk0, "wk0")), s_weights0)
            a_load(0)
            load_weights(((wv0, "wv0"), (bv0, "bv0"), (bo0, "bo0"), (ident, "ident")), s_weights0)
            load_weights(((wv3, "wv3"), (wo3, "wo3"), (wq3, "wq3"), (wk3, "wk3"), (wkv1, "wkv1"), (wo0, "wo0"), (w_up, "w_up"),
                          (w_down, "w_down"), (b_down, "b_down"), (wq1, "wq1"), (wo1, "wo1"), (bo1, "bo1"), (gamma, "gamma"),
                          (beta, "beta"), (wq2, "wq2"), (wk2, "wk2"), (wv2, "wv2"), (bv2, "bv2")), s_weights)

            def a_later_load(u):
                if not isinstance(u, int) or u > 0:
                    a_load(u)

            def start(u):
                if isinstance(u, int) and u == 0:
                    sp.wait_ge(s_const, CONSTANTS)
                    sp.wait_ge(s_ones, 1)

            def a_gather(u):
                before_made(sp, "a", u, A_ST + 7 + A_NEXT)
                sp.wait_ge(s_q0, 3 * u + 3)
                for p, block_at in ((0, 0), (1, 3), (2, 5)):
                    for t in range(KT):
                        r = D0 * block_at + 8 * t
                        sp.dma_start(q0s[r:r + 8], q0p[:, p, t, :]).then_inc(s_q0_gather, 16)
                sp.wait_ge(s_k0, 3 * u + 3)
                for p in range(3):
                    for t in range(KT):
                        r = D0 * p + 8 * t
                        sp.dma_start(k0s[r:r + 8], k0p[:, p, t, :]).then_inc(s_k0_gather, 16)
                sp.wait_ge(s_mask_b, u + 1)
                sp.dma_start(k0s[MASK_ROW:MASK_ROW + 1],
                             mask_b[:].rearrange("o j s p -> o (j s p)").unsqueeze(1).broadcast_to([1, NH0, 2 * T])).then_inc(s_k0_stack, 16)
                sp.wait_ge(s_q0_gather, 16 * (6 * u + 6))
                for of, to in ((0, 1), (0, 2), (3, 4)):
                    sp.dma_start(q0s[D0 * to:D0 * to + D0], q0s[D0 * of:D0 * of + D0]).then_inc(s_q0_stack, 16)
                sp.wait_ge(s_k0_gather, 16 * (6 * u + 6))
                sp.dma_start(k0s[3 * D0:5 * D0], k0s[0:2 * D0]).then_inc(s_k0_stack, 16)
                sp.dma_start(k0s[5 * D0:6 * D0], k0s[0:D0]).then_inc(s_k0_stack, 16)

            def a_maxima(u):
                wait_read(sp, "a", u, A_M)
                sp.dma_start(q0s[MASK_ROW + 1:R0], m0t[:]).then_inc(s_m0_stack, 16)

            def b_load(u):
                before_made(sp, "c", u, C_PV + 1 + C_NEXT)
                sp.dma_start(m_l[:], mask1[u]).then_inc(s_masks1, 16)
                sp.dma_start(m_s[:], mask1_t[u]).then_inc(s_masks1, 16)

            def b_stack(u):
                before_made(sp, "c", u, C_ST + 7 + C_NEXT)
                sp.wait_ge(s_k1, 4 * u + 4)
                for p in range(3):
                    sp.dma_start(k1s[D1 * p:D1 * p + D1], k1p[:, p, :]).then_inc(s_k1_gather, 16)
                sp.wait_ge(s_q1, 3 * u + 3)
                for p in range(3):
                    for t in range(KT):
                        r = D1 * p + 4 * t
                        sp.dma_start(q1s[r:r + 4], q1p[:, p, t, :]).then_inc(s_q1_gather, 16)
                sp.wait_ge(s_k1_gather, 16 * (3 * u + 3))
                for of, to, n in ((1, 3, 2), (0, 5, 1), (2, 6, 1), (0, 7, 2)):
                    sp.dma_start(k1s[D1 * to:D1 * (to + n)], k1s[D1 * of:D1 * (of + n)]).then_inc(s_k1_stack, 16)
                sp.wait_ge(s_q1_gather, 16 * (6 * u + 6))
                for to in (3, 6):
                    sp.dma_start(q1s[D1 * to:D1 * (to + 3)], q1s[0:3 * D1]).then_inc(s_q1_stack, 16)

            def c_maxima(u):
                wait_read(sp, "c", u, C_M)
                sp.dma_start(q1s[S1:R1], m1t[:]).then_inc(s_m1_stack, 16)

            def d_load(u):
                before_made(sp, "d", u, D_VV)
                sp.dma_start(ctx_d[:], ctx[u]).then_inc(s_ctxd, 16)
                sp.dma_start(ctx_td[:], ctx_t[u]).then_inc(s_ctxd, 16)

            def d_output(u):
                wait_read(sp, "d", u, D_OUT)
                sp.dma_start(out[u], x3[:]).then_inc(s_out, 16)

            each_round(sp, dict(start=start, a_load=a_later_load, a_gather=a_gather, a_maxima=a_maxima, b_load=b_load, b_stack=b_stack,
                                c_maxima=c_maxima, d_load=d_load, d_output=d_output))
            sp.wait_ge(s_out, 16 * UNITS)

        @block.tensor
        def _(pe):
            def dense(dst, lhs, rhs):
                for t in range(KT):
                    mm = pe.matmul(dst, lhs(t), rhs(t), start=(t == 0), stop=(t == KT - 1))
                return mm

            pe.wait_ge(s_weights0, 16 * WEIGHTS0)

            def start(u):
                if isinstance(u, int) and u == 0:
                    pe.wait_ge(s_weights, 16 * WEIGHTS)
                    pe.wait_ge(s_const, CONSTANTS)
                    pe.wait_ge(s_ones, 1)
                    for n, (left, right) in enumerate(((wk3, wq3), (wv3, wo3))):
                        for m in range(KT):
                            mm = dense(bank["d"][n][:, m * H:(m + 1) * H], lambda t: left[:, t, m * P:(m + 1) * P], lambda t: right[:, t, :])
                        mm.then_inc(s_fused, 1)

            def a_project(u, n):
                k = A_Q + n
                if n == 0:
                    pe.wait_ge(s_ha, 16 * (2 * u + 2))
                wait_bank(pe, "a", u, k)
                if n == 0:
                    for m in range(KT):
                        mm = dense(tile("a", k)[:, m * T:(m + 1) * T].rearrange("p (j q) -> p j q", j=J), lambda t: wq0[:, t, m * P:(m + 1) * P],
                                   lambda t: h_t[:, t, :, 1, :])
                else:
                    m = k - A_K
                    mm = dense(tile("a", k)[:, :], lambda t: wk0[:, t, m * P:(m + 1) * P], lambda t: h_t[:, t].rearrange("p j s q -> p (j s q)"))
                mm.then_inc(made["a"], 1)

            def a_values(u, j):
                wait_bank(pe, "a", u, A_V + j)
                for s in range(2):
                    mm = dense(tile("a", A_V + j)[:, s * H:(s + 1) * H], lambda t: h_t[:, t, j, s, :], lambda t: wv0[:, t, :])
                mm.then_inc(made["a"], 1)

            def b_keys(u):
                wait_bank(pe, "b", u, B_KV)
                dense(tile("b", B_KV)[:, 0:T].rearrange("p (j q) -> p j q", j=J), lambda t: wkv1[:, t, :], lambda t: h_t[:, t, :, 0, :]).then_inc(made["b"], 1)

            def a_scores(u, j, pair):
                if (j, pair) == (0, 0):
                    pe.wait_ge(s_q0_stack, 16 * (3 * u + 3))
                    pe.wait_ge(s_q0_gather, 16 * (6 * u + 6))
                    pe.wait_ge(s_k0_stack, 16 * (3 * u + 3))
                    pe.wait_ge(s_k0_gather, 16 * (6 * u + 6))
                for n in (2 * pair, 2 * pair + 1):
                    k = A_S + 8 * j + n
                    wait_bank(pe, "a", u, k)
                    for h in (2 * n, 2 * n + 1):
                        mm = pe.matmul(tile("a", k)[:, (h % 2) * 2 * P:(h % 2 + 1) * 2 * P], q0s[0:S0 + 1, h, j * P:(j + 1) * P],
                                       k0s[0:S0 + 1, h, j * 2 * P:(j + 1) * 2 * P], start=True, stop=True)
                    mm.then_inc(made["a"], 1)

            def a_maxima(u):
                pe.wait_ge(s_m0, 4 * u + 4)
                wait_bank(pe, "a", u, A_M)
                for j in range(J):
                    mm = pe.transpose(tile("a", A_M).bitcast(BF16)[0:M0_COLS * NH0, j * P:(j + 1) * P], m0p[:, j].rearrange("p c h -> p (c h)"), ident_bf[:])
                mm.then_inc(made["a"], 1)

            def a_weights(u, j, pair):
                if (j, pair) == (0, 0):
                    pe.wait_ge(s_m0_stack, 16 * (u + 1))
                s = pair // 2
                for g in (pair % 2 * 2, pair % 2 * 2 + 1):
                    k = A_ST + A_NEXT * j + 4 * s + g
                    wait_bank(pe, "a", u, k)
                    for h in range(4 * g, 4 * g + 4):
                        mm = pe.matmul(tile("a", k)[:, (h % 4) * P:(h % 4 + 1) * P], k0s[0:R0, h, (2 * j + s) * P:(2 * j + s + 1) * P],
                                       q0s[0:R0, h, j * P:(j + 1) * P], start=True, stop=True)
                    mm.then_inc(made["a"], 1)

            def a_attend(u, j):
                wait_read(pe, "a", u, A_ST + A_NEXT * j + 7)
                wait_bank(pe, "a", u, A_PV + A_NEXT * j)
                for g in range(4):
                    for s in range(2):
                        for c in range(4):
                            mm = pe.matmul(tile("a", A_PV + A_NEXT * j)[32 * c:32 * c + 32, g * P:(g + 1) * P], v0[:, j, s, 4 * g + c, :],
                                           p0[:, s, 4 * g + c, :], start=(s == 0), stop=(s == 1), tile_position=(0, 32 * c))
                mm.then_inc(made["a"], 1)

            def a_turn(u, j):
                wait_read(pe, "a", u, A_PV + A_NEXT * j)
                wait_bank(pe, "a", u, A_OT + A_NEXT * j)
                for g in range(4):
                    mm = pe.transpose(tile("a", A_OT + A_NEXT * j)[:, g * P:(g + 1) * P], o0t[:, g * P:(g + 1) * P], ident[:])
                mm.then_inc(made["a"], 1)

            def a_join(u):
                wait_bank(pe, "a", u, A_FT)
                wait_read(pe, "a", u, A_OT + A_NEXT)
                for j in range(J):
                    for t in range(KT):
                        mm = pe.transpose(tile("a", A_FT)[:, t * T + j * P:t * T + (j + 1) * P], o0[:, j, t * P:(t + 1) * P], ident[:])
                mm.then_inc(made["a"], 1)

            def a_out(u):
                wait_read(pe, "a", u, A_FT)
                wait_bank(pe, "a", u, A_OUT)
                for j in range(J):
                    mm = dense(tile("a", A_OUT)[:, j * H:(j + 1) * H], lambda t: f0t[:, t, j * P:(j + 1) * P], lambda t: wo0[:, t, :])
                mm.then_inc(made["a"], 1)

            def b_norm(u):
                pe.wait_ge(s_rms, 5 * u + 5)
                wait_bank(pe, "b", u, B_NT)
                for j in range(J):
                    for t in range(KT):
                        mm = pe.transpose(tile("b", B_NT)[:, t * T + j * P:t * T + (j + 1) * P], y0n[:, j, t * P:(t + 1) * P], ident[:])
                mm.then_inc(made["b"], 1)

            def b_up(u, n):
                if n == 0:
                    wait_read(pe, "b", u, B_NT)
                wait_bank(pe, "b", u, B_UP + n)
                for m in (2 * n, 2 * n + 1):
                    mm = dense(tile("b", B_UP + n)[:, (m % 2) * T:(m % 2 + 1) * T], lambda t: w_up[:, t, m * P:(m + 1) * P], lambda t: n_t[:, t, :])
                mm.then_inc(made["b"], 1)

            def b_down_(u, n):
                j, half = n // 2, n % 2
                if n == 0:
                    wait_read(pe, "b", u, B_UP + 3)
                    wait_bank(pe, "b", u, B_DOWN)
                for m in range(half * MT // 2, (half + 1) * MT // 2):
                    mm = pe.matmul(tile("b", B_DOWN)[:, j * H:(j + 1) * H], up[:, m, j * P:(j + 1) * P], w_down[:, m, :], start=(m == 0), stop=(m == MT - 1))
                if n == 3:
                    mm.then_inc(made["b"], 1)

            def b_turn(u):
                wait_read(pe, "b", u, B_DOWN)
                wait_bank(pe, "b", u, B_XT)
                for j in range(J):
                    for t in range(KT):
                        mm = pe.transpose(tile("b", B_XT)[:, t * T + j * P:t * T + (j + 1) * P], x1[:, j, t * P:(t + 1) * P], ident[:])
                mm.then_inc(made["b"], 1)

            def b_project(u):
                wait_read(pe, "b", u, B_XT)
                wait_bank(pe, "b", u, B_Q)
                for m in range(KT):
                    mm = dense(tile("b", B_Q)[:, m * T:(m + 1) * T], lambda t: wq1[:, t, m * P:(m + 1) * P], lambda t: x1_t[:, t, :])
                mm.then_inc(made["b"], 1)

            def b_keep(u):
                wait_read(pe, "b", u, B_KV)
                wait_bank(pe, "b", u, B_V)
                for j in range(J):
                    mm = pe.transpose(tile("b", B_V)[:, j * P:(j + 1) * P], kv1f[:, j * P:(j + 1) * P], ident[:])
                mm.then_inc(made["b"], 1)

            def c_scores(u, j, pair):
                if (j, pair) == (0, 0):
                    pe.wait_ge(s_q1_stack, 16 * (2 * u + 2))
                    pe.wait_ge(s_q1_gather, 16 * (6 * u + 6))
                    pe.wait_ge(s_k1_stack, 16 * (4 * u + 4))
                    pe.wait_ge(s_k1_gather, 16 * (3 * u + 3))
                for kv in (2 * pair, 2 * pair + 1):
                    k = C_S + 8 * j + kv
                    wait_bank(pe, "c", u, k)
                    for g in range(G1):
                        mm = pe.matmul(tile("c", k)[:, g * P:(g + 1) * P], q1s[0:S1, kv * G1 + g, j * P:(j + 1) * P],
                                       k1s[0:S1, kv, j * P:(j + 1) * P], start=True, stop=True)
                    mm.then_inc(made["c"], 1)

            def c_maxima(u):
                pe.wait_ge(s_m1, 5 * u + 5)
                wait_bank(pe, "c", u, C_M)
                for j in range(J):
                    mm = pe.transpose(tile("c", C_M).bitcast(BF16)[0:3 * NH1, j * P:(j + 1) * P], m1p[:, j].rearrange("p c h -> p (c h)"), ident_bf[:])
                mm.then_inc(made["c"], 1)

            def c_weights(u, j, pair):
                if (j, pair) == (0, 0):
                    pe.wait_ge(s_m1_stack, 16 * (u + 1))
                for kv in (2 * pair, 2 * pair + 1):
                    k = C_ST + C_NEXT * j + kv
                    wait_bank(pe, "c", u, k)
                    pe.matmul(tile("c", k)[:, :].rearrange("p (g q) -> p g q", g=G1), k1s[0:R1, kv, j * P:(j + 1) * P],
                              q1s[0:R1, kv * G1:(kv + 1) * G1, j * P:(j + 1) * P], start=True, stop=True).then_inc(made["c"], 1)

            def c_attend(u, j):
                if j == 0:
                    wait_read(pe, "b", u, B_V)
                pe.wait_ge(s_exp1, 16 * u + 8 * j + 8)
                for half in range(2):
                    k = C_PV + C_NEXT * j + half
                    wait_bank(pe, "c", u, k)
                    for c in range(4):
                        kv = 4 * half + c
                        mm = pe.matmul(tile("c", k)[32 * c:32 * c + 32, :], v1[:, j, kv, :],
                                       p1[:, kv * G1:(kv + 1) * G1, :].rearrange("p g q -> p (g q)"), start=True, stop=True, tile_position=(0, 32 * c))
                    mm.then_inc(made["c"], 1)

            def c_turn(u, j):
                for half in range(2):
                    k = C_TR + C_NEXT * j + half
                    wait_read(pe, "c", u, k - 2)
                    wait_bank(pe, "c", u, k)
                    for g in range(G1):
                        mm = pe.transpose(tile("c", k)[:, g * P:(g + 1) * P], o1t[:, half, g * P:(g + 1) * P], ident[:])
                    mm.then_inc(made["c"], 1)

            def c_join(u):
                wait_bank(pe, "c", u, C_FT)
                wait_read(pe, "c", u, C_TR + C_NEXT + 1)
                for j in range(J):
                    for t in range(KT):
                        mm = pe.transpose(tile("c", C_FT)[:, t * T + j * P:t * T + (j + 1) * P], o1[:, j, t * P:(t + 1) * P], ident[:])
                mm.then_inc(made["c"], 1)

            def c_out(u, j):
                if j == 0:
                    wait_read(pe, "c", u, C_FT)
                wait_bank(pe, "c", u, C_OUT + j)
                dense(tile("c", C_OUT + j)[:, 0:H], lambda t: f1t[:, t, j * P:(j + 1) * P], lambda t: wo1[:, t, :]).then_inc(made["c"], 1)

            def d_context(u, n):
                if n == 0:
                    if isinstance(u, int) and u == 0:
                        pe.wait_ge(s_fused_read, 2)
                    pe.wait_ge(s_ctxd, 16 * (2 * u + 2))
                    wait_bank(pe, "d", u, D_K)
                    mm = pe.matmul(tile("d", D_K)[0:D2, :], wk2[:], ctx_d[:].rearrange("p j n -> p (j n)"), start=True, stop=True)
                else:
                    wait_bank(pe, "d", u, D_V)
                    for j in range(J):
                        for t in range(KT):
                            mm = pe.matmul(tile("d", D_V)[:, (KT * j + t) * P:(KT * j + t + 1) * P], ctx_d[:, j, t * P:(t + 1) * P], wv2[:], start=True, stop=True)
                mm.then_inc(made["d"], 1)

            def d_context_keys(u):
                wait_bank(pe, "d", u, D_KK)
                for m in range(KT):
                    mm = dense(tile("d", D_KK)[:, m * T:(m + 1) * T], lambda t: key3[:, t, m * P:(m + 1) * P], lambda t: ctx_td[:, t, :])
                mm.then_inc(made["d"], 1)

            def d_context_values(u):
                wait_bank(pe, "d", u, D_VV)
                for j in range(J):
                    mm = dense(tile("d", D_VV)[:, j * H:(j + 1) * H], lambda t: ctx_td[:, t, j * P:(j + 1) * P], lambda t: val3[:, t, :])
                mm.then_inc(made["d"], 1)

            def d_query(u):
                pe.wait_ge(s_x2, u + 1)
                wait_bank(pe, "d", u, D_Q)
                pe.matmul(tile("d", D_Q)[0:D2, :], wq2[:], x2[:].rearrange("p j n -> p (j n)"), start=True, stop=True).then_inc(made["d"], 1)

            def d_scores(u, j):
                wait_read(pe, "d", u, D_Q)
                wait_bank(pe, "d", u, D_S + j)
                for t in range(KT):
                    mm = pe.matmul(tile("d", D_S + j)[:, t * H:(t + 1) * H], q2[:, j, t * P:(t + 1) * P], k2[:, j, :], start=True, stop=True)
                mm.then_inc(made["d"], 1)

            def d_turn(u, j):
                pe.wait_ge(s_p2n, 2 * u + j + 1)
                wait_bank(pe, "d", u, D_PT + j)
                for m in range(KT):
                    for t in range(KT):
                        mm = pe.transpose(tile("d", D_PT + j)[:, m * H + t * P:m * H + (t + 1) * P], p2[:, j, t, m * P:(m + 1) * P], ident[:])
                mm.then_inc(made["d"], 1)

            def d_attend(u):
                wait_bank(pe, "d", u, D_PV)
                for j in range(J):
                    wait_read(pe, "d", u, D_PT + j)
                    for m in range(KT):
                        mm = pe.matmul(tile("d", D_PV)[:, j * H:(j + 1) * H], v2[:, j, m, :], p2t[:, j, m, :], start=(m == 0), stop=(m == KT - 1))
                mm.then_inc(made["d"], 1)

            def d_x(u):
                wait_read(pe, "d", u, D_PV)
                wait_bank(pe, "d", u, D_XT)
                for j in range(J):
                    for t in range(KT):
                        mm = pe.transpose(tile("d", D_XT)[:, t * T + j * P:t * T + (j + 1) * P], x3[:, j, t * P:(t + 1) * P], ident[:])
                mm.then_inc(made["d"], 1)

            def d_text_scores(u):
                wait_read(pe, "d", u, D_XT)
                wait_bank(pe, "d", u, D_S3)
                for j in range(J):
                    mm = dense(tile("d", D_S3)[:, j * P:(j + 1) * P], lambda t: x3_t[:, t, j * P:(j + 1) * P], lambda t: kk3[:, t, j * P:(j + 1) * P])
                mm.then_inc(made["d"], 1)

            def d_text(u):
                wait_read(pe, "d", u, D_S3)
                wait_bank(pe, "d", u, D_PT3)
                for j in range(J):
                    mm = pe.transpose(tile("d", D_PT3)[:, j * P:(j + 1) * P], p3[:, j, :], ident[:])
                mm.then_inc(made["d"], 1)

            def d_output(u):
                wait_read(pe, "d", u, D_PT3)
                wait_bank(pe, "d", u, D_OUT)
                for j in range(J):
                    mm = pe.matmul(tile("d", D_OUT)[:, j * H:(j + 1) * H], p3t[:, j, :], vv3[:, j, :], start=True, stop=True)
                mm.then_inc(made["d"], 1)

            each_round(pe, dict(start=start, a_project=a_project, a_values=a_values, a_scores=a_scores, a_maxima=a_maxima, a_weights=a_weights,
                                a_attend=a_attend, a_turn=a_turn, a_join=a_join, a_out=a_out, b_keys=b_keys, b_norm=b_norm, b_up=b_up,
                                b_down=b_down_, b_turn=b_turn, b_project=b_project, b_keep=b_keep, c_scores=c_scores, c_maxima=c_maxima,
                                c_weights=c_weights, c_attend=c_attend, c_turn=c_turn, c_join=c_join, c_out=c_out,
                                d_context=d_context, d_context_keys=d_context_keys, d_context_values=d_context_values,
                                d_query=d_query, d_scores=d_scores, d_turn=d_turn, d_attend=d_attend, d_x=d_x,
                                d_text_scores=d_text_scores, d_text=d_text, d_output=d_output))

        @block.scalar
        def _(act):
            act.wait_ge(s_weights0, 16 * WEIGHTS0)
            act.activation(bq1[:], bq1_raw, ACT.Copy, scale=float(D1) ** -0.5).then_inc(s_const, 1)
            act.activation(ident_bf[:], ident[:], ACT.Copy).then_inc(s_const, 1)

            def start(u):
                if isinstance(u, int) and u == 0:
                    act.wait_ge(s_weights, 16 * WEIGHTS)
                    act.wait_ge(s_const, CONSTANTS)
                    for n, dst in enumerate((key3, val3)):
                        act.wait_ge(s_fused, n + 1)
                        act.activation(dst[:].rearrange("p t h -> p (t h)"), bank["d"][n][:, :], ACT.Copy).then_inc(s_fused_read, 1)

            def a_project(u, n):
                k = A_Q + n
                wait_made(act, "a", u, k)
                if n == 0:
                    before(act, s_q0_gather, 16 * 6 * u)
                    for dst in (q0f, q0p[:, 0]):
                        for m in range(KT):
                            ins = act.activation(dst[:, m, :], tile("a", k)[:, m * T:(m + 1) * T], ACT.Identity, bias=bq0[:, m:m + 1])
                else:
                    if n == 1:
                        before(act, s_k0_gather, 16 * 6 * u)
                    m = k - A_K
                    for dst in (k0f, k0p[:, 0]):
                        ins = act.activation(dst[:, m, :], tile("a", k)[:, :], ACT.Identity, bias=bk0[:, m:m + 1])
                ins.then_inc(read["a"][k % 2], 1)

            def b_keys(u):
                before(act, s_k1, 4 * u)
                before_made(act, "b", u, B_V)
                wait_made(act, "b", u, B_KV)
                act.activation(kv1f[:], tile("b", B_KV)[:, 0:T], ACT.Identity, bias=bkv1).then_inc(read["b"][B_KV % 2], 1)

            def a_weights(u, j, pair):
                if (j, pair) == (0, 0):
                    before_made(act, "b", u, B_DOWN)
                s = pair // 2
                for g in (pair % 2 * 2, pair % 2 * 2 + 1):
                    k = A_ST + A_NEXT * j + 4 * s + g
                    wait_made(act, "a", u, k)
                    act.activation(p0[:, s, 4 * g:4 * g + 4, :].rearrange("p h q -> p (h q)"), tile("a", k)[:, :], ACT.Exp,
                                   scale=1.0 / D0).then_inc(read["a"][k % 2], 1)

            def a_attend(u, j):
                wait_made(act, "a", u, A_PV + A_NEXT * j)
                act.activation(o0t[:], tile("a", A_PV + A_NEXT * j)[:, :], ACT.Copy).then_inc(read["a"][(A_PV + A_NEXT * j) % 2], 1)

            def a_join(u):
                wait_made(act, "a", u, A_FT)
                act.activation(f0t.rearrange("p t q -> p (t q)"), tile("a", A_FT)[:, :], ACT.Copy).then_inc(read["a"][A_FT % 2], 1)

            def a_out(u):
                before(act, s_rms, 5 * u)
                before_made(act, "b", u, B_NT)
                wait_read(act, "a", u, A_OUT)
                for j in range(J):
                    act.activation(y0n[:, j, :], y0[:, j, :], ACT.Square, accum_out=ss0[:, j:j + 1]).then_inc(s_rms, 1)

            def b_norm(u):
                before_made(act, "b", u, B_UP + 3)
                wait_made(act, "b", u, B_NT)
                for t in range(KT):
                    ins = act.activation(n_t[:, t, :], tile("b", B_NT)[:, t * T:(t + 1) * T], ACT.Copy, scale=norm_w[:, t:t + 1])
                ins.then_inc(read["b"][B_NT % 2], 1)

            def b_up_(u, n):
                if n == 0:
                    wait_made(act, "a", u, A_PV + A_NEXT)
                wait_made(act, "b", u, B_UP + n)
                for m in (2 * n, 2 * n + 1):
                    ins = act.activation(up[:, m, :], tile("b", B_UP + n)[:, (m % 2) * T:(m % 2 + 1) * T], ACT.Gelu_apprx_tanh, bias=b_up[:, m:m + 1])
                ins.then_inc(read["b"][(B_UP + n) % 2], 1)

            def b_turn(u):
                wait_made(act, "b", u, B_XT)
                act.activation(x1_t[:].rearrange("p t q -> p (t q)"), tile("b", B_XT)[:, :], ACT.Copy).then_inc(read["b"][B_XT % 2], 1)

            def b_keep(u):
                before_made(act, "c", u, C_PV + 1 + C_NEXT)
                wait_made(act, "b", u, B_Q)
                before(act, s_q1_gather, 16 * 6 * u)
                for dst in (q1f, q1p[:, 0]):
                    for m in range(KT):
                        ins = act.activation(dst[:, m, :], tile("b", B_Q)[:, m * T:(m + 1) * T], ACT.Identity, bias=bq1[:, m:m + 1], scale=float(D1) ** -0.5)
                ins.then_inc(read["b"][B_Q % 2], 1)

            def c_weights(u, j, pair):
                for kv in (2 * pair, 2 * pair + 1):
                    wait_read(act, "c", u, C_ST + C_NEXT * j + kv)
                    rows = p1[:, kv * G1:(kv + 1) * G1, :]
                    act.activation(rows, rows, ACT.Exp).then_inc(s_exp1, 1)

            def c_attend(u, j):
                for half in range(2):
                    k = C_PV + C_NEXT * j + half
                    wait_made(act, "c", u, k)
                    act.activation(o1t[:, half, :], tile("c", k)[:, :], ACT.Copy).then_inc(read["c"][k % 2], 1)

            def c_join(u):
                wait_made(act, "c", u, C_FT)
                act.activation(f1t[:].rearrange("p t q -> p (t q)"), tile("c", C_FT)[:, :], ACT.Copy).then_inc(read["c"][C_FT % 2], 1)

            def d_context(u, n):
                if n == 1:
                    return
                wait_made(act, "d", u, D_K)
                act.activation(k2[:].rearrange("p j n -> p (j n)"), tile("d", D_K)[0:D2, :], ACT.Identity, bias=bk2).then_inc(read["d"][D_K % 2], 1)

            def d_context_keys(u):
                wait_made(act, "d", u, D_KK)
                act.activation(kk3[:].rearrange("p t s -> p (t s)"), tile("d", D_KK)[:, :], ACT.Copy).then_inc(read["d"][D_KK % 2], 1)

            def d_context_values(u):
                wait_made(act, "d", u, D_VV)
                act.activation(vv3[:].rearrange("p j o -> p (j o)"), tile("d", D_VV)[:, :], ACT.Copy).then_inc(read["d"][D_VV % 2], 1)

            def d_query(u):
                wait_made(act, "d", u, D_Q)
                act.activation(q2[:].rearrange("p j n -> p (j n)"), tile("d", D_Q)[0:D2, :], ACT.Identity, bias=bq2).then_inc(read["d"][D_Q % 2], 1)

            def d_scores(u, j):
                before(act, s_p2n, 2 * (u - 1) + j + 1)
                act.wait_ge(s_m2, 2 * u + j + 1)
                for t in range(KT):
                    ins = act.activation(p2[:, j, t, :], tile("d", D_S + j)[:, t * H:(t + 1) * H], ACT.Exp, bias=m2[:, j, t:t + 1],
                                         accum_out=sum2[:, j, t:t + 1])
                ins.then_inc(read["d"][(D_S + j) % 2], 1)

            def d_turn(u, j):
                wait_made(act, "d", u, D_PT + j)
                act.activation(p2t[:, j].rearrange("p m n -> p (m n)"), tile("d", D_PT + j)[:, :], ACT.Copy).then_inc(read["d"][(D_PT + j) % 2], 1)

            def d_x(u):
                wait_made(act, "d", u, D_XT)
                act.activation(x3_t.rearrange("p t q -> p (t q)"), tile("d", D_XT)[:, :], ACT.Copy).then_inc(read["d"][D_XT % 2], 1)

            def d_text_scores(u):
                act.wait_ge(s_m3, 2 * u + 2)
                for j in range(J):
                    ins = act.activation(p3[:, j, :], tile("d", D_S3)[:, j * P:(j + 1) * P], ACT.Exp, bias=m3s[:, j:j + 1], scale=1.0 / 16,
                                         accum_out=sum3[:, j:j + 1])
                ins.then_inc(read["d"][D_S3 % 2], 1)

            each_round(act, dict(start=start, a_project=a_project, a_weights=a_weights, a_attend=a_attend, a_join=a_join, a_out=a_out, b_keys=b_keys,
                                 b_norm=b_norm, b_up=b_up_, b_turn=b_turn, b_keep=b_keep, c_weights=c_weights,
                                 c_attend=c_attend, c_join=c_join, d_context=d_context, d_context_keys=d_context_keys,
                                 d_context_values=d_context_values, d_query=d_query, d_scores=d_scores, d_turn=d_turn, d_x=d_x,
                                 d_text_scores=d_text_scores))

        @block.vector
        def _(dve):
            dve.memset(power[:], -0.5).then_inc(s_const, 1)
            dve.memset(mask_b[:, :, 1, :], 0.0).then_inc(s_const, 1)
            dve.memset(m0p[:, :, 3:M0_COLS, :], 0.0).then_inc(s_const, 1)
            dve.memset(v0[:, :, :, :, D0:D0 + 1], 1.0).then_inc(s_const, 1)
            dve.memset(v0[:, :, :, :, D0 + 1:OUT_W], 0.0).then_inc(s_const, 1)
            dve.memset(v1[:, :, :, D1:D1 + 1], 1.0).then_inc(s_const, 1)
            dve.memset(v1[:, :, :, D1 + 1:OUT_W], 0.0).then_inc(s_const, 1)
            dve.memset(k1s[64:P], 1.0).then_inc(s_const, 1)
            dve.memset(q0s[MASK_ROW:P], 1.0).then_inc(s_const, 1)
            dve.wait_ge(s_weights0, 16 * WEIGHTS0)

            def start(u):
                if isinstance(u, int) and u == 0:
                    dve.wait_ge(s_weights, 16 * WEIGHTS)
                    dve.wait_ge(s_const, CONSTANTS)

            def middle(rest, pieces, sem, rested):
                dve.wait_ge(sem, rested)
                dve.tensor_copy(pieces, rest).then_inc(sem, 1)

            def split_maxima(steps, m, rest, pieces, sem):
                dve.tensor_copy(pieces[:, :, 0, :], m).then_inc(sem, 1)
                dve.wait_ge(sem, steps + 1)
                dve.tensor_tensor(rest, m, pieces[:, :, 0, :], ALU.subtract).then_inc(sem, 1)
                dve.wait_ge(sem, steps + 2)
                dve.tensor_copy(pieces[:, :, 1, :], rest).then_inc(sem, 1)
                dve.wait_ge(sem, steps + 3)
                dve.tensor_tensor(pieces[:, :, 2, :], rest, pieces[:, :, 1, :], ALU.subtract).then_inc(sem, 1)

            def a_project(u, n):
                if n == 0:
                    before(dve, s_k0_stack, 16 * 3 * u)
                    dve.wait_ge(s_mask_i, 16 * (u + 1))
                    dve.tensor_scalar(mask_b[:, :, 0, :], mask_i[:], 0.0, MASKED, ALU.is_equal, ALU.mult).then_inc(s_mask_b, 1)

            def a_values(u, j):
                wait_made(dve, "a", u, A_V + j)
                dve.tensor_tensor(v0[:, j, :, :, 0:D0], tile("a", A_V + j)[:, :].rearrange("p (s h d) -> p s h d", s=2, h=NH0),
                                  bv0[:].rearrange("p (o h d) -> p o h d", o=1, h=NH0).broadcast_to([P, 2, NH0, D0]),
                                  ALU.add).then_inc(read["a"][(A_V + j) % 2], 1)

            def a_stack(u):
                middle(q0f, q0p[:, 1], s_q0, 3 * u + 1)
                middle(k0f, k0p[:, 1], s_k0, 3 * u + 1)

            def a_scores(u, j, pair):
                if (j, pair) == (0, 0):
                    before(dve, s_m0, 4 * u)
                for n in (2 * pair, 2 * pair + 1):
                    k = A_S + 8 * j + n
                    wait_made(dve, "a", u, k)
                    dve.tensor_reduce(m0[:, j, 2 * n:2 * n + 2], tile("a", k)[:, :].rearrange("p (h n) -> p h n", h=2), AX_X, ALU.max,
                                      negate=True).then_inc(read["a"][k % 2], 1)

            def a_split(u):
                for n in (14, 15):
                    wait_read(dve, "a", u, A_S + n)
                split_maxima(4 * u, m0[:], m0r[:], m0p, s_m0)

            def a_maxima(u):
                before(dve, s_m0_stack, 16 * u)
                wait_made(dve, "a", u, A_M)
                dve.tensor_copy(m0t[:], tile("a", A_M).bitcast(BF16)[0:3 * NH0, 0:T]).then_inc(read["a"][A_M % 2], 1)

            def a_turn(u, j):
                heads = tile("a", A_OT + A_NEXT * j)[:, :].rearrange("p (h e) -> p h e", h=NH0)
                wait_made(dve, "a", u, A_OT + A_NEXT * j)
                dve.reciprocal(rc0[:, j, :].unsqueeze(2), heads[:, :, D0:D0 + 1]).then_inc(s_rc0, 1)
                dve.wait_ge(s_rc0, 2 * u + j + 1)
                dve.tensor_tensor(o0[:, j, :].rearrange("p (h d) -> p h d", h=NH0), heads[:, :, 0:D0],
                                  rc0[:, j, :].unsqueeze(2).broadcast_to([P, NH0, D0]), ALU.mult).then_inc(read["a"][(A_OT + A_NEXT * j) % 2], 1)

            def a_out(u):
                dve.wait_ge(s_res0, u + 1)
                wait_made(dve, "a", u, A_OUT)
                dve.tensor_tensor(y0[:], tile("a", A_OUT)[:, :].rearrange("p (j h) -> p j h", j=J), res0[:], ALU.add).then_inc(read["a"][A_OUT % 2], 1)

            def a_norm(u):
                dve.wait_ge(s_rms, 5 * u + 2)
                dve.tensor_scalar(ms0[:], ss0[:], 1.0 / H, EPS, ALU.mult, ALU.add).then_inc(s_rms, 1)
                dve.wait_ge(s_rms, 5 * u + 4)
                for j in range(J):
                    ins = dve.tensor_scalar(y0n[:, j, :], y0[:, j, :], rs0[:, j:j + 1], None, ALU.mult)
                ins.then_inc(s_rms, 1)

            def b_add(u):
                dve.wait_ge(s_resb, u + 1)
                before(dve, s_res1, u)
                wait_made(dve, "b", u, B_DOWN)
                dve.tensor_tensor(x1[:], tile("b", B_DOWN)[:, :].rearrange("p (j h) -> p j h", j=J), res_b[:], ALU.add).then_inc(read["b"][B_DOWN % 2], 1)

            def b_keep(u):
                wait_read(dve, "b", u, B_KV)
                before(dve, s_k1_gather, 16 * 3 * u)
                dve.tensor_copy(k1p[:, 0], kv1f[0:KV1 * D1]).then_inc(s_k1, 1)
                before_made(dve, "c", u, C_PV + 1 + C_NEXT)
                wait_made(dve, "b", u, B_V)
                dve.tensor_copy(v1[:, :, :, 0:D1], tile("b", B_V)[:, 0:T].rearrange("p (j c) -> p j c", j=J)[:, :, KV1 * D1:]
                                .rearrange("p j (k d) -> p j k d", d=D1)).then_inc(read["b"][B_V % 2], 1)

            def b_stack(u):
                middle(k1r, k1p[:, 1], s_k1, 4 * u + 2)
                middle(q1f, q1p[:, 1], s_q1, 3 * u + 1)

            def c_scores(u, j, pair):
                if (j, pair) == (0, 0):
                    dve.wait_ge(s_masks1, 16 * (2 * u + 2))
                    before(dve, s_m1, 5 * u)
                for n in (2 * pair, 2 * pair + 1):
                    k = C_S + 8 * j + n
                    wait_made(dve, "c", u, k)
                    dve.memset(spare[:, k + 1:k + 2], 0.0)
                    for g in range(G1):
                        ins = dve.tensor_tensor_reduce(masked[:, k % 2, g, :], tile("c", k)[:, g * P:(g + 1) * P], m_l[:, j, :], 1.0, LOWEST,
                                                       ALU.add, ALU.max, m1[:, j, n * G1 + g:n * G1 + g + 1])
                    ins.then_inc(read["c"][k % 2], 1)

            def c_split(u):
                for n in (14, 15):
                    wait_read(dve, "c", u, C_S + n)
                dve.tensor_scalar(m1[:], m1[:], -1.0, None, ALU.mult).then_inc(s_m1, 1)
                dve.wait_ge(s_m1, 5 * u + 1)
                split_maxima(5 * u + 1, m1[:], m1r[:], m1p, s_m1)

            def c_maxima(u):
                before(dve, s_m1_stack, 16 * u)
                wait_made(dve, "c", u, C_M)
                dve.tensor_copy(m1t[:], tile("c", C_M).bitcast(BF16)[0:3 * NH1, 0:T]).then_inc(read["c"][C_M % 2], 1)

            def c_weights(u, j, pair):
                if (j, pair) == (0, 0):
                    before_made(dve, "d", u, D_OUT)
                    dve.wait_ge(s_q1, 3 * u + 3)
                    dve.wait_ge(s_k1, 4 * u + 4)
                for kv in (2 * pair, 2 * pair + 1):
                    k = C_ST + C_NEXT * j + kv
                    wait_made(dve, "c", u, k)
                    dve.tensor_tensor(p1[:, kv * G1:(kv + 1) * G1, :], tile("c", k)[:, :].rearrange("p (g s) -> p g s", g=G1),
                                      m_s[:, j:j + 1, :].broadcast_to([P, G1, P]), ALU.add).then_inc(read["c"][k % 2], 1)

            def c_turn(u, j):
                for half in range(2):
                    k = C_TR + C_NEXT * j + half
                    heads = tile("c", k)[:, :].rearrange("p (g k e) -> p g k e", g=G1, k=4)
                    wait_made(dve, "c", u, k)
                    dve.reciprocal(rc1[:, half].unsqueeze(3), heads[:, :, :, D1:D1 + 1]).then_inc(s_rc1, 1)
                    dve.wait_ge(s_rc1, 4 * u + 2 * j + half + 1)
                    dve.tensor_tensor(o1[:, j, half * P:(half + 1) * P].rearrange("p (k g d) -> p g k d", k=4, g=G1), heads[:, :, :, 0:D1],
                                      rc1[:, half].unsqueeze(3).broadcast_to([P, G1, 4, D1]), ALU.mult).then_inc(read["c"][k % 2], 1)

            def c_out(u, j):
                if j == 0:
                    dve.wait_ge(s_res1, u + 1)
                    before(dve, s_x2, u)
                wait_made(dve, "c", u, C_OUT + j)
                dve.tensor_tensor(y1[:, j, :], tile("c", C_OUT + j)[:, 0:H], res1[:, j, :], ALU.add).then_inc(read["c"][(C_OUT + j) % 2], 1)

            def c_norm(u, part):
                if part == 0:
                    for j in range(J):
                        wait_read(dve, "c", u, C_OUT + j)
                        dve.bn_stats(st1[:, j, :], y1[:, j, :]).then_inc(s_ln, 1)
                elif part == 1:
                    dve.wait_ge(s_ln, 8 * u + 2)
                    dve.memset(spare[:, 0:1], 0.0)
                    for j in range(J):
                        dve.bn_aggr(mv1[:, j, :], st1[:, j, :]).then_inc(s_ln, 1)
                    dve.wait_ge(s_ln, 8 * u + 4)
                    dve.tensor_scalar(ve1[:], mv1[:, :, 1], EPS, None, ALU.add).then_inc(s_ln, 1)
                    for j in range(J):
                        dve.scalar_tensor_tensor(out=y1[:, j, :], in0=y1[:, j, :], scalar=mv1[:, j, 0:1], in1=gamma[:],
                                                 op0=ALU.subtract, op1=ALU.mult).then_inc(s_ln, 1)
                else:
                    dve.wait_ge(s_ln, 8 * u + 8)
                    before_made(dve, "d", u, D_Q)
                    for j in range(J):
                        ins = dve.scalar_tensor_tensor(out=x2[:, j, :], in0=y1[:, j, :], scalar=rs1[:, j:j + 1], in1=beta[:],
                                                       op0=ALU.mult, op1=ALU.add)
                    ins.then_inc(s_x2, 1)

            def d_context(u, n):
                if n == 0:
                    return
                wait_made(dve, "d", u, D_V)
                dve.tensor_tensor(v2[:].rearrange("p j t c -> p (j t) c"), tile("d", D_V)[:, :].rearrange("p (j c) -> p j c", j=J * KT),
                                  bv2[:].unsqueeze(1).broadcast_to([P, J * KT, P]), ALU.add).then_inc(read["d"][D_V % 2], 1)

            def d_scores(u, j):
                wait_made(dve, "d", u, D_S + j)
                dve.tensor_reduce(m2[:, j, :], tile("d", D_S + j)[:, :].rearrange("p (t m) -> p t m", t=KT), AX_X, ALU.max,
                                  negate=True).then_inc(s_m2, 1)

            def d_scale(u, j):
                wait_read(dve, "d", u, D_S + j)
                dve.reciprocal(rc2[:, j, :], sum2[:, j, :]).then_inc(s_rc2, 1)
                dve.wait_ge(s_rc2, 2 * u + j + 1)
                for t in range(KT):
                    ins = dve.tensor_scalar(p2[:, j, t, :], p2[:, j, t, :], rc2[:, j, t:t + 1], None, ALU.mult)
                ins.then_inc(s_p2n, 1)

            def d_attend(u):
                before(dve, s_out, 16 * u)
                wait_made(dve, "d", u, D_PV)
                dve.tensor_tensor(x3[:], tile("d", D_PV)[:, :].rearrange("p (j n) -> p j n", j=J), x2[:], ALU.add).then_inc(read["d"][D_PV % 2], 1)

            def d_text_scores(u):
                wait_made(dve, "d", u, D_S3)
                dve.tensor_reduce(m3[:], tile("d", D_S3)[:, 0:T].rearrange("p (j s) -> p j s", j=J), AX_X, ALU.max, negate=True).then_inc(s_m3, 1)
                dve.wait_ge(s_m3, 2 * u + 1)
                dve.tensor_scalar(m3s[:], m3[:], 1.0 / 16, None, ALU.mult).then_inc(s_m3, 1)

            def d_text(u):
                wait_read(dve, "d", u, D_S3)
                dve.reciprocal(rc3[:], sum3[:]).then_inc(s_r3, 1)
                dve.wait_ge(s_r3, 2 * u + 1)
                dve.tensor_scalar(ar3[:], rc3[:], alpha, None, ALU.mult).then_inc(s_r3, 1)
                wait_made(dve, "d", u, D_PT3)
                dve.tensor_copy(p3t.rearrange("p j q -> p (j q)"), tile("d", D_PT3)[:, 0:T]).then_inc(read["d"][D_PT3 % 2], 1)

            def d_output(u):
                dve.wait_ge(s_r3, 2 * u + 2)
                wait_made(dve, "d", u, D_OUT)
                for j in range(J):
                    ins = dve.scalar_tensor_tensor(out=x3[:, j, :], in0=tile("d", D_OUT)[:, j * H:(j + 1) * H], scalar=ar3[:, j:j + 1],
                                                   in1=x3[:, j, :], op0=ALU.mult, op1=ALU.add)
                ins.then_inc(read["d"][D_OUT % 2], 1)

            each_round(dve, dict(start=start, a_project=a_project, a_values=a_values, a_stack=a_stack, a_scores=a_scores, a_split=a_split,
                                 a_maxima=a_maxima, a_turn=a_turn, a_out=a_out, a_norm=a_norm, b_add=b_add, b_keep=b_keep,
                                 b_stack=b_stack, c_scores=c_scores, c_split=c_split, c_maxima=c_maxima, c_weights=c_weights,
                                 c_turn=c_turn, c_out=c_out, c_norm=c_norm, d_context=d_context, d_scores=d_scores, d_scale=d_scale,
                                 d_attend=d_attend, d_text_scores=d_text_scores, d_text=d_text, d_output=d_output))

        @block.gpsimd
        def _(pool):
            pool.memset(k0s[MASK_ROW:P], 1.0).then_inc(s_ones, 1)
            pool.wait_ge(s_ones, 1)
            pool.wait_ge(s_weights0, 16 * WEIGHTS0)

            def start(u):
                if isinstance(u, int) and u == 0:
                    pool.wait_ge(s_weights, 16 * WEIGHTS)
                    pool.wait_ge(s_const, CONSTANTS)

            def a_residual(u):
                pool.wait_ge(s_xa, 16 * (u + 1))
                before_read(pool, "a", u, A_OUT)
                pool.tensor_tensor(res0[:], x_a[:], bo0[:].unsqueeze(1).broadcast_to([P, J, H]), ALU.add).then_inc(s_res0, 1)

            def b_residual(u):
                before_read(pool, "b", u, B_DOWN)
                pool.tensor_tensor(res_b[:], x_a[:], b_down[:].unsqueeze(1).broadcast_to([P, J, H]), ALU.add).then_inc(s_resb, 1)

            def rest(to, full, piece, sem):
                pool.tensor_tensor(to, full, piece, ALU.subtract).then_inc(sem, 1)

            def low(piece, left, middle, sem, halved):
                pool.wait_ge(sem, halved)
                pool.tensor_tensor(piece, left, middle, ALU.subtract).then_inc(sem, 1)

            def a_project(u, n):
                if n == 0:
                    wait_read(pool, "a", u, A_Q)
                    rest(q0f, q0f, q0p[:, 0], s_q0)
                elif n == KT:
                    for m in range(KT):
                        wait_read(pool, "a", u, A_K + m)
                    rest(k0f, k0f, k0p[:, 0], s_k0)

            def a_stack(u):
                low(q0p[:, 2], q0f, q0p[:, 1], s_q0, 3 * u + 2)
                low(k0p[:, 2], k0f, k0p[:, 1], s_k0, 3 * u + 2)

            def a_norm(u):
                pool.wait_ge(s_rms, 5 * u + 3)
                pool.tensor_tensor(rs0[:], ms0[:], power[:], ALU.pow).then_inc(s_rms, 1)

            def b_stack(u):
                before_made(pool, "c", u, C_PV + 1 + C_NEXT)
                pool.wait_ge(s_k1, 4 * u + 1)
                rest(k1r, kv1f[0:KV1 * D1], k1p[:, 0], s_k1)
                wait_read(pool, "b", u, B_Q)
                rest(q1f, q1f, q1p[:, 0], s_q1)
                low(k1p[:, 2], k1r, k1p[:, 1], s_k1, 4 * u + 3)
                low(q1p[:, 2], q1f, q1p[:, 1], s_q1, 3 * u + 2)

            def c_residual(u):
                wait_read(pool, "b", u, B_DOWN)
                for j in range(J):
                    before_read(pool, "c", u, C_OUT + j)
                pool.tensor_tensor(res1[:], x1[:], bo1[:].unsqueeze(1).broadcast_to([P, J, H]), ALU.add).then_inc(s_res1, 1)

            def c_norm(u, part):
                if part != 2:
                    return
                pool.wait_ge(s_ln, 8 * u + 5)
                pool.tensor_tensor(rs1[:], ve1[:], power[:], ALU.pow).then_inc(s_ln, 1)

            each_round(pool, dict(start=start, a_residual=a_residual, b_residual=b_residual, a_project=a_project, a_stack=a_stack, a_norm=a_norm, b_stack=b_stack,
                                  c_residual=c_residual, c_norm=c_norm))


def kernel(**inputs):
    import numpy as np
    import concourse.bacc as bacc
    from concourse.bass_utils import run_bass_kernel_spmd

    a = {name: np.asarray(value) for name, value in inputs.items()}

    def by_partition(m):
        return m.reshape(-1, P, m.shape[1]).transpose(1, 0, 2)

    def channel_major(heads, channels):
        return np.arange(heads * channels).reshape(heads, channels).T.ravel()

    def column(v):
        return v.reshape(-1, P).T

    order0, order1, order_k1 = channel_major(NH0, D0), channel_major(NH1, D1), channel_major(KV1, D1)
    kv_w, kv_b = a["L0_xattn_kv_w"].reshape(H, H, 2), a["L0_xattn_kv_b"].reshape(H, 2)
    pad = lambda v: np.concatenate([v, np.zeros(P - v.shape[0], v.dtype)])[:, None]
    w = {
        "wq0": by_partition(a["L0_xattn_q_w"][:, order0]), "wk0": by_partition(kv_w[:, order0, 0]), "wv0": by_partition(kv_w[:, :, 1]),
        "wo0": by_partition(a["L0_xattn_out_w"]), "w_up": by_partition(a["L0_xattn_mlp_w1"]), "w_down": by_partition(a["L0_xattn_mlp_w2"]),
        "wq1": by_partition(a["L1_xattn_Wq"][:, order1]),
        "wkv1": by_partition(np.concatenate([a["L1_xattn_Wk"][:, order_k1], a["L1_xattn_Wv"]], axis=1)),
        "wo1": by_partition(a["L1_xattn_Wo"]),
        "wq2": a["L2_xattn_Wq"].T, "wk2": a["L2_xattn_Wk"].T, "wv2": a["L2_xattn_Wv"].T,
        "wq3": by_partition(a["L3_xattn_w_q"]), "wk3": by_partition(a["L3_xattn_w_k"]), "wv3": by_partition(a["L3_xattn_w_v"]),
        "wo3": by_partition(a["L3_xattn_w_o"].T),
        "cols": np.concatenate([
            column(a["L0_xattn_q_b"][order0]), column(kv_b[order0, 0]), column(a["L0_xattn_postnorm_w"]), column(a["L0_xattn_mlp_b1"]),
            column(a["L1_xattn_bq"][order1]), column(np.concatenate([a["L1_xattn_bk"][order_k1], a["L1_xattn_bv"]])),
            pad(a["L2_xattn_bq"]), pad(a["L2_xattn_bk"]), np.broadcast_to(a["L3_xattn_alpha"].reshape(1, 1), (P, 1))], axis=1),
        "bv0": kv_b[:, 1], "bo0": a["L0_xattn_out_b"], "b_down": a["L0_xattn_mlp_b2"], "bo1": a["L1_xattn_bo"],
        "gamma": a["L1_xattn_gamma"], "beta": a["L1_xattn_beta"], "bv2": a["L2_xattn_bv"], "ident": np.eye(P, dtype=np.float32),
    }

    def tokens(m):
        return m.reshape(UNITS, J, P, m.shape[2]).transpose(0, 2, 1, 3)

    def features(m):
        return m.reshape(UNITS, J, P, KT, P).transpose(0, 4, 3, 1, 2)

    x, ctx, mask1 = a["x"], a["ctx_2048"], a["mask_Bx1xSxS2_ff0"][:, 0]
    data = {"x": tokens(x), "x_t": features(x), "ctx": tokens(ctx), "ctx_t": features(ctx),
            "mask0": a["mask_BxS2_ik0"].reshape(UNITS, 1, J, P), "mask1": tokens(mask1), "mask1_t": tokens(mask1.transpose(0, 2, 1))}

    nc = bacc.Bacc("TRN2", target_bir_lowering=False, num_devices=1)
    arrays = {name: np.ascontiguousarray(v) for name, v in {**data, **w}.items()}
    aps = {name: nc.dram_tensor("in_" + name, v.shape, mybir.dt.from_np(v.dtype), kind="ExternalInput").ap() for name, v in arrays.items()}
    out = nc.dram_tensor("out", (UNITS, P, J, H), F32, kind="ExternalOutput").ap()
    build(nc, *(aps[name] for name in data), {name: aps[name] for name in w}, out)
    got = run_bass_kernel_spmd(nc, [{"in_" + name: v for name, v in arrays.items()}], core_ids=[0]).results[0]["out"]
    return np.asarray(got).reshape(UNITS, P, J, H).transpose(0, 2, 1, 3).reshape(B, P, H)
```
